# Optimizing a Trainium2 kernel written in Bass

```python
import numpy as np
import jax
import jax.numpy as jnp

def _softmax(x, axis=-1):
    return jax.nn.softmax(x, axis=axis)

def _gelu(x):
    return jax.nn.gelu(x, approximate=True)

def _silu(x):
    return jax.nn.silu(x)

def _sigmoid(x):
    return jax.nn.sigmoid(x)

def _layernorm(x, axis=-1, eps=1e-05):
    m = jnp.mean(x, axis=axis, keepdims=True)
    v = jnp.var(x, axis=axis, keepdims=True)
    return (x - m) / jnp.sqrt(v + eps)

def _scatter_add(tgt, idx, src, axis=0):
    return tgt.at[idx].add(src)

def _segment_sum(src, seg, n):
    return jax.ops.segment_sum(src, seg, n)
kernel_name = 'mk_conv_attn_hybrid_d2_conv_nhwc256_r2_eed214'

def setup_inputs(seed: int=0):
    np.random.seed(seed)
    _w = jnp.asarray

    def _rec_inputs():
        import jax
        import jax.numpy as jnp
        _gk = jax.random.key(seed)
        x = -0.0006537 + 1.001 * jax.random.normal(jax.random.fold_in(_gk, 1), (4, 48, 48, 128), jnp.float32)
        return x
    x = _rec_inputs()

    def _L0_conv_setup():
        import jax, jax.numpy as jnp
        import jax.lax as lax
        import numpy as np

        def angle_transform(x, sin, cos):
            x1 = x[..., ::2]
            x2 = x[..., 1::2]
            rot = jnp.stack([-x2, x1], axis=-1).reshape(x.shape)
            return x * cos + rot * sin
        key = jax.random.key(seed)
        ks = jax.random.split(key, 14)
        B, H, W, C, nH = (4, 48, 48, 128, 8)
        d = C // nH
        N = H * W
        x = jax.random.normal(ks[0], (B, H, W, C), jnp.float32)
        sin = jax.random.uniform(ks[1], (H, W, d), jnp.float32, -1.0, 1.0)
        cos = jax.random.uniform(ks[2], (H, W, d), jnp.float32, -1.0, 1.0)
        mask = jax.random.normal(ks[3], (nH, N, N), jnp.float32) * 0.02
        w_scale = 0.02
        Wq = jax.random.normal(ks[4], (C, C), jnp.float32) * w_scale
        bq = jnp.zeros((C,), jnp.float32)
        Wk = jax.random.normal(ks[5], (C, C), jnp.float32) * w_scale
        bk = jnp.zeros((C,), jnp.float32)
        Wv = jax.random.normal(ks[6], (C, C), jnp.float32) * w_scale
        bv = jnp.zeros((C,), jnp.float32)
        dw_w = jax.random.normal(ks[7], (5, 5, 1, C), jnp.float32) * 0.05
        dw_b = jnp.zeros((C,), jnp.float32)
        Wo = jax.random.normal(ks[8], (C, C), jnp.float32) * w_scale
        bo = jnp.zeros((C,), jnp.float32)
        return {'x': x, 'sin': sin, 'cos': cos, 'mask': mask, 'Wq': Wq, 'bq': bq, 'Wk': Wk, 'bk': bk, 'Wv': Wv, 'bv': bv, 'dw_w': dw_w, 'dw_b': dw_b, 'Wo': Wo, 'bo': bo, 'num_heads': 8}
    _L0_conv_all = _L0_conv_setup()
    _L0_conv_in = {k: v for k, v in _L0_conv_all.items() if k in ('sin', 'cos', 'mask', 'Wq', 'bq', 'Wk', 'bk', 'Wv', 'bv', 'dw_w', 'dw_b', 'Wo', 'bo')}
    del _L0_conv_all

    def _L1_attn_setup():
        import jax, jax.numpy as jnp
        import numpy as np
        N_EMBED = 128
        B, T = (2, 4096)
        key = jax.random.key(seed)
        ks = jax.random.split(key, 7)
        s = 1.0 / np.sqrt(N_EMBED)
        return {'x': jax.random.normal(ks[0], (B, T, N_EMBED), dtype=jnp.float32), 'Wq': jax.random.normal(ks[1], (N_EMBED, N_EMBED), dtype=jnp.float32) * s, 'bq': jax.random.normal(ks[2], (N_EMBED,), dtype=jnp.float32) * s, 'Wk': jax.random.normal(ks[3], (N_EMBED, N_EMBED), dtype=jnp.float32) * s, 'bk': jax.random.normal(ks[4], (N_EMBED,), dtype=jnp.float32) * s, 'Wv': jax.random.normal(ks[5], (N_EMBED, N_EMBED), dtype=jnp.float32) * s, 'bv': jax.random.normal(ks[6], (N_EMBED,), dtype=jnp.float32) * s}
    _L1_attn_all = _L1_attn_setup()
    _L1_attn_in = {k: v for k, v in _L1_attn_all.items() if k in ('Wq', 'bq', 'Wk', 'bk', 'Wv', 'bv')}
    del _L1_attn_all

    def _L1_ffn_setup():
        import math
        import jax, jax.numpy as jnp
        import numpy as np
        CAPACITY_FACTOR = 1.25
        TOP_K = 2
        LN_EPS = 1e-05

        def _layer_norm(x, gamma, beta):
            mu = jnp.mean(x, axis=-1, keepdims=True)
            var = jnp.var(x, axis=-1, keepdims=True)
            return (x - mu) * jax.lax.rsqrt(var + LN_EPS) * gamma + beta
        key = jax.random.key(seed)
        ks = jax.random.split(key, 4)
        B, S, D, F, E = (8, 2048, 128, 256, 8)
        x = jax.random.normal(ks[0], (B, S, D), dtype=jnp.float32)
        Wr = jax.random.normal(ks[1], (D, E), dtype=jnp.float32) / np.sqrt(D)
        br = jnp.zeros((E,), jnp.float32)
        W1 = jax.random.normal(ks[2], (E, D, F), dtype=jnp.float32) / np.sqrt(D)
        b1 = jnp.zeros((E, F), jnp.float32)
        W2 = jax.random.normal(ks[3], (E, F, D), dtype=jnp.float32) / np.sqrt(F)
        b2 = jnp.zeros((E, D), jnp.float32)
        gamma = jnp.ones((D,), jnp.float32)
        beta = jnp.zeros((D,), jnp.float32)
        return {'x': x, 'Wr': Wr, 'br': br, 'W1': W1, 'b1': b1, 'W2': W2, 'b2': b2, 'gamma': gamma, 'beta': beta}
    _L1_ffn_all = _L1_ffn_setup()
    _L1_ffn_in = {k: v for k, v in _L1_ffn_all.items() if k in ('Wr', 'br', 'W1', 'b1', 'W2', 'b2', 'gamma', 'beta')}
    del _L1_ffn_all
    return {'x': x, 'L0_conv_sin': _L0_conv_in['sin'], 'L0_conv_cos': _L0_conv_in['cos'], 'L0_conv_mask': _L0_conv_in['mask'], 'L0_conv_Wq': _L0_conv_in['Wq'], 'L0_conv_bq': _L0_conv_in['bq'], 'L0_conv_Wk': _L0_conv_in['Wk'], 'L0_conv_bk': _L0_conv_in['bk'], 'L0_conv_Wv': _L0_conv_in['Wv'], 'L0_conv_bv': _L0_conv_in['bv'], 'L0_conv_dw_w': _L0_conv_in['dw_w'], 'L0_conv_dw_b': _L0_conv_in['dw_b'], 'L0_conv_Wo': _L0_conv_in['Wo'], 'L0_conv_bo': _L0_conv_in['bo'], 'L1_attn_Wq': _L1_attn_in['Wq'], 'L1_attn_bq': _L1_attn_in['bq'], 'L1_attn_Wk': _L1_attn_in['Wk'], 'L1_attn_bk': _L1_attn_in['bk'], 'L1_attn_Wv': _L1_attn_in['Wv'], 'L1_attn_bv': _L1_attn_in['bv'], 'L1_ffn_Wr': _L1_ffn_in['Wr'], 'L1_ffn_br': _L1_ffn_in['br'], 'L1_ffn_W1': _L1_ffn_in['W1'], 'L1_ffn_b1': _L1_ffn_in['b1'], 'L1_ffn_W2': _L1_ffn_in['W2'], 'L1_ffn_b2': _L1_ffn_in['b2'], 'L1_ffn_gamma': _L1_ffn_in['gamma'], 'L1_ffn_beta': _L1_ffn_in['beta']}

def reference(x, L0_conv_sin, L0_conv_cos, L0_conv_mask, L0_conv_Wq, L0_conv_bq, L0_conv_Wk, L0_conv_bk, L0_conv_Wv, L0_conv_bv, L0_conv_dw_w, L0_conv_dw_b, L0_conv_Wo, L0_conv_bo, L1_attn_Wq, L1_attn_bq, L1_attn_Wk, L1_attn_bk, L1_attn_Wv, L1_attn_bv, L1_ffn_Wr, L1_ffn_br, L1_ffn_W1, L1_ffn_b1, L1_ffn_W2, L1_ffn_b2, L1_ffn_gamma, L1_ffn_beta):
    import jax
    import jax.numpy as jnp

    def _L0_conv_ref(x, sin, cos, mask, Wq, bq, Wk, bk, Wv, bv, dw_w, dw_b, Wo, bo, num_heads):
        import jax, jax.numpy as jnp
        import jax.lax as lax
        import numpy as np

        def angle_transform(x, sin, cos):
            x1 = x[..., ::2]
            x2 = x[..., 1::2]
            rot = jnp.stack([-x2, x1], axis=-1).reshape(x.shape)
            return x * cos + rot * sin
        B, H, W, C = x.shape
        d = C // num_heads
        N = H * W
        scaling = d ** (-0.5)
        q = x @ Wq + bq
        k = (x @ Wk + bk) * scaling
        v = x @ Wv + bv
        lepe = lax.conv_general_dilated(v, dw_w, window_strides=(1, 1), padding=((2, 2), (2, 2)), dimension_numbers=('NHWC', 'HWIO', 'NHWC'), feature_group_count=C) + dw_b
        qh = q.reshape(B, H, W, num_heads, d).transpose(0, 3, 1, 2, 4)
        kh = k.reshape(B, H, W, num_heads, d).transpose(0, 3, 1, 2, 4)
        vh = v.reshape(B, H, W, num_heads, d).transpose(0, 3, 1, 2, 4)
        qr = angle_transform(qh, sin, cos).reshape(B, num_heads, N, d)
        kr = angle_transform(kh, sin, cos).reshape(B, num_heads, N, d)
        vr = vh.reshape(B, num_heads, N, d)
        attn = jnp.einsum('bhnd,bhmd->bhnm', qr, kr) + mask
        out = jnp.einsum('bhnm,bhmd->bhnd', jax.nn.softmax(attn, axis=-1), vr)
        out = out.transpose(0, 2, 1, 3).reshape(B, H, W, C)
        out = out + lepe
        return out @ Wo + bo

    def _L1_attn_ref(x, Wq, bq, Wk, bk, Wv, bv):
        import jax, jax.numpy as jnp
        import numpy as np
        N_EMBED = 128
        B, T = (2, 4096)
        q = x @ Wq + bq
        k = x @ Wk + bk
        v = x @ Wv + bv
        scores = jnp.einsum('btd,bsd->bts', q, k)
        attn = jax.nn.softmax(scores, axis=-1)
        return jnp.einsum('bts,bsd->btd', attn, v)

    def _L1_ffn_ref(x, Wr, br, W1, b1, W2, b2, gamma, beta):
        import math
        import jax, jax.numpy as jnp
        import numpy as np
        CAPACITY_FACTOR = 1.25
        TOP_K = 2
        LN_EPS = 1e-05

        def _layer_norm(x, gamma, beta):
            mu = jnp.mean(x, axis=-1, keepdims=True)
            var = jnp.var(x, axis=-1, keepdims=True)
            return (x - mu) * jax.lax.rsqrt(var + LN_EPS) * gamma + beta
        B, S, D = x.shape
        E = Wr.shape[1]
        N = B * S
        K = TOP_K
        logits = jnp.mean(x, axis=1) @ Wr + br
        routing_weights = jax.nn.softmax(logits, axis=-1)
        capacity = float(math.ceil(N * CAPACITY_FACTOR / E))
        expected_loads = routing_weights.sum(axis=0) * (N / B)
        scale = jnp.where(expected_loads > capacity, capacity / expected_loads, 1.0)
        routing_weights = jax.nn.softmax(routing_weights * scale, axis=-1)
        rw_tok = jnp.broadcast_to(routing_weights[:, None, :], (B, S, E)).reshape(N, E)
        top_w, top_i = jax.lax.top_k(rw_tok, K)
        top_w = jax.nn.softmax(top_w, axis=-1)
        xf = x.reshape(N, D)
        h = jax.nn.gelu(jnp.einsum('nd,edf->enf', xf, W1) + b1[:, None, :], approximate=False)
        y = jnp.einsum('enf,efd->end', h, W2) + b2[:, None, :]
        w_dense = jnp.zeros((N, E), x.dtype).at[jnp.arange(N)[:, None], top_i].add(top_w)
        out = jnp.einsum('ne,end->nd', w_dense, y).reshape(B, S, D)
        out = _layer_norm(out + x, gamma, beta)
        return out

    def _gn(v, G=32, eps=1e-05):
        B_, H_, W_, C_ = v.shape
        g = v.reshape(B_, H_, W_, G, C_ // G)
        m = jnp.mean(g, axis=(1, 2, 4), keepdims=True)
        s = jnp.var(g, axis=(1, 2, 4), keepdims=True)
        return ((g - m) / jnp.sqrt(s + eps)).reshape(v.shape)

    def _ln_c(v, eps=1e-06):
        m = jnp.mean(v, axis=-1, keepdims=True)
        s = jnp.var(v, axis=-1, keepdims=True)
        return (v - m) / jnp.sqrt(s + eps)

    def _ln_t(v, eps=1e-05):
        m = jnp.mean(v, axis=-1, keepdims=True)
        s = jnp.var(v, axis=-1, keepdims=True)
        return (v - m) / jnp.sqrt(s + eps)

    def _to_tokens(v):
        B_, H_, W_, C_ = v.shape
        return v.reshape(B_, H_ * W_, C_)

    def _from_tokens(t, like):
        return t.reshape(like.shape)
    x = x + _L0_conv_ref(_gn(x), L0_conv_sin, L0_conv_cos, L0_conv_mask, L0_conv_Wq, L0_conv_bq, L0_conv_Wk, L0_conv_bk, L0_conv_Wv, L0_conv_bv, L0_conv_dw_w, L0_conv_dw_b, L0_conv_Wo, L0_conv_bo, 8)
    t = _to_tokens(x)
    t = t + _L1_attn_ref(_ln_t(t), L1_attn_Wq, L1_attn_bq, L1_attn_Wk, L1_attn_bk, L1_attn_Wv, L1_attn_bv)
    t = t + _L1_ffn_ref(_ln_t(t), L1_ffn_Wr, L1_ffn_br, L1_ffn_W1, L1_ffn_b1, L1_ffn_W2, L1_ffn_b2, L1_ffn_gamma, L1_ffn_beta)
    x = _from_tokens(t, x)
    return x

_drawn_inputs = setup_inputs


def setup_inputs(seed=0):
    import zlib

    import numpy as np

    out = dict(_drawn_inputs(seed))
    spreads = {'L0_conv_bq': (0.0, 0.8),
     'L0_conv_bk': (0.0, 0.8),
     'L0_conv_bv': (0.0, 0.1),
     'L0_conv_dw_b': (0.0, 0.1),
     'L0_conv_bo': (0.0, 0.1),
     'L1_ffn_br': (0.0, 0.1),
     'L1_ffn_b1': (0.0, 0.396),
     'L1_ffn_b2': (0.0, 0.274),
     'L1_ffn_gamma': (1.0, 0.2),
     'L1_ffn_beta': (0.0, 0.1)}
    factors = {'L0_conv_sin': 8.0,
     'L0_conv_cos': 8.0,
     'L0_conv_Wq': 8.0,
     'L0_conv_Wk': 8.0,
     'L1_attn_bk': 8.0}
    for name, (base, spread) in spreads.items():
        noise = np.random.default_rng([zlib.crc32(name.encode()), seed]).standard_normal(out[name].shape)
        drawn = base * np.exp(spread * noise) if base else spread * noise
        out[name] = jnp.asarray(drawn.astype(out[name].dtype))
    for name, factor in factors.items():
        out[name] = (out[name] * factor).astype(out[name].dtype)
    return out
```

```python
from contextlib import ExitStack

import numpy as np
import concourse.bass as bass
from concourse import mybir

F32 = mybir.dt.float32
BF16 = mybir.dt.bfloat16
ALU = mybir.AluOpType
ACT = mybir.ActivationFunctionType
AX = mybir.AxisListType

P = 128
B, H, W, C = 4, 48, 48, 128
N = H * W
HEADS = 8
D = C // HEADS
TILES = N // P
HT = TILES // 2
GB = 3
GW = GB * P
NG = TILES // GB
CH = 2 * GW
NCH = N // CH
BANK = 512
GROUP = 4
PAD = 2
WP = W + 2 * PAD
TAPS = 25
HALF_H = H // 2
HALF_OUT = HALF_H * WP
PIECES = TILES // 2
PIECE = -(-HALF_OUT // PIECES)
HALF_IN = PIECE * PIECES + (TAPS // 5 - 1) * (WP + 1)
IMAGE_IN = HALF_OUT + HALF_IN
Q_SLOTS = [0, 0, 0, 1, 1, 2]
K_SLOTS = [0, 1, 2, 0, 1, 0]
KR = len(Q_SLOTS) * D
E = 8
FF = 256
FH = FF // P
TOPK = 2
CAPACITY = float(-(-B * N * 1.25 // E))
LOWEST = -3.0e38


def sem_maker(nc, ctx, prefix):
    return lambda name: ctx.enter_context(nc.semaphore(f"{prefix}_{name}"))


def buffers(nc, ctx, prefix):
    def sb(name, shape, dt=F32):
        return ctx.enter_context(nc.sbuf_tensor(f"{prefix}_{name}", shape, dt))

    def ps(name, shape):
        return ctx.enter_context(nc.psum_tensor(f"{prefix}_{name}", shape, F32))

    return sb, ps


def alone(engine):
    engine.nop(nofuse=True)


def cols(b, g):
    return slice(g * b, (g + 1) * b)


def layer0_front(nc, a, s, ident, taps, conv_bias):
    with ExitStack() as ctx:
        sb, ps = buffers(nc, ctx, "f")
        sem = sem_maker(nc, ctx, "f")
        X = sb("X", [P, TILES, C])
        XT = sb("XT", [P, N])
        XN = sb("XN", [P, N])
        cosT = sb("cosT", [P, N])
        sinT = sb("sinT", [P, N])
        angles = sb("angles", [P, 2, TILES, D])
        angles8 = sb("angles8", [P, TILES, HEADS, D])
        rot_sum = sb("rot_sum", [P, 2, N])
        parts = sb("parts", [P, 2, 3, N], BF16)
        t1 = sb("t1", [P, 2, GW])
        t2 = sb("t2", [P, 2, GW])
        V = sb("V", [P, HEADS, TILES, D])
        vpad = sb("vpad", [P, IMAGE_IN])
        weights = sb("weights", [P, 5, C])
        rows = sb("rows", [1, 6, C])
        biases = sb("biases", [P, 6])
        bv_all = sb("bv_all", [P, GB, C])
        ones = sb("ones", [1, P])
        eps = sb("eps", [P, 1])
        average = sb("average", [P, P])
        taps_row = sb("taps_row", [TAPS, C])
        stats = sb("stats", [P, NG, 6])
        mv = sb("mv", [P, 2])
        moments = sb("moments", [P, 2])
        group = sb("group", [P, 2])
        var = sb("var", [P, 1])
        sd = sb("sd", [P, 1])
        rstd = sb("rstd", [P, 1])

        tr = ps("tr", [P, 2, BANK])
        mm = ps("mm", [P, 4, BANK])
        vps = ps("vps", [P, BANK])
        misc = ps("misc", [P, BANK])

        weights_in = sem("weights_in")
        x_in = sem("x_in")
        constants = sem("constants")
        prep = sem("prep")
        scaled_k = sem("scaled_k")
        rotated_w = sem("rotated_w")
        angles_wide = sem("angles_wide")
        small_ready = sem("small_ready")
        small_taken = sem("small_taken")
        tr_ready = sem("tr_ready")
        tr_taken = sem("tr_taken")
        stats_ready = sem("stats_ready")
        norm_step = sem("norm_step")
        group_ready = sem("group_ready")
        var_ready = sem("var_ready")
        sd_ready = sem("sd_ready")
        xn_ready = sem("xn_ready")
        mm_ready = sem("mm_ready")
        mm_taken = sem("mm_taken")
        rot_ready = sem("rot_ready")
        p1_ready = sem("p1_ready")
        d1_ready = sem("d1_ready")
        p2_ready = sem("p2_ready")
        p3_ready = sem("p3_ready")
        q_stored = sem("q_stored")
        k_stored = sem("k_stored")
        v_stored = sem("v_stored")
        vpad_stored = sem("vpad_stored")
        vps_ready = sem("vps_ready")
        vps_taken = sem("vps_taken")
        vpad_ready = sem("vpad_ready")

        TR_USES = 2 * NG
        ANGLE_USES = 2 * NG
        MM_USES = 4 * NG

        block = ctx.enter_context(nc.Block())

        @block.sync
        def _(sp):
            for i, w in enumerate((a["Wq"], None, a["Wk"], None, a["Wv"])):
                if w is not None:
                    sp.dma_start(weights[:, i, :], w).then_inc(weights_in, 16)
            for i, v in enumerate((a["bq"], None, a["bk"], None, a["bv"], a["dw_b"])):
                if v is not None:
                    sp.dma_start(rows[:, i, :], v.rearrange("(a n) -> a n", a=1)).then_inc(weights_in, 16)
            sp.dma_start(angles[:, 0, :, :], a["cos"].rearrange("h w d -> (h w) d").rearrange("(t p) d -> p t d", p=P)).then_inc(weights_in, 16)
            sp.dma_start(angles[:, 1, :, :], a["sin"].rearrange("h w d -> (h w) d").rearrange("(t p) d -> p t d", p=P)).then_inc(weights_in, 16)
            sp.dma_start(taps_row[:, :], a["dw_w"].rearrange("a b o c -> (a b o) c")).then_inc(weights_in, 16)
            for half in range(2):
                sp.dma_start(X[:, cols(HT, half), :], s["x_tiles"][0][:, cols(HT, half), :]).then_inc(x_in, 16)

            def store(b):
                sp.wait_ge(p3_ready, 2 * b + 1 + 2)
                for slot, part in enumerate(Q_SLOTS):
                    sp.dma_start(s["q_store"][b, slot], parts[:, 0, part, :]).then_inc(q_stored, 16)
                sp.wait_ge(p3_ready, 2 * b + 2 + 2)
                for part in range(3):
                    sp.dma_start(s["k_store"][b, part], parts[:, 1, part, :]).then_inc(k_stored, 16)
                sp.wait_ge(vps_taken, NG * (b + 1) + 1)
                sp.dma_start(s["v_store"][b], V[:, :, :, :].rearrange("p h t d -> p h (t d)")).then_inc(v_stored, 16)
                sp.wait_ge(tr_taken, ANGLE_USES + TR_USES * (b + 1) + 2)
                sp.dma_start(s["vpad_store"][b], vpad[:, :]).then_inc(vpad_stored, 16)

            with sp.Fori(0, B - 1) as b:
                sp.wait_ge(tr_ready, ANGLE_USES + TR_USES * b + NG)
                for half in range(2):
                    sp.dma_start(X[:, cols(HT, half), :], s["x_tiles"][b + 1][:, cols(HT, half), :]).then_inc(x_in, 16)
                store(b)
            store(B - 1)
            sp.wait_ge(q_stored, 16 * len(Q_SLOTS) * B)
            sp.wait_ge(k_stored, 16 * 3 * B)
            sp.wait_ge(v_stored, 16 * B)
            sp.wait_ge(vpad_stored, 16 * B)

        @block.gpsimd
        def _(pool):
            pool.memset(average[:, :], 1.0 / GROUP).then_inc(prep, 1)
            pool.memset(ident[:, :], 0.0).then_inc(prep, 1)
            pool.memset(vpad[:, :], 0.0).then_inc(constants, 1)
            pool.memset(ones[:, :], 1.0).then_inc(constants, 1)
            pool.memset(eps[:, :], 1e-5).then_inc(constants, 1)
            pool.wait_ge(prep, 2)
            pool.affine_select(out=ident[:, :], in_=ident[:, :], compare_op=ALU.not_equal, fill=1.0,
                               base=0, pattern=[[-1, P]], channel_multiplier=1).then_inc(constants, 1)
            av = average[:, :].rearrange("p (g k) -> p g k", k=GROUP)
            pool.affine_select(out=av, in_=av, compare_op=ALU.is_ge, fill=0.0, base=0,
                               pattern=[[-GROUP, P // GROUP], [0, GROUP]], channel_multiplier=1).then_inc(prep, 1)
            pool.wait_ge(prep, 3)
            pool.affine_select(out=av, in_=av, compare_op=ALU.is_ge, fill=0.0, base=GROUP - 1,
                               pattern=[[GROUP, P // GROUP], [0, GROUP]], channel_multiplier=-1).then_inc(constants, 1)
            with pool.Fori(0, B) as b:
                for m in range(2):
                    src = rot_sum[:, m, :]
                    pool.wait_ge(p1_ready, 2 * b + m + 1)
                    alone(pool)
                    pool.tensor_tensor(src, src, parts[:, m, 0, :], ALU.subtract).then_inc(d1_ready, 1)
                    pool.wait_ge(p2_ready, 2 * b + m + 1)
                    alone(pool)
                    pool.tensor_tensor(parts[:, m, 2, :], src, parts[:, m, 1, :], ALU.subtract).then_inc(p3_ready, 1)

        @block.scalar
        def _(act):
            act.sem_inc(tr_taken, 2)
            for m in range(2):
                for g in range(NG):
                    act.wait_ge(tr_ready, m * NG + g + 1)
                    dst = (cosT, sinT)[m][:, cols(GW, g)]
                    act.activation(dst, tr[:, g % 2, 0:GW], ACT.Copy).then_inc(tr_taken, 1)
            with act.Fori(0, B) as b:
                for g in range(NG):
                    if g == 0:
                        act.wait_ge(xn_ready, b)
                    act.wait_ge(tr_ready, ANGLE_USES + TR_USES * b + g + 1)
                    act.activation(XT[:, cols(GW, g)], tr[:, g % 2, 0:GW], ACT.Copy).then_inc(tr_taken, 1)
                act.wait_ge(var_ready, b + 1)
                act.activation(sd[:, :], var[:, :], ACT.Sqrt, bias=eps[:, :]).then_inc(sd_ready, 1)
                act.wait_ge(vpad_stored, 16 * b)
                for g in range(NG):
                    act.wait_ge(tr_ready, ANGLE_USES + TR_USES * b + NG + g + 1)
                    rows_of = GW // W
                    image = vpad[:, 0:(H + 2 * PAD) * WP].rearrange("p (h w) -> p h w", w=WP)
                    dst = image[:, PAD + g * rows_of:PAD + (g + 1) * rows_of, PAD:PAD + W]
                    src = tr[:, g % 2, 0:GW].rearrange("p (h w) -> p h w", w=W)
                    act.activation(dst, src, ACT.Identity, bias=biases[:, 4:5]).then_inc(tr_taken, 1)
                for m in range(2):
                    act.wait_ge((q_stored, k_stored)[m], 16 * (len(Q_SLOTS), 3)[m] * b)
                    act.wait_ge(rot_ready, 2 * b + m + 1)
                    act.activation(parts[:, m, 0, :], rot_sum[:, m, :], ACT.Copy).then_inc(p1_ready, 1)
                    act.wait_ge(d1_ready, 2 * b + m + 1)
                    act.activation(parts[:, m, 1, :], rot_sum[:, m, :], ACT.Copy).then_inc(p2_ready, 1)

        @block.tensor
        def _(pe):
            pe.wait_ge(constants, 5)
            pe.wait_ge(rotated_w, 1)
            for i in range(6):
                pe.matmul(misc[:, i:i + 1], rows[0:1, i, :], ones[0:1, 0:1], start=True, stop=True)
            pe.matmul(misc[:, P:2 * P], ones[0:1, :], rows[0:1, 4, :], start=True, stop=True)
            pe.transpose(misc[:, 2 * P:2 * P + TAPS], taps_row[:, :], ident[0:TAPS, 0:TAPS]).then_inc(small_ready, 1)
            for m in range(2):
                pe.wait_ge(angles_wide, m + 1)
                for g in range(NG):
                    pe.wait_ge(tr_taken, m * NG + g + 1)
                    for k in range(GB):
                        t = g * GB + k
                        last = pe.transpose(tr[:, g % 2, cols(P, k)],
                                            angles8[:, t, :, :].rearrange("p h d -> p (h d)"), ident[:, :])
                    last.then_inc(tr_ready, 1)
            pe.wait_ge(small_taken, 3)
            with pe.Fori(0, B) as b:
                pe.wait_ge(x_in, 32 * (b + 1))
                for g in range(NG):
                    pe.wait_ge(tr_taken, ANGLE_USES + TR_USES * b + g + 1)
                    for k in range(GB):
                        last = pe.transpose(tr[:, g % 2, cols(P, k)], X[:, g * GB + k, :], ident[:, :])
                    last.then_inc(tr_ready, 1)
                pe.wait_ge(stats_ready, b + 1)
                pe.matmul(misc[:, 0:2], average[:, :], moments[:, :], start=True, stop=True).then_inc(group_ready, 1)
                pe.wait_ge(xn_ready, b + 1)
                for g in range(NG):
                    pe.wait_ge(tr_taken, ANGLE_USES + TR_USES * b + NG + g + 1)
                    pe.matmul(tr[:, g % 2, 0:GW], weights[:, 4, :], XN[:, cols(GW, g)],
                              start=True, stop=True).then_inc(tr_ready, 1)
                for g in range(NG):
                    pe.wait_ge(vps_taken, NG * b + g + 1)
                    for k in range(GB):
                        last = pe.matmul(vps[:, cols(P, k)], XN[:, cols(P, g * GB + k)], weights[:, 4, :],
                                         start=True, stop=True)
                    last.then_inc(vps_ready, 1)
                for m in range(2):
                    for g in range(NG):
                        for r in range(2):
                            n = (m * NG + g) * 2 + r
                            pe.wait_ge(mm_taken, MM_USES * b + n + 1)
                            pe.matmul(mm[:, n % 4, 0:GW], weights[:, 2 * m + r, :], XN[:, cols(GW, g)],
                                      start=True, stop=True).then_inc(mm_ready, 1)

        @block.vector
        def _(dve):
            dve.sem_inc(mm_taken, 4)
            dve.sem_inc(vps_taken, 1)
            pool_credit = 2
            dve.sem_inc(p3_ready, pool_credit)
            dve.wait_ge(weights_in, 16 * 10)
            dve.tensor_scalar(weights[:, 2, :], weights[:, 2, :], D ** -0.5, None, ALU.mult).then_inc(scaled_k, 1)
            dve.tensor_scalar(rows[:, 2, :], rows[:, 2, :], D ** -0.5, None, ALU.mult).then_inc(scaled_k, 1)
            dve.wait_ge(scaled_k, 2)
            for t, parts_of in ((weights, P), (rows, 1)):
                for src_i in (0, 2):
                    src = t[:, src_i, :].rearrange("p (i two) -> p i two", two=2)
                    dst = t[:, src_i + 1, :].rearrange("p (i two) -> p i two", two=2)
                    dve.tensor_scalar(dst[:, :, 0], src[:, :, 1], -1.0, None, ALU.mult)
                    last = dve.tensor_copy(dst[:, :, 1], src[:, :, 0])
            last.then_inc(rotated_w, 1)
            for m in range(2):
                if m:
                    dve.wait_ge(tr_ready, NG)
                for h in range(HEADS):
                    last = dve.tensor_copy(angles8[:, :, h, :], angles[:, m, :, :])
                last.then_inc(angles_wide, 1)
            dve.wait_ge(small_ready, 1)
            dve.tensor_copy(conv_bias[:, :], misc[:, 5:6])
            dve.tensor_copy(biases[:, :], misc[:, 0:6]).then_inc(small_taken, 1)
            for k in range(GB):
                last = dve.tensor_copy(bv_all[:, k, :], misc[:, P:2 * P])
            last.then_inc(small_taken, 1)
            dve.tensor_copy(taps[:, :], misc[:, 2 * P:2 * P + TAPS]).then_inc(small_taken, 1)
            dve.wait_ge(small_taken, 3)
            dve.wait_ge(tr_taken, 2 * NG + 2)
            with dve.Fori(0, B) as b:
                for g in range(NG):
                    dve.wait_ge(tr_taken, ANGLE_USES + TR_USES * b + g + 1 + 2)
                    last = dve.bn_stats(stats[:, g, :], XT[:, cols(GW, g)])
                NS = 6
                last.then_inc(norm_step, 1)
                dve.wait_ge(norm_step, NS * b + 1)
                alone(dve)
                dve.bn_aggr(mv[:, :], stats[:, :, :]).then_inc(norm_step, 1)
                dve.wait_ge(norm_step, NS * b + 2)
                dve.tensor_copy(moments[:, 0:1], mv[:, 0:1])
                dve.scalar_tensor_tensor(out=moments[:, 1:2], in0=mv[:, 0:1], scalar=mv[:, 0:1], in1=mv[:, 1:2],
                                         op0=ALU.mult, op1=ALU.add).then_inc(stats_ready, 1)
                dve.wait_ge(group_ready, b + 1)
                dve.tensor_copy(group[:, :], misc[:, 0:2]).then_inc(norm_step, 1)
                dve.wait_ge(norm_step, NS * b + 3)
                dve.tensor_tensor(var[:, :], group[:, 0:1], group[:, 0:1], ALU.mult).then_inc(norm_step, 1)
                dve.wait_ge(norm_step, NS * b + 4)
                dve.tensor_tensor(var[:, :], group[:, 1:2], var[:, :], ALU.subtract).then_inc(norm_step, 1)
                dve.wait_ge(norm_step, NS * b + 5)
                dve.tensor_scalar(var[:, :], var[:, :], 0.0, None, ALU.max).then_inc(var_ready, 1)
                dve.wait_ge(sd_ready, b + 1)
                dve.reciprocal(rstd[:, :], sd[:, :]).then_inc(norm_step, 1)
                dve.wait_ge(norm_step, NS * b + 6)
                dve.wait_ge(mm_ready, MM_USES * b)
                dve.tensor_scalar(XN[:, :], XT[:, :], group[:, 0:1], rstd[:, :], ALU.subtract, ALU.mult).then_inc(xn_ready, 1)
                dve.wait_ge(v_stored, 16 * b)
                for g in range(NG):
                    dve.wait_ge(vps_ready, NG * b + g + 1)
                    dst = V[:, :, cols(GB, g), :].rearrange("p h t d -> p t h d")
                    src = vps[:, 0:GW].rearrange("p (t h d) -> p t h d", t=GB, h=HEADS)
                    bias = bv_all[:, :, :].rearrange("p t (h d) -> p t h d", h=HEADS)
                    dve.tensor_tensor(dst, src, bias, ALU.add).then_inc(vps_taken, 1)
                for m in range(2):
                    dve.wait_ge(p3_ready, 2 * b + m + 1)
                    for g in range(NG):
                        n = (m * NG + g) * 2
                        dve.wait_ge(mm_ready, MM_USES * b + n + 2)
                        dve.scalar_tensor_tensor(out=t1[:, g % 2, :], in0=mm[:, n % 4, 0:GW], scalar=biases[:, 2 * m:2 * m + 1],
                                                 in1=cosT[:, cols(GW, g)], op0=ALU.add, op1=ALU.mult).then_inc(mm_taken, 1)
                        dve.scalar_tensor_tensor(out=t2[:, g % 2, :], in0=mm[:, (n + 1) % 4, 0:GW], scalar=biases[:, 2 * m + 1:2 * m + 2],
                                                 in1=sinT[:, cols(GW, g)], op0=ALU.add, op1=ALU.mult).then_inc(mm_taken, 1)
                        dve.wait_ge(mm_taken, MM_USES * b + n + 2 + 4)
                        last = dve.tensor_tensor(rot_sum[:, m, cols(GW, g)], t1[:, g % 2, :], t2[:, g % 2, :], ALU.add)
                    last.then_inc(rot_ready, 1)


def layer0_core(nc, a, s, ident, taps, conv_bias):
    with ExitStack() as ctx:
        sb, ps = buffers(nc, ctx, "c")
        sem = sem_maker(nc, ctx, "c")
        K = sb("K", [KR, 2 * B * N], BF16)
        Q = sb("Q", [KR, 2, B, P], BF16)
        mask = sb("mask", [P, 2, N])
        S = sb("S", [P, B, N])
        part_max = sb("part_max", [P, B, NCH])
        row_max = sb("row_max", [P, B])
        PT = sb("PT", [P, 2, TILES, P])
        V_next = sb("V_next", [P, B * TILES, D])
        V = sb("V", [P, B * TILES, 2 * D])
        O = sb("O", [P, 2, B, P])

        vpad = sb("vpad", [P, 2 * HALF_IN])
        conv = sb("conv", [P, 2 * PIECE * PIECES])

        Sps = ps("Sps", [P, 2, 2, BANK])
        Tps = ps("Tps", [P, 3, BANK])
        Ops = ps("Ops", [P, B, P])

        k_in, v_in, tile_in = sem("k_in"), sem("v_in"), sem("tile_in")
        v_ones, v_placed = sem("v_ones"), sem("v_placed")
        s_ready, s_taken = sem("s_ready"), sem("s_taken")
        max_ready, shifted = sem("max_ready"), sem("shifted")
        t_ready, exp_done, pt_used = sem("t_ready"), sem("exp_done"), sem("pt_used")
        o_taken, o_stored = sem("o_taken"), sem("o_stored")
        vpad_in, conv_step, conv_stored = sem("vpad_in"), sem("conv_step"), sem("conv_stored")

        ITERS = HEADS * TILES
        PAIRS = TILES // 2
        IC, IG = B * NCH, B * NG
        COLS = 4
        STORES = COLS + 1
        S_SLOTS, T_SLOTS, PT_SLOTS, O_SLOTS = 2, 3, 2, 1

        block = ctx.enter_context(nc.Block())

        @block.sync
        def _(sp):
            def load_head(h):
                k = K[:, bass.ds((h % 2) * (B * N), B * N)]
                sp.dma_start(k[0:3 * D, :], s["k_load"][h]).then_inc(k_in, 16)
                sp.dma_start(k[3 * D:5 * D, :], s["k_load"][h][0:2 * D, :]).then_inc(k_in, 16)
                sp.dma_start(k[5 * D:6 * D, :], s["k_load"][h][0:D, :]).then_inc(k_in, 16)
                sp.dma_start(V_next[:, :, :].rearrange("p t d -> p (t d)"), s["v_load"][h]).then_inc(v_in, 16)

            def load_half(h):
                sp.dma_start(vpad[:, bass.ds((h % 2) * HALF_IN, HALF_IN)],
                             s["vpad_load"][h // 2][:, bass.ds((h % 2) * HALF_OUT, HALF_IN)]).then_inc(vpad_in, 16)

            def store_half(h):
                sp.wait_ge(conv_step, TAPS * PIECES * (h + 1))
                alone(sp)
                rows = conv[:, bass.ds((h % 2) * PIECE * PIECES, HALF_OUT)].rearrange("p (h w) -> p h w", w=WP)
                sp.dma_start(s["conv_store"][h // 2][h % 2], rows[:, :, 0:W]).then_inc(conv_stored, 16)

            def load_tile(it):
                slot = it % 2
                sp.dma_start(mask[:, bass.ds(slot, 1), :].rearrange("p a n -> p (a n)"),
                             s["mask"][it]).then_inc(tile_in, 16)
                sp.dma_start(Q[:, bass.ds(slot, 1), :, :].rearrange("r a b q -> r (a b) q"),
                             s["q_load"][it // TILES][:, :, bass.ds((it % TILES) * P, P)]).then_inc(tile_in, 16)

            def store_tile(it):
                o = O[:, bass.ds(it % 2, 1), :, :].rearrange("p a b q -> p (a b) q")
                sp.wait_ge(o_stored, 16 * STORES * (it + 1))
                sp.wait_ge(o_taken, it + 1)
                h, qt = it // TILES, it % TILES
                for j in range(COLS):
                    sp.dma_start(s["o_store"][j][h][:, :, bass.ds(qt * P, P)], o[32 * j:32 * j + D]).then_inc(o_stored, 16)
                sp.dma_start(s["den_store"][h][:, :, bass.ds(qt * P, P)], o[D:P:32]).then_inc(o_stored, 16)

            def step(it):
                sp.wait_ge(tile_in, 32 * (it + 2))
                sp.wait_ge(s_taken, IC * (it + 1) + S_SLOTS)
                load_tile(it + 2)
                store_tile(it)

            load_head(0)
            load_half(0)
            load_tile(0)
            sp.wait_ge(tile_in, 32)
            load_tile(1)
            with sp.Fori(0, HEADS - 1) as h:
                step(h * TILES)
                sp.wait_ge(k_in, 48 * (h + 1))
                sp.wait_ge(v_placed, h + 1)
                load_head(h + 1)
                sp.wait_ge(conv_step, TAPS * PIECES * h)
                alone(sp)
                sp.wait_ge(vpad_in, 16 * (h + 1))
                alone(sp)
                load_half(h + 1)
                with sp.Fori(1, TILES) as qt:
                    step(h * TILES + qt)
                store_half(h)
            with sp.Fori(ITERS - TILES, ITERS - 2) as it:
                step(it)
            store_half(HEADS - 1)
            store_tile(ITERS - 2)
            store_tile(ITERS - 1)
            sp.wait_ge(conv_stored, 16 * (HEADS + 1))
            sp.wait_ge(o_stored, 16 * STORES * (ITERS + 1))

        @block.gpsimd
        def _(pool):
            pool.memset(V[:, :, :], 1.0).then_inc(v_ones, 1)
            with pool.Fori(0, ITERS) as it:
                for b in range(B):
                    pool.wait_ge(max_ready, B * it + b + 1)
                    alone(pool)
                    pool.tensor_scalar(S[:, b, :], S[:, b, :], -1.0, row_max[:, b:b + 1],
                                       ALU.mult, ALU.add).then_inc(shifted, 1)

        @block.scalar
        def _(act):
            act.sem_inc(exp_done, T_SLOTS)
            act.sem_inc(o_stored, 16 * STORES)

            def place_v(h):
                act.wait_ge(v_in, 16 * (h + 1))
                act.activation(V[:, :, 0:D], V_next[:, :, :], ACT.Copy).then_inc(v_placed, 1)

            def exp(it, b, g):
                m = IG * it + NG * b + g
                act.wait_ge(t_ready, m + 1 + IG)
                act.activation(PT[:, b % 2, cols(GB, g), :], Tps[:, g % T_SLOTS, 0:GW].rearrange("p (t q) -> p t q", t=GB),
                               ACT.Exp, scale=-1.0).then_inc(exp_done, 1)

            def first_groups(it):
                act.wait_ge(pt_used, B * it + 1)
                exp(it, 0, 0)
                exp(it, 0, 1)

            def rest(it):
                for b in range(B):
                    if b:
                        act.wait_ge(pt_used, B * it + b + 1)
                    for g in range(2 if b == 0 else 0, NG):
                        exp(it, b, g)

            def take_o(it, slot):
                act.wait_ge(pt_used, B * (it + 1) + PT_SLOTS)
                act.wait_ge(o_stored, 16 * STORES * it)
                act.activation(O[:, slot, :, :], Ops[:, :, :], ACT.Copy).then_inc(o_taken, 1)

            def pair(it, last=None):
                for t in range(2):
                    rest(it + t)
                    if not (t and last == "end"):
                        first_groups(it + t + 1)
                    take_o(it + t, t)

            act.wait_ge(v_ones, 1)
            place_v(0)
            first_groups(0)
            with act.Fori(0, HEADS - 1) as h:
                with act.Fori(0, PAIRS) as qp:
                    pair(h * TILES + 2 * qp)
                place_v(h + 1)
            with act.Fori(0, PAIRS - 1) as qp:
                pair((HEADS - 1) * TILES + 2 * qp)
            pair(ITERS - 2, "end")

        @block.vector
        def _(dve):
            dve.sem_inc(s_taken, S_SLOTS)
            dve.sem_inc(conv_stored, 16)
            with dve.Fori(0, ITERS // 2) as ip:
                h, piece = ip // PIECES, ip % PIECES

                def conv_tap(tap):
                    if tap == 0:
                        dve.wait_ge(vpad_in, 16 * (h + 1))
                        dve.wait_ge(conv_stored, 16 * h)
                    else:
                        dve.wait_ge(conv_step, TAPS * ip + tap)
                    dy, dx = divmod(tap, 5)
                    window = vpad[:, bass.ds((h % 2) * HALF_IN + piece * PIECE + (dy * WP + dx), PIECE)]
                    dst = conv[:, bass.ds((h % 2) * (PIECE * PIECES) + piece * PIECE, PIECE)]
                    if tap == 0:
                        dve.tensor_scalar(dst, window, taps[:, 0:1], conv_bias[:, :], ALU.mult, ALU.add).then_inc(conv_step, 1)
                    else:
                        dve.scalar_tensor_tensor(out=dst, in0=window, scalar=taps[:, tap:tap + 1], in1=dst,
                                                 op0=ALU.mult, op1=ALU.add).then_inc(conv_step, 1)

                for t in range(2):
                    it = ip * 2 + t
                    for b in range(B):
                        for c in range(NCH):
                            n = B * NCH * t + b * NCH + c
                            if b == 0 and c == 0:
                                dve.wait_ge(tile_in, 32 * (it + 1))
                            if c == 0:
                                dve.wait_ge(t_ready, IG * it + NG * (b + 1))
                            dve.wait_ge(s_ready, 2 * IC * ip + n + 1)
                            alone(dve)
                            dve.tensor_tensor_reduce(
                                out=S[:, b, cols(CH, c)].rearrange("p (k n) -> p k n", k=2),
                                in0=Sps[:, n % S_SLOTS, :, 0:GW],
                                in1=mask[:, t, cols(CH, c)].rearrange("p (k n) -> p k n", k=2),
                                scale=1.0, scalar=LOWEST, op0=ALU.add, op1=ALU.max,
                                accum_out=part_max[:, b, c:c + 1]).then_inc(s_taken, 1)
                            if c < NCH - 1:
                                conv_tap(n)
                        dve.wait_ge(s_taken, 2 * IC * ip + n + 1 + S_SLOTS)
                        dve.tensor_reduce(row_max[:, b:b + 1], part_max[:, b, :], AX.X, ALU.max).then_inc(max_ready, 1)
                        conv_tap(n)
                conv_tap(TAPS - 1)

        @block.tensor
        def _(pe):
            pe.sem_inc(t_ready, IG)
            pe.sem_inc(pt_used, PT_SLOTS)

            def scores(it, t, b, c):
                if b == 0 and c == 0:
                    pe.wait_ge(tile_in, 32 * (it + 1))
                    pe.wait_ge(k_in, 48 * (it // TILES + 1))
                n = IC * t + NCH * b + c
                pe.wait_ge(s_taken, IC * it + NCH * b + c + 1)
                for k in range(2):
                    start = ((it // TILES) % 2) * (B * N) + (b * N + c * CH + k * GW)
                    last = pe.matmul(Sps[:, n % S_SLOTS, k, 0:GW], Q[:, t, b, :], K[:, bass.ds(start, GW)],
                                     start=True, stop=True)
                last.then_inc(s_ready, 1)

            def transposes(it, b, g):
                m = IG * it + NG * b + g
                if g == 0:
                    pe.wait_ge(shifted, B * it + b + 1)
                pe.wait_ge(exp_done, m + 1)
                for k in range(GB):
                    last = pe.transpose(Tps[:, g % T_SLOTS, cols(P, k)], S[:, b, cols(P, g * GB + k)], ident[:, :])
                last.then_inc(t_ready, 1)

            def values(it, b, c):
                if b == 0 and c == 0:
                    pe.wait_ge(o_taken, it)
                    pe.wait_ge(v_placed, it // TILES + 1)
                pe.wait_ge(exp_done, IG * it + NG * b + 2 * (c + 1) + T_SLOTS)
                for kt in range(2 * GB * c, 2 * GB * (c + 1)):
                    j = kt % COLS
                    last = pe.matmul(Ops[32 * j:32 * (j + 1), b, :], V[:, b * TILES + kt, :], PT[:, b % 2, kt, :],
                                     start=kt < COLS, stop=kt >= TILES - COLS)
                if c == NCH - 1:
                    last.then_inc(pt_used, 1)

            def iteration(it, t, start=False, end=False):
                for b in range(B):
                    for c in range(NCH):
                        if b + 2 < B:
                            scores(it, t, b + 2, c)
                        elif not end:
                            scores(it + 1, 1 - t, b + 2 - B, c)
                        transposes(it, b, 2 * c)
                        transposes(it, b, 2 * c + 1)
                        if c:
                            values(it, b, c - 1)
                        elif b:
                            values(it, b - 1, NCH - 1)
                        elif not start:
                            values(it - 1, B - 1, NCH - 1)

            for b in range(2):
                for c in range(NCH):
                    scores(0, 0, b, c)
            iteration(0, 0, start=True)
            iteration(1, 1)
            with pe.Fori(1, ITERS // 2 - 1) as ip:
                iteration(ip * 2, 0)
                iteration(ip * 2 + 1, 1)
            iteration(ITERS - 2, 0)
            iteration(ITERS - 1, 1, end=True)
            values(ITERS - 1, B - 1, NCH - 1)


def layer1_attention(nc, a, s, ident, x1):
    with ExitStack() as ctx:
        sb, ps = buffers(nc, ctx, "l")
        sem = sem_maker(nc, ctx, "l")
        SEG = N // D
        num = sb("num", [P, 4, N])
        den = sb("den", [P, 4, SEG])
        den_sum = sb("den_sum", [P, SEG])
        inv = sb("inv", [P, N])
        conv = sb("conv", [P, N])
        xin = sb("xin", [P, TILES, C])
        ln = sb("ln", [P, TILES, C])
        lnT = sb("lnT", [P, N])
        qT = sb("qT", [P, N])
        kT = sb("kT", [P, N])
        v = sb("v", [P, TILES, C])
        q_tile = sb("q_tile", [P, 2, P])
        S = sb("S", [P, 2, N])
        PT = sb("PT", [P, TILES, P])
        weights = sb("weights", [P, 4, C])
        rows = sb("rows", [1, 4, C])
        biases = sb("biases", [P, 2])
        bo_all = sb("bo_all", [P, GB, C])
        bv_all = sb("bv_all", [P, GB, C])
        ones = sb("ones", [1, P])
        eps = sb("eps", [P, 1])
        stats = sb("stats", [P, TILES, 6])
        mv = sb("mv", [P, TILES, 2])
        sd = sb("sd", [P, TILES])
        rstd = sb("rstd", [P, TILES])
        part_max = sb("part_max", [P, 2, NCH])
        neg_max = sb("neg_max", [P, 2])
        total = sb("total", [P, 2])
        inv_total = sb("inv_total", [P, 2])

        Sps = ps("Sps", [P, 2, 2, BANK])
        Tps = ps("Tps", [P, 2, BANK])
        Ops = ps("Ops", [P, 2, BANK])

        weights_in, constants, small_ready, small_taken = sem("weights_in"), sem("constants"), sem("small_ready"), sem("small_taken")
        num_in, den_in, inv_stored, inv_in = sem("num_in"), sem("den_in"), sem("inv_stored"), sem("inv_in")
        den_step, inv_ready, z_step, z_ready = sem("den_step"), sem("inv_ready"), sem("z_step"), sem("z_ready")
        x_biased = sem("x_biased")
        x1_ready, ln_step, var_ready, sd_ready, ln_ready = sem("x1_ready"), sem("ln_step"), sem("var_ready"), sem("sd_ready"), sem("ln_ready")
        t_ready, t_taken, o_ready, o_taken = sem("t_ready"), sem("t_taken"), sem("o_ready"), sem("o_taken")
        q_staged, s_ready, s_taken = sem("q_staged"), sem("s_ready"), sem("s_taken")
        max_ready, p_ready, p_used, inv_step = sem("max_ready"), sem("p_ready"), sem("p_used"), sem("inv_step")

        T_SLOTS = O_SLOTS = S_SLOTS = 2
        T_PRE = 3 * NG
        T_USES = T_PRE + NG * TILES
        O_PRE = 2 * NG
        O_USES = O_PRE + TILES
        S_USES = NCH * TILES

        block = ctx.enter_context(nc.Block())

        @block.sync
        def _(sp):
            for i, w in enumerate(("Wo0", "Wq1", "Wk1", "Wv1")):
                sp.dma_start(weights[:, i, :], a[w]).then_inc(weights_in, 16)
            for i, w in enumerate(("bo0", "bq1", "bk1", "bv1")):
                sp.dma_start(rows[:, i, :], a[w].rearrange("(a n) -> a n", a=1)).then_inc(weights_in, 16)
            with sp.Fori(0, B) as b:
                sp.wait_ge(o_taken, O_USES * b + O_SLOTS)
                sp.dma_start(den[:, :, :], s["den_load"][b]).then_inc(den_in, 16)
                sp.dma_start(num[:, :, :], s["o_load"][b]).then_inc(num_in, 16)
                sp.dma_start(conv[:, :], s["conv"][b]).then_inc(num_in, 16)
                for half in range(2):
                    sp.dma_start(xin[:, cols(HT, half), :], s["x_tiles"][b][:, cols(HT, half), :]).then_inc(num_in, 16)
                sp.wait_ge(inv_ready, b + 1)
                sp.dma_start(s["inv_store"][b], den_sum[:, :]).then_inc(inv_stored, 16)
                sp.wait_ge(inv_stored, 16 * (b + 1))
                sp.dma_start(inv[:, :], s["inv_load"][b].unsqueeze(1).to_broadcast([HEADS, D, N])).then_inc(inv_in, 16)

        @block.gpsimd
        def _(pool):
            pool.memset(ones[:, :], 1.0).then_inc(constants, 1)
            pool.memset(eps[:, :], 1e-5).then_inc(constants, 1)
            pool.wait_ge(small_taken, 3)
            with pool.Fori(0, B) as b:
                pool.wait_ge(num_in, 64 * (b + 1))
                for g in range(NG):
                    last = pool.tensor_tensor(xin[:, cols(GB, g), :], xin[:, cols(GB, g), :], bo_all[:, :, :], ALU.add)
                last.then_inc(x_biased, 1)

        @block.scalar
        def _(act):
            act.sem_inc(t_taken, T_SLOTS)
            act.wait_ge(small_taken, 3)
            with act.Fori(0, B) as b:
                act.wait_ge(var_ready, b + 1)
                act.activation(sd[:, :], mv[:, :, 1:2].rearrange("p t a -> p (t a)"), ACT.Sqrt, bias=eps[:, :]).then_inc(sd_ready, 1)
                for g in range(NG):
                    act.wait_ge(t_ready, T_USES * b + g + 1)
                    act.activation(lnT[:, cols(GW, g)], Tps[:, g % 2, 0:GW], ACT.Copy).then_inc(t_taken, 1)
                for m in range(2):
                    for g in range(NG):
                        act.wait_ge(t_ready, T_USES * b + NG * (m + 1) + g + 1)
                        act.activation((qT, kT)[m][:, cols(GW, g)], Tps[:, g % 2, 0:GW], ACT.Identity,
                                       bias=biases[:, m:m + 1]).then_inc(t_taken, 1)
                with act.Fori(0, TILES // 2) as qp:
                    for t in range(2):
                        qt = 2 * qp + t
                        act.wait_ge(max_ready, TILES * b + qt + 1)
                        act.activation(S[:, t, :], S[:, t, :], ACT.Exp, bias=neg_max[:, t:t + 1],
                                       accum_out=total[:, t:t + 1]).then_inc(p_ready, 1)
                        for g in range(NG):
                            if g == 0:
                                act.wait_ge(o_ready, O_USES * b + O_PRE + qt)
                            act.wait_ge(t_ready, T_USES * b + T_PRE + NG * qt + g + 1)
                            act.activation(PT[:, cols(GB, g), :], Tps[:, g % 2, 0:GW].rearrange("p (t q) -> p t q", t=GB),
                                           ACT.Copy).then_inc(t_taken, 1)

        @block.tensor
        def _(pe):
            pe.wait_ge(weights_in, 16 * 8)
            pe.wait_ge(constants, 2)
            for i in range(2):
                pe.matmul(Tps[:, 0, i:i + 1], rows[0:1, 1 + i, :], ones[0:1, 0:1], start=True, stop=True)
            pe.matmul(Tps[:, 1, 0:C], ones[0:1, :], rows[0:1, 0, :], start=True, stop=True)
            pe.matmul(Tps[:, 1, C:2 * C], ones[0:1, :], rows[0:1, 3, :], start=True, stop=True).then_inc(small_ready, 1)
            pe.wait_ge(small_taken, 3)

            with pe.Fori(0, B) as b:
                def tps(n):
                    pe.wait_ge(t_taken, T_USES * b + n + 1)
                    return Tps[:, n % 2, 0:GW]

                def ops(n):
                    pe.wait_ge(o_taken, O_USES * b + n + 1)
                    return Ops[:, n % 2, 0:GW]

                def scores(qt, t):
                    pe.wait_ge(q_staged, TILES * b + qt + 1)
                    for c in range(NCH):
                        n = NCH * t + c
                        pe.wait_ge(s_taken, S_USES * b + NCH * qt + c + 1)
                        for k in range(2):
                            last = pe.matmul(Sps[:, n % 2, k, 0:GW], q_tile[:, t, :],
                                             kT[:, c * CH + k * GW:c * CH + (k + 1) * GW], start=True, stop=True)
                        last.then_inc(s_ready, 1)

                def probabilities(qt, t):
                    pe.wait_ge(p_ready, TILES * b + qt + 1)
                    for g in range(NG):
                        pe.wait_ge(t_taken, T_USES * b + T_PRE + NG * qt + g + 1)
                        for k in range(GB):
                            last = pe.transpose(Tps[:, g % 2, cols(P, k)], S[:, t, cols(P, g * GB + k)], ident[:, :])
                        last.then_inc(t_ready, 1)

                def values(qt, t):
                    pe.wait_ge(o_taken, O_USES * b + O_PRE + qt + 1)
                    for kt in range(TILES):
                        if kt % GB == 0:
                            pe.wait_ge(t_taken, T_USES * b + T_PRE + NG * qt + kt // GB + 1 + T_SLOTS)
                        last = pe.matmul(Ops[:, t, 0:C], PT[:, kt, :], v[:, kt, :], start=kt == 0, stop=kt == TILES - 1)
                    last.then_inc(o_ready, 1)

                def tile(qt, t, ahead=True):
                    if ahead:
                        scores(qt + 1, 1 - t)
                    probabilities(qt, t)
                    values(qt, t)

                pe.wait_ge(z_ready, b + 1)
                for g in range(NG):
                    dst = ops(g)
                    for k in range(GB):
                        last = pe.matmul(dst[:, cols(P, k)], num[:, 0, cols(P, g * GB + k)], weights[:, 0, :],
                                         start=True, stop=True)
                    last.then_inc(o_ready, 1)
                pe.wait_ge(ln_ready, b + 1)
                for g in range(NG):
                    dst = tps(g)
                    for k in range(GB):
                        last = pe.transpose(dst[:, cols(P, k)], ln[:, g * GB + k, :], ident[:, :])
                    last.then_inc(t_ready, 1)
                pe.wait_ge(t_taken, T_USES * b + NG + T_SLOTS)
                for m in range(2):
                    for g in range(NG):
                        pe.matmul(tps(NG * (m + 1) + g), weights[:, 1 + m, :], lnT[:, cols(GW, g)],
                                  start=True, stop=True).then_inc(t_ready, 1)
                for g in range(NG):
                    dst = ops(NG + g)
                    for k in range(GB):
                        last = pe.matmul(dst[:, cols(P, k)], lnT[:, cols(P, g * GB + k)], weights[:, 3, :],
                                         start=True, stop=True)
                    last.then_inc(o_ready, 1)
                pe.wait_ge(t_taken, T_USES * b + T_PRE + T_SLOTS)
                pe.wait_ge(o_taken, O_USES * b + O_PRE + O_SLOTS)
                scores(0, 0)
                with pe.Fori(0, TILES // 2 - 1) as qp:
                    tile(2 * qp, 0)
                    tile(2 * qp + 1, 1)
                tile(TILES - 2, 0)
                tile(TILES - 1, 1, ahead=False)

        @block.vector
        def _(dve):
            dve.sem_inc(o_taken, O_SLOTS)
            dve.sem_inc(s_taken, S_SLOTS)
            dve.wait_ge(small_ready, 1)
            dve.tensor_copy(biases[:, :], Tps[:, 0, 0:2]).then_inc(small_taken, 1)
            for dst, src in ((bo_all, Tps[:, 1, 0:C]), (bv_all, Tps[:, 1, C:2 * C])):
                for k in range(GB):
                    last = dve.tensor_copy(dst[:, k, :], src)
                last.then_inc(small_taken, 1)
            dve.wait_ge(small_taken, 3)
            with dve.Fori(0, B) as b:
                def image(lo, hi):
                    return x1[:, bass.ds(b * TILES + lo, hi - lo), :]

                dve.wait_ge(den_in, 16 * (b + 1))
                for n, (x, y, z) in enumerate(((0, 1, 0), (2, 3, 2))):
                    last = dve.tensor_tensor(den[:, x, :], den[:, x, :], den[:, y, :], ALU.add)
                last.then_inc(den_step, 1)
                dve.wait_ge(den_step, 2 * b + 1)
                dve.tensor_tensor(den_sum[:, :], den[:, 0, :], den[:, 2, :], ALU.add).then_inc(den_step, 1)
                dve.wait_ge(den_step, 2 * b + 2)
                dve.reciprocal(den_sum[:, :], den_sum[:, :]).then_inc(inv_ready, 1)
                dve.wait_ge(num_in, 64 * (b + 1))
                for x in (0, 2):
                    last = dve.tensor_tensor(num[:, x, :], num[:, x, :], num[:, x + 1, :], ALU.add)
                last.then_inc(z_step, 1)
                dve.wait_ge(z_step, 3 * b + 1)
                dve.tensor_tensor(num[:, 0, :], num[:, 0, :], num[:, 2, :], ALU.add).then_inc(z_step, 1)
                dve.wait_ge(z_step, 3 * b + 2)
                dve.wait_ge(inv_in, 16 * (b + 1))
                dve.tensor_tensor(num[:, 0, :], num[:, 0, :], inv[:, :], ALU.mult).then_inc(z_step, 1)
                dve.wait_ge(z_step, 3 * b + 3)
                dve.tensor_tensor(num[:, 0, :], num[:, 0, :], conv[:, :], ALU.add).then_inc(z_ready, 1)
                dve.wait_ge(x_biased, b + 1)
                for g in range(NG):
                    dve.wait_ge(o_ready, O_USES * b + g + 1)
                    alone(dve)
                    last = dve.tensor_tensor(image(g * GB, (g + 1) * GB), Ops[:, g % 2, 0:GW].rearrange("p (t c) -> p t c", t=GB),
                                             xin[:, cols(GB, g), :], ALU.add).then_inc(o_taken, 1)
                dve.wait_ge(o_taken, O_USES * b + NG + O_SLOTS)
                alone(dve)
                for t in range(TILES):
                    last = dve.bn_stats(stats[:, t, :], image(t, t + 1).rearrange("p t c -> p (t c)"))
                last.then_inc(ln_step, 1)
                dve.wait_ge(ln_step, 2 * b + 1)
                alone(dve)
                for t in range(TILES):
                    last = dve.bn_aggr(mv[:, t, :], stats[:, t, :])
                last.then_inc(var_ready, 1)
                dve.wait_ge(sd_ready, b + 1)
                dve.reciprocal(rstd[:, :], sd[:, :]).then_inc(ln_step, 1)
                dve.wait_ge(ln_step, 2 * b + 2)
                for t in range(TILES):
                    last = dve.tensor_scalar(ln[:, t, :], image(t, t + 1).rearrange("p t c -> p (t c)"), mv[:, t, 0:1], rstd[:, t:t + 1],
                                             ALU.subtract, ALU.mult)
                last.then_inc(ln_ready, 1)
                for g in range(NG):
                    dve.wait_ge(o_ready, O_USES * b + NG + g + 1)
                    dve.tensor_tensor(v[:, cols(GB, g), :], Ops[:, g % 2, 0:GW].rearrange("p (t c) -> p t c", t=GB),
                                      bv_all[:, :, :], ALU.add).then_inc(o_taken, 1)

                def stage(qt, t):
                    dve.wait_ge(small_taken, 3)
                    dve.tensor_copy(q_tile[:, t, :], qT[:, bass.ds(qt * P, P)]).then_inc(q_staged, 1)

                def take_scores(qt, t):
                    for c in range(NCH):
                        n = NCH * t + c
                        if c == 0:
                            dve.wait_ge(t_taken, T_USES * b + T_PRE + NG * (qt - 1) + T_SLOTS)
                        dve.wait_ge(s_ready, S_USES * b + NCH * qt + c + 1)
                        dve.tensor_scalar(S[:, t, cols(CH, c)].rearrange("p (k n) -> p k n", k=2), Sps[:, n % 2, :, 0:GW],
                                          1.0, None, ALU.mult, ALU.max, accum_out=part_max[:, t, c:c + 1]).then_inc(s_taken, 1)
                    dve.wait_ge(s_taken, S_USES * b + NCH * (qt + 1) + S_SLOTS)
                    dve.tensor_reduce(neg_max[:, t:t + 1], part_max[:, t, :], AX.X, ALU.max, negate=True).then_inc(max_ready, 1)

                def take_values(qt, t):
                    dve.wait_ge(p_ready, TILES * b + qt + 1)
                    dve.reciprocal(inv_total[:, t:t + 1], total[:, t:t + 1]).then_inc(inv_step, 1)
                    dve.wait_ge(inv_step, TILES * b + qt + 1)
                    dve.wait_ge(o_ready, O_USES * b + O_PRE + qt + 1)
                    alone(dve)
                    row = x1[:, bass.ds(b * TILES + qt, 1), :].rearrange("p t c -> p (t c)")
                    dve.scalar_tensor_tensor(out=row, in0=Ops[:, t, 0:C], scalar=inv_total[:, t:t + 1], in1=row,
                                             op0=ALU.mult, op1=ALU.add).then_inc(o_taken, 1)

                def tile(qt, t, ahead=True, stage_ahead=True):
                    if ahead:
                        take_scores(qt + 1, 1 - t)
                    if stage_ahead:
                        stage(qt + 3, 1 - t)
                    take_values(qt, t)

                dve.wait_ge(t_taken, T_USES * b + T_PRE + T_SLOTS)
                stage(0, 0)
                stage(1, 1)
                take_scores(0, 0)
                stage(2, 0)
                with dve.Fori(0, TILES // 2 - 2) as qp:
                    tile(2 * qp, 0)
                    tile(2 * qp + 1, 1)
                tile(TILES - 4, 0)
                tile(TILES - 3, 1, stage_ahead=False)
                tile(TILES - 2, 0, stage_ahead=False)
                tile(TILES - 1, 1, ahead=False, stage_ahead=False)


def layer1_ffn(nc, a, s, ident, x1, out):
    with ExitStack() as ctx:
        sb, ps = buffers(nc, ctx, "e")
        sem = sem_maker(nc, ctx, "e")
        ln = sb("ln", [P, B * TILES, C])
        lnT = sb("lnT", [P, B, N])
        W1 = sb("W1", [P, E, FF])
        W2 = sb("W2", [P, E, FH * C])
        b1_rows = sb("b1_rows", [E * FH, P])
        b1 = sb("b1", [P, E, FH])
        b2 = sb("b2", [P, E, C])
        Wr = sb("Wr", [P, E])
        br = sb("br", [1, E])
        vectors = sb("vectors", [1, 2, C])
        gamma = sb("gamma", [P, 1, C])
        beta = sb("beta", [P, 1, C])
        ones = sb("ones", [P, P])
        eps = sb("eps", [P, 1])
        stats = sb("stats", [P, TILES, 6])
        mv = sb("mv", [P, TILES, 2])
        sd = sb("sd", [P, TILES])
        rstd = sb("rstd", [P, TILES])
        sums = sb("sums", [P, B, NG])
        means = sb("means", [P, B])
        r = sb("r", [B, 16, E])
        rc = sb("rc", [B, 16])
        greater = sb("greater", [B, E, 2 * E])
        choice = sb("choice", [B, 2 * TOPK, E])
        pick = sb("pick", [B, B, P])
        sel = sb("sel", [P, B, 2 * TOPK * E])
        w1s = sb("w1s", [P, 2, TOPK, FF])
        w2s = sb("w2s", [P, 2, TOPK, FH * C])
        b1s = sb("b1s", [P, 2, TOPK, FH])
        b2s = sb("b2s", [P, 2, C])
        hid = sb("hid", [P, 2, TOPK * FH, GW])
        ystats = sb("ystats", [P, TILES, 6])
        ymv = sb("ymv", [P, TILES, 2])
        ysd = sb("ysd", [P, TILES])
        yrstd = sb("yrstd", [P, TILES])
        ln_stage = sb("ln_stage", [P, TILES, C])

        Hps = ps("Hps", [P, 4, BANK])
        Yps = ps("Yps", [P, 2, BANK])
        Rps = ps("Rps", [P, 2, BANK])

        weights_in, constants, small_ready, small_taken = sem("weights_in"), sem("constants"), sem("small_ready"), sem("small_taken")
        ln_step, var_ready, sd_ready, ln_ready = sem("ln_step"), sem("var_ready"), sem("sd_ready"), sem("ln_ready")
        t_ready, t_taken = sem("t_ready"), sem("t_taken")
        route_pe, route_act, route_dve = sem("route_pe"), sem("route_act"), sem("route_dve")
        select_step, selected = sem("select_step"), sem("selected")
        h_ready, h_taken, y_ready, y_taken = sem("h_ready"), sem("h_taken"), sem("y_ready"), sem("y_taken")
        base_ready, y_step, yvar_ready, ysd_ready = sem("base_ready"), sem("y_step"), sem("yvar_ready"), sem("ysd_ready")
        y_normed, res_ready, scaled, out_ready, out_stored = sem("y_normed"), sem("res_ready"), sem("scaled"), sem("out_ready"), sem("out_stored")
        mean_step, sel_ready = sem("mean_step"), sem("sel_ready")
        ROUTE_STEPS = 21
        SELECT_STEPS = E + TOPK * E - 1
        HK = TOPK * FH

        block = ctx.enter_context(nc.Block())

        @block.sync
        def _(sp):
            sp.dma_start(W1[:, :, :], a["W1"].rearrange("e p f -> p e f")).then_inc(weights_in, 16)
            sp.dma_start(W2[:, :, :].rearrange("p e (h d) -> p e h d", h=FH), a["W2"].rearrange("e (h p) d -> p e h d", p=P)).then_inc(weights_in, 16)
            sp.dma_start(b1_rows[:, :], a["b1"].rearrange("e (h p) -> (e h) p", p=P)).then_inc(weights_in, 16)
            sp.dma_start(b2[:, :, :], a["b2"].unsqueeze(0).to_broadcast([P, E, C])).then_inc(weights_in, 16)
            sp.dma_start(Wr[:, :], a["Wr"]).then_inc(weights_in, 16)
            sp.dma_start(br[:, :], a["br"].rearrange("(a n) -> a n", a=1)).then_inc(weights_in, 16)
            sp.dma_start(vectors[:, 0, :], a["gamma"].rearrange("(a n) -> a n", a=1)).then_inc(weights_in, 16)
            sp.dma_start(vectors[:, 1, :], a["beta"].rearrange("(a n) -> a n", a=1)).then_inc(weights_in, 16)
            with sp.Fori(0, B) as b:
                for half in range(2):
                    sp.wait_ge(out_ready, 2 * b + half + 1)
                    alone(sp)
                    sp.dma_start(out[b][:, cols(HT, half), :], ln[:, bass.ds(b * TILES + half * HT, HT), :]).then_inc(out_stored, 16)
            sp.wait_ge(out_stored, 32 * B)

        @block.gpsimd
        def _(pool):
            pool.memset(ones[:, :], 1.0).then_inc(constants, 1)
            pool.memset(eps[:, :], 1e-5).then_inc(constants, 1)
            pool.memset(greater[:, :, :], 0.0).then_inc(constants, 1)
            pool.wait_ge(small_taken, 3)
            with pool.Fori(0, B // 2) as bp:
                for t in range(2):
                    b = 2 * bp + t

                    def tokens(of, half):
                        return of[:, bass.ds(b * TILES + half * HT, HT), :]

                    def everywhere(vector):
                        return vector.to_broadcast([P, HT, C])

                    pool.wait_ge(selected, b + 1)
                    alone(pool)
                    for half in range(2):
                        last = pool.tensor_tensor(tokens(ln, half), tokens(ln, half), everywhere(b2s[:, t:t + 1, :]), ALU.add)
                    last.then_inc(base_ready, 1)
                    for half in range(2):
                        last = pool.tensor_tensor(tokens(x1, half), tokens(x1, half), everywhere(beta[:, :, :]), ALU.add)
                    last.then_inc(res_ready, 1)
                    for half in range(2):
                        pool.wait_ge(y_normed, 2 * b + half + 1)
                        alone(pool)
                        pool.tensor_tensor(tokens(ln, half), tokens(ln, half), everywhere(gamma[:, :, :]), ALU.mult).then_inc(scaled, 1)
                        pool.wait_ge(res_ready, b + 1)
                        pool.wait_ge(scaled, 2 * b + half + 1)
                        alone(pool)
                        pool.tensor_tensor(tokens(ln, half), tokens(ln, half), tokens(x1, half), ALU.add).then_inc(out_ready, 1)

        @block.scalar
        def _(act):
            act.sem_inc(t_taken, 2)
            act.sem_inc(h_taken, 4)
            with act.Fori(0, B) as b:
                act.wait_ge(var_ready, b + 1)
                act.activation(sd[:, :], mv[:, :, 1:2].rearrange("p t a -> p (t a)"), ACT.Sqrt, bias=eps[:, :]).then_inc(sd_ready, 1)
                for g in range(NG):
                    act.wait_ge(t_ready, NG * b + g + 1)
                    alone(act)
                    act.activation(lnT[:, bass.ds(b, 1), cols(GW, g)].rearrange("p a n -> p (a n)"), Rps[:, g % 2, 0:GW], ACT.Copy,
                                   accum_out=sums[:, bass.ds(b, 1), g:g + 1].rearrange("p a n -> p (a n)")).then_inc(t_taken, 1)
            act.wait_ge(route_dve, 2)
            act.activation(r[:, 1, :], r[:, 0, :], ACT.Exp, bias=rc[:, 0:1], accum_out=rc[:, 1:2]).then_inc(route_act, 1)
            act.wait_ge(route_dve, 9)
            act.activation(r[:, 6, :], r[:, 5, :], ACT.Exp, bias=rc[:, 3:4], accum_out=rc[:, 4:5]).then_inc(route_act, 1)
            act.wait_ge(route_dve, 17)
            act.activation(rc[:, 9:10], rc[:, 8:9], ACT.Exp).then_inc(route_act, 1)

            def gelu(b, g):
                n = NG * b + g
                act.wait_ge(selected, b + 1)
                act.wait_ge(y_ready, max(n - 1, 0))
                for i in range(HK):
                    act.wait_ge(h_ready, HK * n + i + 1)
                    act.activation(hid[:, g % 2, i, :], Hps[:, i, 0:GW], ACT.Gelu,
                                   bias=b1s[:, b % 2, i // FH, i % FH:i % FH + 1]).then_inc(h_taken, 1)

            gelu(0, 0)
            for b in range(B):
                for g in range(1, NG):
                    gelu(b, g)
                if b + 1 < B:
                    gelu(b + 1, 0)
                act.wait_ge(yvar_ready, b + 1)
                act.activation(ysd[:, :], ymv[:, :, 1:2].rearrange("p t a -> p (t a)"), ACT.Sqrt, bias=eps[:, :]).then_inc(ysd_ready, 1)

        @block.tensor
        def _(pe):
            pe.wait_ge(weights_in, 16 * 8)
            pe.wait_ge(constants, 3)
            pe.matmul(Hps[:, 0, 0:C], ones[0:1, :], vectors[0:1, 0, :], start=True, stop=True)
            pe.matmul(Hps[:, 1, 0:C], ones[0:1, :], vectors[0:1, 1, :], start=True, stop=True)
            pe.transpose(Hps[:, 2, 0:E * FH], b1_rows[:, :], ident[0:E * FH, 0:E * FH]).then_inc(small_ready, 1)
            with pe.Fori(0, B) as b:
                pe.wait_ge(ln_ready, b + 1)
                for g in range(NG):
                    pe.wait_ge(t_taken, NG * b + g + 1)
                    for k in range(GB):
                        last = pe.transpose(Rps[:, g % 2, cols(P, k)], ln_stage[:, g * GB + k, :], ident[:, :])
                    last.then_inc(t_ready, 1)
            pe.wait_ge(route_dve, 1)
            pe.matmul(Rps[0:B, 0, 0:E], means[:, :], Wr[:, :], start=True, stop=False)
            pe.matmul(Rps[0:B, 0, 0:E], ones[0:1, 0:B], br[:, :], start=False, stop=True).then_inc(route_pe, 1)
            pe.wait_ge(route_dve, 4)
            pe.matmul(Rps[0:B, 0, 0:E], ones[0:B, 0:B], r[:, 2, :], start=True, stop=True).then_inc(route_pe, 1)
            pe.wait_ge(route_dve, ROUTE_STEPS)
            for b in range(B):
                last = pe.matmul(Rps[:, 0, cols(2 * TOPK * E, b)], pick[:, b, :], choice[:, :, :].rearrange("b s e -> b (s e)"), start=True, stop=True)
            last.then_inc(route_pe, 1)
            pe.wait_ge(small_taken, 3)

            def hidden(b, t, g):
                n = NG * b + g
                if g == 0:
                    pe.wait_ge(selected, b + 1)
                for i in range(HK):
                    pe.wait_ge(h_taken, HK * n + i + 1)
                    pe.matmul(Hps[:, i, 0:GW], w1s[:, t, i // FH, cols(P, i % FH)],
                              lnT[:, bass.ds(b, 1), cols(GW, g)].rearrange("p a n -> p (a n)"), start=True, stop=True).then_inc(h_ready, 1)

            def outputs(b, t, g):
                n = NG * b + g
                pe.wait_ge(h_taken, HK * (n + 1) + 4)
                pe.wait_ge(y_taken, n + 1)
                for k in range(GB):
                    for i in range(HK):
                        last = pe.matmul(Yps[:, g % 2, cols(P, k)], hid[:, g % 2, i, cols(P, k)],
                                         w2s[:, t, i // FH, cols(C, i % FH)], start=i == 0, stop=i == HK - 1)
                last.then_inc(y_ready, 1)

            hidden(0, 0, 0)
            with pe.Fori(0, B // 2 - 1) as bp:
                for t in range(2):
                    for g in range(NG):
                        if g + 1 < NG:
                            hidden(2 * bp + t, t, g + 1)
                        else:
                            hidden(2 * bp + t + 1, 1 - t, 0)
                        outputs(2 * bp + t, t, g)
            for t in range(2):
                for g in range(NG):
                    if g + 1 < NG:
                        hidden(B - 2 + t, t, g + 1)
                    elif t == 0:
                        hidden(B - 1, 1, 0)
                    outputs(B - 2 + t, t, g)

        @block.vector
        def _(dve):
            dve.sem_inc(y_taken, 2)
            dve.wait_ge(small_ready, 1)
            dve.tensor_copy(gamma[:, 0, :], Hps[:, 0, 0:C]).then_inc(small_taken, 1)
            dve.tensor_copy(beta[:, 0, :], Hps[:, 1, 0:C]).then_inc(small_taken, 1)
            dve.tensor_copy(b1[:, :, :].rearrange("p e h -> p (e h)"), Hps[:, 2, 0:E * FH]).then_inc(small_taken, 1)
            with dve.Fori(0, B) as b:
                for t in range(TILES):
                    tok = x1[:, bass.ds(b * TILES + t, 1), :].rearrange("p t c -> p (t c)")
                    last = dve.bn_stats(stats[:, t, :], tok)
                last.then_inc(ln_step, 1)
                dve.wait_ge(ln_step, 3 * b + 1)
                alone(dve)
                for t in range(TILES):
                    last = dve.bn_aggr(mv[:, t, :], stats[:, t, :])
                last.then_inc(var_ready, 1)
                dve.wait_ge(sd_ready, b + 1)
                dve.reciprocal(rstd[:, :], sd[:, :]).then_inc(ln_step, 1)
                dve.wait_ge(ln_step, 3 * b + 2)
                dve.wait_ge(t_ready, NG * b)
                for t in range(TILES):
                    tok = x1[:, bass.ds(b * TILES + t, 1), :].rearrange("p t c -> p (t c)")
                    last = dve.tensor_scalar(ln_stage[:, t, :], tok, mv[:, t, 0:1], rstd[:, t:t + 1], ALU.subtract, ALU.mult)
                last.then_inc(ln_ready, 1)
                dve.wait_ge(ln_ready, b + 1)
                alone(dve)
                dve.tensor_copy(ln[:, bass.ds(b * TILES, TILES), :], ln_stage[:, :, :]).then_inc(ln_step, 1)

            steps = [0]

            def step(instruction):
                steps[0] += 1
                instruction.then_inc(route_dve, 1)
                dve.wait_ge(route_dve, steps[0])

            dve.wait_ge(t_taken, NG * B + 2)
            dve.tensor_reduce(means[:, :], sums[:, :, :], AX.X, ALU.add).then_inc(mean_step, 1)
            dve.wait_ge(mean_step, 1)
            for b in range(B):
                dve.tensor_scalar(pick[:, b, :], ones[0:B, :], ident[0:B, b:b + 1], None, ALU.mult)
            step(dve.tensor_scalar(means[:, :], means[:, :], 1.0 / N, None, ALU.mult))
            dve.wait_ge(route_pe, 1)
            dve.tensor_copy(r[:, 0, :], Rps[0:B, 0, 0:E])
            step(dve.tensor_reduce(rc[:, 0:1], Rps[0:B, 0, 0:E], AX.X, ALU.max, negate=True))
            dve.wait_ge(route_act, 1)
            step(dve.reciprocal(rc[:, 2:3], rc[:, 1:2]))
            step(dve.tensor_scalar(r[:, 2, :], r[:, 1, :], rc[:, 2:3], None, ALU.mult))
            dve.wait_ge(route_pe, 2)
            step(dve.tensor_scalar(r[:, 3, :], Rps[0:B, 0, 0:E], float(N), None, ALU.mult))
            step(dve.reciprocal(r[:, 4, :], r[:, 3, :]))
            step(dve.tensor_scalar(r[:, 4, :], r[:, 4, :], CAPACITY, 1.0, ALU.mult, ALU.min))
            step(dve.tensor_tensor(r[:, 5, :], r[:, 2, :], r[:, 4, :], ALU.mult))
            step(dve.tensor_reduce(rc[:, 3:4], r[:, 5, :], AX.X, ALU.max, negate=True))
            dve.wait_ge(route_act, 2)
            step(dve.reciprocal(rc[:, 5:6], rc[:, 4:5]))
            step(dve.tensor_scalar(r[:, 7, :], r[:, 6, :], rc[:, 5:6], None, ALU.mult))
            for e in range(E):
                last = dve.tensor_scalar(greater[:, e, 0:E], r[:, 7, :], r[:, 7, e:e + 1], None, ALU.is_gt)
                if e:
                    last = dve.tensor_scalar(greater[:, e, E:E + e], r[:, 7, 0:e], r[:, 7, e:e + 1], None, ALU.is_equal)
            step(last)
            step(dve.tensor_reduce(r[:, 8, :], greater[:, :, :], AX.X, ALU.add))
            for k in range(TOPK):
                last = dve.tensor_scalar(choice[:, k, :], r[:, 8, :], float(k), None, ALU.is_equal)
            step(last)
            for k in range(TOPK):
                last = dve.tensor_tensor(r[:, 9 + k, :], choice[:, k, :], r[:, 7, :], ALU.mult)
            step(last)
            step(dve.tensor_reduce(rc[:, 6:8], r[:, 9:9 + TOPK, :], AX.X, ALU.add))
            step(dve.tensor_tensor(rc[:, 8:9], rc[:, 7:8], rc[:, 6:7], ALU.subtract))
            assert steps[0] == 17, steps
            dve.wait_ge(route_act, 3)
            step(dve.tensor_scalar(rc[:, 10:11], rc[:, 9:10], 1.0, None, ALU.add))
            step(dve.reciprocal(rc[:, 11:12], rc[:, 10:11]))
            step(dve.tensor_tensor(rc[:, 12:13], rc[:, 11:12], rc[:, 9:10], ALU.mult))
            for k in range(TOPK):
                last = dve.tensor_scalar(choice[:, TOPK + k, :], choice[:, k, :], rc[:, 11 + k:12 + k], None, ALU.mult)
            step(last)
            assert steps[0] == ROUTE_STEPS, steps
            dve.wait_ge(route_pe, 3)
            dve.tensor_copy(sel[:, :, :].rearrange("p b s -> p (b s)"), Rps[:, 0, 0:B * 2 * TOPK * E]).then_inc(sel_ready, 1)
            dve.wait_ge(sel_ready, 1)

            def select(b, t):
                for e in range(E):
                    def of(slot):
                        return sel[:, bass.ds(b, 1), slot * E + e:slot * E + e + 1].rearrange("p a n -> p (a n)")

                    jobs = []
                    for k in range(TOPK):
                        jobs.append((w1s[:, t, k, :], W1[:, e, :], of(k)))
                        jobs.append((b1s[:, t, k, :], b1[:, e, :], of(k)))
                        jobs.append((w2s[:, t, k, :], W2[:, e, :], of(TOPK + k)))
                    for dst, src, factor in jobs:
                        if e == 0:
                            last = dve.tensor_scalar(dst, src, factor, None, ALU.mult)
                        else:
                            last = dve.scalar_tensor_tensor(out=dst, in0=src, scalar=factor, in1=dst, op0=ALU.mult, op1=ALU.add)
                    last.then_inc(select_step, 1)
                    dve.wait_ge(select_step, SELECT_STEPS * b + e + 1)
                for k in range(TOPK):
                    for e in range(E):
                        factor = sel[:, bass.ds(b, 1), (TOPK + k) * E + e:(TOPK + k) * E + e + 1].rearrange("p a n -> p (a n)")
                        if k == 0 and e == 0:
                            last = dve.tensor_scalar(b2s[:, t, :], b2[:, e, :], factor, None, ALU.mult)
                        else:
                            last = dve.scalar_tensor_tensor(out=b2s[:, t, :], in0=b2[:, e, :], scalar=factor, in1=b2s[:, t, :],
                                                            op0=ALU.mult, op1=ALU.add)
                        if k == TOPK - 1 and e == E - 1:
                            last.then_inc(selected, 1)
                        else:
                            last.then_inc(select_step, 1)
                            dve.wait_ge(select_step, SELECT_STEPS * b + E + k * E + e + 1)

            def close(b, g):
                n = NG * b + g
                if g == 0:
                    dve.wait_ge(base_ready, b + 1)
                dve.wait_ge(y_ready, n + 1)
                alone(dve)
                tok = ln[:, bass.ds(b * TILES + g * GB, GB), :]
                dve.tensor_tensor(tok, Yps[:, g % 2, 0:GW].rearrange("p (t c) -> p t c", t=GB), tok, ALU.add).then_inc(y_taken, 1)
                dve.wait_ge(y_taken, n + 1 + 2)
                alone(dve)
                for k in range(GB):
                    last = dve.bn_stats(ystats[:, g * GB + k, :], ln[:, bass.ds(b * TILES + g * GB + k, 1), :].rearrange("p t c -> p (t c)"))
                last.then_inc(y_step, 1)

            def finish(b):
                dve.wait_ge(y_step, (NG + 1) * b + NG)
                alone(dve)
                for t in range(TILES):
                    last = dve.bn_aggr(ymv[:, t, :], ystats[:, t, :])
                last.then_inc(yvar_ready, 1)
                dve.wait_ge(ysd_ready, b + 1)
                dve.reciprocal(yrstd[:, :], ysd[:, :]).then_inc(y_step, 1)
                dve.wait_ge(y_step, (NG + 1) * (b + 1))
                alone(dve)
                for t in range(TILES):
                    row = ln[:, bass.ds(b * TILES + t, 1), :].rearrange("p t c -> p (t c)")
                    last = dve.tensor_scalar(row, row, ymv[:, t, 0:1], yrstd[:, t:t + 1], ALU.subtract, ALU.mult)
                    if t % HT == HT - 1:
                        last.then_inc(y_normed, 1)

            select(0, 0)
            with dve.Fori(0, B // 2 - 1) as bp:
                for t in range(2):
                    select(2 * bp + t + 1, 1 - t)
                    for g in range(NG):
                        close(2 * bp + t, g)
                    finish(2 * bp + t)
            for t in range(2):
                if t == 0:
                    select(B - 1, 1)
                for g in range(NG):
                    close(B - 2 + t, g)
                finish(B - 2 + t)


def hybrid(nc, a, out):
    def scratch(name, n, dt=F32):
        return nc.dram_tensor(name, (n,), dt, kind="Internal").ap()

    q = scratch("q_parts", HEADS * KR * B * N, BF16).rearrange(
        "(h s d b n) -> h s d b n", h=HEADS, s=len(Q_SLOTS), d=D, b=B)
    k = scratch("k_parts", HEADS * 3 * D * B * N, BF16).rearrange(
        "(h s d b n) -> h s d b n", h=HEADS, s=3, d=D, b=B)
    v = scratch("v_heads", HEADS * P * B * TILES * D).rearrange("(h p b x) -> h p b x", h=HEADS, p=P, b=B)
    num = scratch("numerators", B * 4 * C * N)
    den = scratch("denominators", B * 4 * HEADS * N)
    inv = scratch("inverses", B * HEADS * N).rearrange("(b h n) -> b h n", b=B, h=HEADS)
    vpad = scratch("v_padded", B * C * IMAGE_IN).rearrange("(b c n) -> b c n", b=B, c=C)
    conv = scratch("conv_out", B * C * N)
    s = {
        "x_tiles": a["x"].rearrange("b h w c -> b (h w) c").rearrange("b (t p) c -> b p t c", p=P),
        "mask": a["mask"].rearrange("h (t p) n -> (h t) p n", p=P),
        "q_store": q.rearrange("h s d b n -> b s h d n"),
        "k_store": k.rearrange("h s d b n -> b s h d n"),
        "v_store": v.rearrange("h p b x -> b p h x"),
        "q_load": q.rearrange("h s d b n -> h (s d) b n"),
        "k_load": k.rearrange("h s d b n -> h (s d) (b n)"),
        "v_load": v.rearrange("h p b x -> h p (b x)"),
        "o_store": num.rearrange("(b j h d n) -> j h d b n", b=B, j=4, h=HEADS, d=D),
        "o_load": num.rearrange("(b j c n) -> b c j n", b=B, j=4, c=C),
        "den_store": den.rearrange("(b j h n) -> h j b n", b=B, j=4, h=HEADS),
        "den_load": den.rearrange("(b j p n) -> b p j n", b=B, j=4, p=P),
        "inv_store": inv.rearrange("b h (s n) -> b (h s) n", s=D),
        "inv_load": inv,
        "vpad_store": vpad,
        "vpad_load": vpad,
        "conv_store": conv.rearrange("(b c f h w) -> b f c h w", b=B, c=C, f=2, w=W),
        "conv": conv.rearrange("(b c n) -> b c n", b=B, c=C),
    }
    out_tiles = out.rearrange("b h w c -> b (h w) c").rearrange("b (t p) c -> b p t c", p=P)
    with ExitStack() as ctx:
        ident = ctx.enter_context(nc.sbuf_tensor("ident", [P, P], F32))
        taps = ctx.enter_context(nc.sbuf_tensor("taps", [P, TAPS], F32))
        conv_bias = ctx.enter_context(nc.sbuf_tensor("conv_bias", [P, 1], F32))
        layer0_front(nc, {k: a[k] for k in ("Wq", "Wk", "Wv", "bq", "bk", "bv", "dw_w", "dw_b", "sin", "cos")}, s, ident, taps, conv_bias)
        layer0_core(nc, a, s, ident, taps, conv_bias)
        x1 = ctx.enter_context(nc.sbuf_tensor("x1", [P, B * TILES, C], F32))
        layer1_attention(nc, a, s, ident, x1)
        layer1_ffn(nc, a, s, ident, x1, out_tiles)


SHORT = {
    "x": "x", "sin": "L0_conv_sin", "cos": "L0_conv_cos", "mask": "L0_conv_mask", "Wq": "L0_conv_Wq",
    "bq": "L0_conv_bq", "Wk": "L0_conv_Wk", "bk": "L0_conv_bk", "Wv": "L0_conv_Wv", "bv": "L0_conv_bv",
    "dw_w": "L0_conv_dw_w", "dw_b": "L0_conv_dw_b", "Wo0": "L0_conv_Wo", "bo0": "L0_conv_bo",
    "Wq1": "L1_attn_Wq", "bq1": "L1_attn_bq", "Wk1": "L1_attn_Wk", "bk1": "L1_attn_bk",
    "Wv1": "L1_attn_Wv", "bv1": "L1_attn_bv", "Wr": "L1_ffn_Wr", "br": "L1_ffn_br", "W1": "L1_ffn_W1",
    "b1": "L1_ffn_b1", "W2": "L1_ffn_W2", "b2": "L1_ffn_b2", "gamma": "L1_ffn_gamma", "beta": "L1_ffn_beta",
}


def kernel(**inputs):
    import concourse.bacc as bacc
    from concourse.bass_utils import run_bass_kernel_spmd

    nc = bacc.Bacc("TRN2", target_bir_lowering=False, num_devices=1)
    arrays, a = {}, {}
    for short, name in SHORT.items():
        x = np.ascontiguousarray(inputs[name])
        arrays[f"in_{short}"] = x
        a[short] = nc.dram_tensor(f"in_{short}", x.shape, mybir.dt.from_np(x.dtype), kind="ExternalInput").ap()
    out = nc.dram_tensor("out", (B, H, W, C), F32, kind="ExternalOutput").ap()
    hybrid(nc, a, out)
    return run_bass_kernel_spmd(nc, [arrays], core_ids=[0]).results[0]["out"]
```

```python
from contextlib import ExitStack

import numpy as np
import concourse.bass as bass
from concourse import mybir

F32 = mybir.dt.float32
BF16 = mybir.dt.bfloat16
ALU = mybir.AluOpType
ACT = mybir.ActivationFunctionType
AX = mybir.AxisListType

P = 128
B, H, W, C = 4, 48, 48, 128
N = H * W
HEADS = 8
D = C // HEADS
TILES = N // P
HT = TILES // 2
GB = 3
GW = GB * P
NG = TILES // GB
CH = 2 * GW
NCH = N // CH
BANK = 512
GROUP = 4
PAD = 2
WP = W + 2 * PAD
TAPS = 25
HALF_H = H // 2
HALF_OUT = HALF_H * WP
PIECES = TILES // 2
PIECE = -(-HALF_OUT // PIECES)
HALF_IN = PIECE * PIECES + (TAPS // 5 - 1) * (WP + 1)
IMAGE_IN = HALF_OUT + HALF_IN
Q_SLOTS = [0, 0, 0, 1, 1, 2]
K_SLOTS = [0, 1, 2, 0, 1, 0]
KR = len(Q_SLOTS) * D
E = 8
FF = 256
FH = FF // P
TOPK = 2
CAPACITY = float(-(-B * N * 1.25 // E))
LOWEST = -3.0e38


def sem_maker(nc, ctx, prefix):
    return lambda name: ctx.enter_context(nc.semaphore(f"{prefix}_{name}"))


def buffers(nc, ctx, prefix):
    def sb(name, shape, dt=F32):
        return ctx.enter_context(nc.sbuf_tensor(f"{prefix}_{name}", shape, dt))

    def ps(name, shape):
        return ctx.enter_context(nc.psum_tensor(f"{prefix}_{name}", shape, F32))

    return sb, ps


def alone(engine):
    engine.nop(nofuse=True)


def cols(b, g):
    return slice(g * b, (g + 1) * b)


def tiles_of(g):
    return range(g * GB, (g + 1) * GB)


def layer0_front(nc, a, s, ident, taps, conv_bias):
    with ExitStack() as ctx:
        sb, ps = buffers(nc, ctx, "f")
        sem = sem_maker(nc, ctx, "f")
        X = sb("X", [P, TILES, C])
        XT = sb("XT", [P, N])
        XN = sb("XN", [P, N])
        cosT = sb("cosT", [P, N])
        sinT = sb("sinT", [P, N])
        angles = sb("angles", [P, 2, TILES, D])
        angles8 = sb("angles8", [P, TILES, HEADS, D])
        rot_sum = sb("rot_sum", [P, 2, N])
        parts = sb("parts", [P, 2, 3, N], BF16)
        t1 = sb("t1", [P, 2, GW])
        t2 = sb("t2", [P, 2, GW])
        V = sb("V", [P, HEADS, TILES, D])
        vpad = sb("vpad", [P, IMAGE_IN])
        weights = sb("weights", [P, 5, C])
        rows = sb("rows", [1, 6, C])
        biases = sb("biases", [P, 6])
        bv_all = sb("bv_all", [P, GB, C])
        ones = sb("ones", [1, P])
        eps = sb("eps", [P, 1])
        average = sb("average", [P, P])
        taps_row = sb("taps_row", [TAPS, C])
        stats = sb("stats", [P, NG, 6])
        mv = sb("mv", [P, 2])
        moments = sb("moments", [P, 2])
        group = sb("group", [P, 2])
        var = sb("var", [P, 1])
        sd = sb("sd", [P, 1])
        rstd = sb("rstd", [P, 1])

        tr = ps("tr", [P, 2, BANK])
        mm = ps("mm", [P, 4, BANK])
        vps = ps("vps", [P, BANK])
        misc = ps("misc", [P, BANK])

        weights_in = sem("weights_in")
        angles_in = sem("angles_in")
        x_in = sem("x_in")
        constants = sem("constants")
        prep = sem("prep")
        scaled_k = sem("scaled_k")
        rotated_w = sem("rotated_w")
        angles_wide = sem("angles_wide")
        small_ready = sem("small_ready")
        small_taken = sem("small_taken")
        tr_ready = sem("tr_ready")
        tr_taken = sem("tr_taken")
        stats_ready = sem("stats_ready")
        norm_step = sem("norm_step")
        group_ready = sem("group_ready")
        var_ready = sem("var_ready")
        sd_ready = sem("sd_ready")
        xn_ready = sem("xn_ready")
        mm_ready = sem("mm_ready")
        mm_taken = sem("mm_taken")
        rot_ready = sem("rot_ready")
        p1_ready = sem("p1_ready")
        d1_ready = sem("d1_ready")
        p2_ready = sem("p2_ready")
        p3_ready = sem("p3_ready")
        q_stored = sem("q_stored")
        k_stored = sem("k_stored")
        v_stored = sem("v_stored")
        vpad_stored = sem("vpad_stored")
        vps_ready = sem("vps_ready")
        vps_taken = sem("vps_taken")

        TR_USES = 2 * NG
        TR_FIRST = 3 * NG
        MM_USES = 4 * NG

        block = ctx.enter_context(nc.Block())

        def remainders(engine, b, m):
            engine.wait_ge(p1_ready, 2 * b + m + 1)
            alone(engine)
            engine.tensor_tensor(rot_sum[:, m, :], rot_sum[:, m, :], parts[:, m, 0, :], ALU.subtract).then_inc(d1_ready, 1)
            engine.wait_ge(p2_ready, 2 * b + m + 1)
            alone(engine)
            engine.tensor_tensor(parts[:, m, 2, :], rot_sum[:, m, :], parts[:, m, 1, :], ALU.subtract).then_inc(p3_ready, 1)

        @block.sync
        def _(sp):
            def load_x(b):
                for half in range(2):
                    sp.dma_start(X[:, cols(HT, half), :], s["x_tiles"][b][:, cols(HT, half), :]).then_inc(x_in, 16)

            load_x(0)
            sp.dma_start(angles[:, 0, :, :], a["cos"].rearrange("h w d -> (h w) d").rearrange("(t p) d -> p t d", p=P)).then_inc(angles_in, 16)
            sp.dma_start(angles[:, 1, :, :], a["sin"].rearrange("h w d -> (h w) d").rearrange("(t p) d -> p t d", p=P)).then_inc(angles_in, 16)
            for i, w in enumerate((a["Wq"], None, a["Wk"], None, a["Wv"])):
                if w is not None:
                    sp.dma_start(weights[:, i, :], w).then_inc(weights_in, 16)
            for i, v in enumerate((a["bq"], None, a["bk"], None, a["bv"], a["dw_b"])):
                if v is not None:
                    sp.dma_start(rows[:, i, :], v.rearrange("(a n) -> a n", a=1)).then_inc(weights_in, 16)
            sp.dma_start(taps_row[:, :], a["dw_w"].rearrange("a b o c -> (a b o) c")).then_inc(weights_in, 16)

            def store_v(b):
                sp.wait_ge(vps_taken, NG * (b + 1) + 1)
                sp.dma_start(s["v_store"][b], V[:, :, :, :].rearrange("p h t d -> p h (t d)")).then_inc(v_stored, 16)

            def store(b):
                sp.wait_ge(tr_taken, TR_FIRST + TR_USES * b + NG + 2)
                sp.dma_start(s["vpad_store"][b], vpad[:, :]).then_inc(vpad_stored, 16)
                sp.wait_ge(p3_ready, 2 * b + 1 + 2)
                for slot, part in enumerate(Q_SLOTS):
                    sp.dma_start(s["q_store"][b, slot], parts[:, 0, part, :]).then_inc(q_stored, 16)
                sp.wait_ge(p3_ready, 2 * b + 2 + 2)
                for part in range(3):
                    sp.dma_start(s["k_store"][b, part], parts[:, 1, part, :]).then_inc(k_stored, 16)

            sp.wait_ge(tr_ready, NG)
            load_x(1)
            with sp.Fori(0, B - 2) as b:
                store_v(b)
                sp.wait_ge(tr_ready, TR_FIRST + TR_USES * (b + 1))
                load_x(b + 2)
                store(b)
            for b in (B - 2, B - 1):
                store_v(b)
                store(b)
            sp.wait_ge(q_stored, 16 * len(Q_SLOTS) * (B + 1))
            sp.wait_ge(k_stored, 16 * 3 * (B + 1))
            sp.wait_ge(v_stored, 16 * (B + 1))
            sp.wait_ge(vpad_stored, 16 * (B + 1))

        @block.gpsimd
        def _(pool):
            pool.memset(average[:, :], 1.0 / GROUP).then_inc(prep, 1)
            pool.memset(ident[:, :], 0.0).then_inc(prep, 1)
            pool.memset(vpad[:, :], 0.0).then_inc(constants, 1)
            pool.memset(ones[:, :], 1.0).then_inc(constants, 1)
            pool.memset(eps[:, :], 1e-5).then_inc(constants, 1)
            pool.wait_ge(prep, 2)
            pool.affine_select(out=ident[:, :], in_=ident[:, :], compare_op=ALU.not_equal, fill=1.0,
                               base=0, pattern=[[-1, P]], channel_multiplier=1).then_inc(constants, 1)
            av = average[:, :].rearrange("p (g k) -> p g k", k=GROUP)
            pool.affine_select(out=av, in_=av, compare_op=ALU.is_ge, fill=0.0, base=0,
                               pattern=[[-GROUP, P // GROUP], [0, GROUP]], channel_multiplier=1).then_inc(prep, 1)
            pool.wait_ge(prep, 3)
            pool.affine_select(out=av, in_=av, compare_op=ALU.is_ge, fill=0.0, base=GROUP - 1,
                               pattern=[[GROUP, P // GROUP], [0, GROUP]], channel_multiplier=-1).then_inc(constants, 1)
            with pool.Fori(0, B - 1) as b:
                for m in range(2):
                    remainders(pool, b, m)
            remainders(pool, B - 1, 0)

        @block.scalar
        def _(act):
            def take_x(b, n):
                for g in range(NG):
                    act.wait_ge(tr_ready, n + g + 1)
                    act.activation(XT[:, cols(GW, g)], tr[:, g % 2, 0:GW], ACT.Copy).then_inc(tr_taken, 1)

            def deviation(b):
                act.wait_ge(var_ready, b + 1)
                act.activation(sd[:, :], var[:, :], ACT.Sqrt, bias=eps[:, :]).then_inc(sd_ready, 1)

            def take_v_image(b):
                act.wait_ge(vpad_stored, 16 * (b + 1))
                for g in range(NG):
                    act.wait_ge(tr_ready, TR_FIRST + TR_USES * b + g + 1)
                    rows_of = GW // W
                    image = vpad[:, 0:(H + 2 * PAD) * WP].rearrange("p (h w) -> p h w", w=WP)
                    dst = image[:, PAD + g * rows_of:PAD + (g + 1) * rows_of, PAD:PAD + W]
                    src = tr[:, g % 2, 0:GW].rearrange("p (h w) -> p h w", w=W)
                    act.activation(dst, src, ACT.Identity, bias=biases[:, 4:5]).then_inc(tr_taken, 1)

            def first_part(b, m):
                act.wait_ge((q_stored, k_stored)[m], 16 * (len(Q_SLOTS), 3)[m] * (b + 1))
                act.wait_ge(rot_ready, 2 * b + m + 1)
                act.activation(parts[:, m, 0, :], rot_sum[:, m, :], ACT.Copy).then_inc(p1_ready, 1)

            def second_part(b, m):
                act.wait_ge(d1_ready, 2 * b + m + 1)
                act.activation(parts[:, m, 1, :], rot_sum[:, m, :], ACT.Copy).then_inc(p2_ready, 1)

            act.sem_inc(q_stored, 16 * len(Q_SLOTS))
            act.sem_inc(k_stored, 16 * 3)
            act.sem_inc(vpad_stored, 16)
            act.sem_inc(tr_taken, 2)
            take_x(0, 0)
            for m in range(2):
                for g in range(NG):
                    if m == 1 and g == 0:
                        deviation(0)
                    act.wait_ge(tr_ready, NG * (m + 1) + g + 1)
                    act.activation((cosT, sinT)[m][:, cols(GW, g)], tr[:, g % 2, 0:GW], ACT.Copy).then_inc(tr_taken, 1)
            with act.Fori(0, B - 1) as b:
                take_v_image(b)
                take_x(b + 1, TR_FIRST + TR_USES * b + NG)
                first_part(b, 0)
                deviation(b + 1)
                second_part(b, 0)
                first_part(b, 1)
                second_part(b, 1)
            take_v_image(B - 1)
            for m in range(2):
                first_part(B - 1, m)
                second_part(B - 1, m)

        @block.tensor
        def _(pe):
            def transpose_x(b, n):
                pe.wait_ge(x_in, 32 * (b + 1))
                for g in range(NG):
                    pe.wait_ge(tr_taken, n + g + 1)
                    for k in range(GB):
                        last = pe.transpose(tr[:, g % 2, cols(P, k)], X[:, g * GB + k, :], ident[:, :])
                    last.then_inc(tr_ready, 1)

            def transpose_angles(m):
                pe.wait_ge(angles_wide, m + 1)
                for g in range(NG):
                    pe.wait_ge(tr_taken, NG * (m + 1) + g + 1)
                    for k in range(GB):
                        t = g * GB + k
                        last = pe.transpose(tr[:, g % 2, cols(P, k)],
                                            angles8[:, t, :, :].rearrange("p h d -> p (h d)"), ident[:, :])
                    last.then_inc(tr_ready, 1)

            def group_means(b):
                pe.wait_ge(stats_ready, b + 1)
                pe.matmul(misc[:, 0:2], average[:, :], moments[:, :], start=True, stop=True).then_inc(group_ready, 1)

            def v_tokens(b):
                pe.wait_ge(xn_ready, b + 1)
                for g in range(NG):
                    pe.wait_ge(vps_taken, NG * b + g + 1)
                    for k in range(GB):
                        last = pe.matmul(vps[:, cols(P, k)], XN[:, cols(P, g * GB + k)], weights[:, 4, :],
                                         start=True, stop=True)
                    last.then_inc(vps_ready, 1)

            def v_image(b):
                for g in range(NG):
                    pe.wait_ge(tr_taken, TR_FIRST + TR_USES * b + g + 1)
                    pe.matmul(tr[:, g % 2, 0:GW], weights[:, 4, :], XN[:, cols(GW, g)],
                              start=True, stop=True).then_inc(tr_ready, 1)

            def project(b, m, groups):
                for g in groups:
                    for r in range(2):
                        n = (m * NG + g) * 2 + r
                        pe.wait_ge(mm_taken, MM_USES * b + n + 1)
                        pe.matmul(mm[:, n % 4, 0:GW], weights[:, 2 * m + r, :], XN[:, cols(GW, g)],
                                  start=True, stop=True).then_inc(mm_ready, 1)

            pe.wait_ge(constants, 5)
            transpose_x(0, 0)
            transpose_angles(0)
            group_means(0)
            transpose_angles(1)
            pe.wait_ge(rotated_w, 1)
            for i in range(6):
                pe.matmul(misc[:, 2 + i:3 + i], rows[0:1, i, :], ones[0:1, 0:1], start=True, stop=True)
            pe.matmul(misc[:, P:2 * P], ones[0:1, :], rows[0:1, 4, :], start=True, stop=True)
            pe.transpose(misc[:, 2 * P:2 * P + TAPS], taps_row[:, :], ident[0:TAPS, 0:TAPS]).then_inc(small_ready, 1)
            pe.wait_ge(small_taken, 3)
            with pe.Fori(0, B - 1) as b:
                v_tokens(b)
                project(b, 0, range(NG))
                v_image(b)
                transpose_x(b + 1, TR_FIRST + TR_USES * b + NG)
                project(b, 1, range(2))
                group_means(b + 1)
                project(b, 1, range(2, NG))
            v_tokens(B - 1)
            project(B - 1, 0, range(NG))
            v_image(B - 1)
            project(B - 1, 1, range(NG))

        @block.vector
        def _(dve):
            NS = 6

            def widen(m):
                for h in range(HEADS):
                    last = dve.tensor_copy(angles8[:, :, h, :], angles[:, m, :, :])
                last.then_inc(angles_wide, 1)

            def statistics(b, n):
                for g in range(NG):
                    dve.wait_ge(tr_taken, n + g + 1 + 2)
                    last = dve.bn_stats(stats[:, g, :], XT[:, cols(GW, g)])
                last.then_inc(norm_step, 1)
                dve.wait_ge(norm_step, NS * b + 1)
                alone(dve)
                dve.bn_aggr(mv[:, :], stats[:, :, :]).then_inc(norm_step, 1)
                dve.wait_ge(norm_step, NS * b + 2)
                dve.tensor_copy(moments[:, 0:1], mv[:, 0:1])
                dve.scalar_tensor_tensor(out=moments[:, 1:2], in0=mv[:, 0:1], scalar=mv[:, 0:1], in1=mv[:, 1:2],
                                         op0=ALU.mult, op1=ALU.add).then_inc(stats_ready, 1)

            def variance(b):
                dve.wait_ge(group_ready, b + 1)
                dve.tensor_copy(group[:, :], misc[:, 0:2]).then_inc(norm_step, 1)
                dve.wait_ge(norm_step, NS * b + 3)
                dve.tensor_tensor(var[:, :], group[:, 0:1], group[:, 0:1], ALU.mult).then_inc(norm_step, 1)
                dve.wait_ge(norm_step, NS * b + 4)
                dve.tensor_tensor(var[:, :], group[:, 1:2], var[:, :], ALU.subtract).then_inc(norm_step, 1)
                dve.wait_ge(norm_step, NS * b + 5)
                dve.tensor_scalar(var[:, :], var[:, :], 0.0, None, ALU.max).then_inc(var_ready, 1)

            def normalise(b, used=None):
                dve.wait_ge(sd_ready, b + 1)
                dve.reciprocal(rstd[:, :], sd[:, :]).then_inc(norm_step, 1)
                dve.wait_ge(norm_step, NS * b + 6)
                if used is not None:
                    dve.wait_ge(mm_ready, used)
                dve.tensor_scalar(XN[:, :], XT[:, :], group[:, 0:1], rstd[:, :], ALU.subtract, ALU.mult).then_inc(xn_ready, 1)

            def take_v(b):
                dve.wait_ge(v_stored, 16 * (b + 1))
                for g in range(NG):
                    dve.wait_ge(vps_ready, NG * b + g + 1)
                    dst = V[:, :, cols(GB, g), :].rearrange("p h t d -> p t h d")
                    src = vps[:, 0:GW].rearrange("p (t h d) -> p t h d", t=GB, h=HEADS)
                    bias = bv_all[:, :, :].rearrange("p t (h d) -> p t h d", h=HEADS)
                    dve.tensor_tensor(dst, src, bias, ALU.add).then_inc(vps_taken, 1)

            def rotate(b, m, groups):
                if 0 in groups:
                    dve.wait_ge(p3_ready, 2 * b + m + 1)
                for g in groups:
                    n = (m * NG + g) * 2
                    dve.wait_ge(mm_ready, MM_USES * b + n + 2)
                    dve.scalar_tensor_tensor(out=t1[:, g % 2, :], in0=mm[:, n % 4, 0:GW], scalar=biases[:, 2 * m:2 * m + 1],
                                             in1=cosT[:, cols(GW, g)], op0=ALU.add, op1=ALU.mult).then_inc(mm_taken, 1)
                    dve.scalar_tensor_tensor(out=t2[:, g % 2, :], in0=mm[:, (n + 1) % 4, 0:GW], scalar=biases[:, 2 * m + 1:2 * m + 2],
                                             in1=sinT[:, cols(GW, g)], op0=ALU.add, op1=ALU.mult).then_inc(mm_taken, 1)
                    dve.wait_ge(mm_taken, MM_USES * b + n + 2 + 4)
                    last = dve.tensor_tensor(rot_sum[:, m, cols(GW, g)], t1[:, g % 2, :], t2[:, g % 2, :], ALU.add)
                if NG - 1 in groups:
                    last.then_inc(rot_ready, 1)

            dve.sem_inc(mm_taken, 4)
            dve.sem_inc(vps_taken, 1)
            dve.sem_inc(p3_ready, 2)
            dve.sem_inc(v_stored, 16)
            dve.wait_ge(angles_in, 32)
            widen(0)
            statistics(0, 0)
            dve.wait_ge(tr_ready, 2 * NG)
            widen(1)
            variance(0)
            dve.wait_ge(weights_in, 16 * 8)
            dve.tensor_scalar(weights[:, 2, :], weights[:, 2, :], D ** -0.5, None, ALU.mult).then_inc(scaled_k, 1)
            dve.tensor_scalar(rows[:, 2, :], rows[:, 2, :], D ** -0.5, None, ALU.mult).then_inc(scaled_k, 1)
            dve.wait_ge(scaled_k, 2)
            for of in (weights, rows):
                for src_i in (0, 2):
                    src = of[:, src_i, :].rearrange("p (i two) -> p i two", two=2)
                    dst = of[:, src_i + 1, :].rearrange("p (i two) -> p i two", two=2)
                    dve.tensor_scalar(dst[:, :, 0], src[:, :, 1], -1.0, None, ALU.mult)
                    last = dve.tensor_copy(dst[:, :, 1], src[:, :, 0])
            last.then_inc(rotated_w, 1)
            normalise(0)
            dve.wait_ge(small_ready, 1)
            dve.tensor_copy(conv_bias[:, :], misc[:, 7:8])
            dve.tensor_copy(biases[:, :], misc[:, 2:8]).then_inc(small_taken, 1)
            for k in range(GB):
                last = dve.tensor_copy(bv_all[:, k, :], misc[:, P:2 * P])
            last.then_inc(small_taken, 1)
            dve.tensor_copy(taps[:, :], misc[:, 2 * P:2 * P + TAPS]).then_inc(small_taken, 1)
            dve.wait_ge(small_taken, 3)
            dve.wait_ge(tr_taken, TR_FIRST + 2)
            with dve.Fori(0, B - 1) as b:
                take_v(b)
                rotate(b, 0, range(NG))
                statistics(b + 1, TR_FIRST + TR_USES * b + NG)
                rotate(b, 1, range(2))
                variance(b + 1)
                rotate(b, 1, range(2, NG))
                normalise(b + 1, MM_USES * (b + 1))
            take_v(B - 1)
            rotate(B - 1, 0, range(NG))
            rotate(B - 1, 1, range(NG))
            dve.wait_ge(p3_ready, 2 * (B - 1) + 1 + 2)
            remainders(dve, B - 1, 1)


def layer0_core(nc, a, s, ident, taps, conv_bias):
    with ExitStack() as ctx:
        sb, ps = buffers(nc, ctx, "c")
        sem = sem_maker(nc, ctx, "c")
        K = sb("K", [KR, 2 * B * N], BF16)
        Q = sb("Q", [KR, 2, B, P], BF16)
        mask = sb("mask", [P, 2, N])
        S = sb("S", [P, B, N])
        part_max = sb("part_max", [P, B, NCH])
        row_max = sb("row_max", [P, B])
        PT = sb("PT", [P, 2, TILES, P])
        V_next = sb("V_next", [P, B * TILES, D])
        V = sb("V", [P, B * TILES, 2 * D])
        O = sb("O", [P, 2, B, P])

        vpad = sb("vpad", [P, 2 * HALF_IN])
        conv = sb("conv", [P, 2 * PIECE * PIECES])

        Sps = ps("Sps", [P, 2, 2, BANK])
        Tps = ps("Tps", [P, 3, BANK])
        Ops = ps("Ops", [P, B, P])

        k_in, v_in, tile_in = sem("k_in"), sem("v_in"), sem("tile_in")
        v_ones, v_placed = sem("v_ones"), sem("v_placed")
        s_ready, s_taken = sem("s_ready"), sem("s_taken")
        max_ready, shifted = sem("max_ready"), sem("shifted")
        t_ready, exp_done, pt_used = sem("t_ready"), sem("exp_done"), sem("pt_used")
        o_taken, o_stored = sem("o_taken"), sem("o_stored")
        vpad_in, conv_step, conv_stored = sem("vpad_in"), sem("conv_step"), sem("conv_stored")

        ITERS = HEADS * TILES
        PAIRS = TILES // 2
        IC, IG = B * NCH, B * NG
        COLS = 4
        STORES = COLS + 1
        S_SLOTS, T_SLOTS, PT_SLOTS, O_SLOTS = 2, 3, 2, 1

        block = ctx.enter_context(nc.Block())

        @block.sync
        def _(sp):
            def load_head(h):
                k = K[:, bass.ds((h % 2) * (B * N), B * N)]
                sp.dma_start(k[0:3 * D, :], s["k_load"][h]).then_inc(k_in, 16)
                sp.dma_start(k[3 * D:5 * D, :], s["k_load"][h][0:2 * D, :]).then_inc(k_in, 16)
                sp.dma_start(k[5 * D:6 * D, :], s["k_load"][h][0:D, :]).then_inc(k_in, 16)
                sp.dma_start(V_next[:, :, :].rearrange("p t d -> p (t d)"), s["v_load"][h]).then_inc(v_in, 16)

            def load_half(h):
                sp.dma_start(vpad[:, bass.ds((h % 2) * HALF_IN, HALF_IN)],
                             s["vpad_load"][h // 2][:, bass.ds((h % 2) * HALF_OUT, HALF_IN)]).then_inc(vpad_in, 16)

            def store_half(h):
                sp.wait_ge(conv_step, TAPS * PIECES * (h + 1))
                alone(sp)
                rows = conv[:, bass.ds((h % 2) * PIECE * PIECES, HALF_OUT)].rearrange("p (h w) -> p h w", w=WP)
                sp.dma_start(s["conv_store"][h // 2][h % 2], rows[:, :, 0:W]).then_inc(conv_stored, 16)

            def load_tile(it):
                slot = it % 2
                sp.dma_start(mask[:, bass.ds(slot, 1), :].rearrange("p a n -> p (a n)"),
                             s["mask"][it]).then_inc(tile_in, 16)
                sp.dma_start(Q[:, bass.ds(slot, 1), :, :].rearrange("r a b q -> r (a b) q"),
                             s["q_load"][it // TILES][:, :, bass.ds((it % TILES) * P, P)]).then_inc(tile_in, 16)

            def store_tile(it):
                o = O[:, bass.ds(it % 2, 1), :, :].rearrange("p a b q -> p (a b) q")
                sp.wait_ge(o_stored, 16 * STORES * (it + 2))
                sp.wait_ge(o_taken, it + 1 + O_SLOTS)
                h, qt = it // TILES, it % TILES
                for j in range(COLS):
                    sp.dma_start(s["o_store"][j][h][:, :, bass.ds(qt * P, P)], o[32 * j:32 * j + D]).then_inc(o_stored, 16)
                sp.dma_start(s["den_store"][h][:, :, bass.ds(qt * P, P)], o[D:P:32]).then_inc(o_stored, 16)

            def step(it):
                sp.wait_ge(tile_in, 32 * (it + 2))
                sp.wait_ge(s_taken, IC * (it + 1) + S_SLOTS)
                load_tile(it + 2)
                store_tile(it)

            load_head(0)
            load_half(0)
            load_tile(0)
            sp.wait_ge(tile_in, 32)
            load_tile(1)
            with sp.Fori(0, HEADS - 1) as h:
                step(h * TILES)
                sp.wait_ge(k_in, 48 * (h + 1))
                sp.wait_ge(v_placed, h + 1)
                load_head(h + 1)
                sp.wait_ge(conv_step, TAPS * PIECES * h + 1)
                alone(sp)
                sp.wait_ge(vpad_in, 16 * (h + 1))
                alone(sp)
                load_half(h + 1)
                with sp.Fori(1, TILES) as qt:
                    step(h * TILES + qt)
                store_half(h)
            with sp.Fori(ITERS - TILES, ITERS - 2) as it:
                step(it)
            store_half(HEADS - 1)
            store_tile(ITERS - 2)
            store_tile(ITERS - 1)
            sp.wait_ge(conv_stored, 16 * (HEADS + 2))
            sp.wait_ge(o_stored, 16 * STORES * (ITERS + 2))

        @block.gpsimd
        def _(pool):
            pool.memset(V[:, :, :], 1.0).then_inc(v_ones, 1)
            with pool.Fori(0, ITERS) as it:
                for b in range(B):
                    pool.wait_ge(max_ready, B * it + b + 1)
                    alone(pool)
                    pool.tensor_scalar(S[:, b, :], S[:, b, :], -1.0, row_max[:, b:b + 1],
                                       ALU.mult, ALU.add).then_inc(shifted, 1)

        @block.scalar
        def _(act):
            act.sem_inc(exp_done, T_SLOTS)
            act.sem_inc(o_stored, 2 * 16 * STORES)

            def place_v(h):
                act.wait_ge(v_in, 16 * (h + 1))
                act.activation(V[:, :, 0:D], V_next[:, :, :], ACT.Copy).then_inc(v_placed, 1)

            def exp(it, b, g):
                m = IG * it + NG * b + g
                act.wait_ge(t_ready, m + 1 + IG)
                act.activation(PT[:, b % 2, cols(GB, g), :], Tps[:, g % T_SLOTS, 0:GW].rearrange("p (t q) -> p t q", t=GB),
                               ACT.Exp, scale=-1.0).then_inc(exp_done, 1)

            def first_groups(it):
                act.wait_ge(pt_used, B * it + 1)
                exp(it, 0, 0)
                exp(it, 0, 1)

            def rest(it):
                for b in range(B):
                    if b:
                        act.wait_ge(pt_used, B * it + b + 1)
                    for g in range(2 if b == 0 else 0, NG):
                        exp(it, b, g)

            def take_o(it, slot):
                act.wait_ge(pt_used, B * (it + 1) + PT_SLOTS)
                act.wait_ge(o_stored, 16 * STORES * (it + 1))
                act.activation(O[:, slot, :, :], Ops[:, :, :], ACT.Copy).then_inc(o_taken, 1)

            def pair(it, last=None):
                for t in range(2):
                    rest(it + t)
                    if not (t and last == "end"):
                        first_groups(it + t + 1)
                    take_o(it + t, t)

            act.wait_ge(v_ones, 1)
            place_v(0)
            first_groups(0)
            with act.Fori(0, HEADS - 1) as h:
                with act.Fori(0, PAIRS) as qp:
                    pair(h * TILES + 2 * qp)
                place_v(h + 1)
            with act.Fori(0, PAIRS - 1) as qp:
                pair((HEADS - 1) * TILES + 2 * qp)
            pair(ITERS - 2, "end")

        @block.vector
        def _(dve):
            dve.sem_inc(s_taken, S_SLOTS)
            dve.sem_inc(conv_stored, 2 * 16)
            with dve.Fori(0, ITERS // 2) as ip:
                h, piece = ip // PIECES, ip % PIECES

                def conv_tap(tap):
                    if tap == 0:
                        dve.wait_ge(vpad_in, 16 * (h + 1))
                        dve.wait_ge(conv_stored, 16 * (h + 1))
                    else:
                        dve.wait_ge(conv_step, TAPS * ip + tap)
                    dy, dx = divmod(tap, 5)
                    window = vpad[:, bass.ds((h % 2) * HALF_IN + piece * PIECE + (dy * WP + dx), PIECE)]
                    dst = conv[:, bass.ds((h % 2) * (PIECE * PIECES) + piece * PIECE, PIECE)]
                    if tap == 0:
                        dve.tensor_scalar(dst, window, taps[:, 0:1], conv_bias[:, :], ALU.mult, ALU.add).then_inc(conv_step, 1)
                    else:
                        dve.scalar_tensor_tensor(out=dst, in0=window, scalar=taps[:, tap:tap + 1], in1=dst,
                                                 op0=ALU.mult, op1=ALU.add).then_inc(conv_step, 1)

                for t in range(2):
                    it = ip * 2 + t
                    for b in range(B):
                        for c in range(NCH):
                            n = B * NCH * t + b * NCH + c
                            if b == 0 and c == 0:
                                dve.wait_ge(tile_in, 32 * (it + 1))
                            if c == 0:
                                dve.wait_ge(t_ready, IG * it + NG * (b + 1))
                            dve.wait_ge(s_ready, 2 * IC * ip + n + 1)
                            alone(dve)
                            dve.tensor_tensor_reduce(
                                out=S[:, b, cols(CH, c)].rearrange("p (k n) -> p k n", k=2),
                                in0=Sps[:, n % S_SLOTS, :, 0:GW],
                                in1=mask[:, t, cols(CH, c)].rearrange("p (k n) -> p k n", k=2),
                                scale=1.0, scalar=LOWEST, op0=ALU.add, op1=ALU.max,
                                accum_out=part_max[:, b, c:c + 1]).then_inc(s_taken, 1)
                            if c < NCH - 1:
                                conv_tap(n)
                        dve.wait_ge(s_taken, 2 * IC * ip + n + 1 + S_SLOTS)
                        dve.tensor_reduce(row_max[:, b:b + 1], part_max[:, b, :], AX.X, ALU.max).then_inc(max_ready, 1)
                        conv_tap(n)
                conv_tap(TAPS - 1)

        @block.tensor
        def _(pe):
            pe.sem_inc(t_ready, IG)
            pe.sem_inc(pt_used, PT_SLOTS)
            pe.sem_inc(o_taken, O_SLOTS)

            def scores(it, t, b, c):
                if b == 0 and c == 0:
                    pe.wait_ge(tile_in, 32 * (it + 1))
                    pe.wait_ge(k_in, 48 * (it // TILES + 1))
                n = IC * t + NCH * b + c
                pe.wait_ge(s_taken, IC * it + NCH * b + c + 1)
                for k in range(2):
                    start = ((it // TILES) % 2) * (B * N) + (b * N + c * CH + k * GW)
                    last = pe.matmul(Sps[:, n % S_SLOTS, k, 0:GW], Q[:, t, b, :], K[:, bass.ds(start, GW)],
                                     start=True, stop=True)
                last.then_inc(s_ready, 1)

            def transposes(it, b, g):
                m = IG * it + NG * b + g
                if g == 0:
                    pe.wait_ge(shifted, B * it + b + 1)
                pe.wait_ge(exp_done, m + 1)
                for k in range(GB):
                    last = pe.transpose(Tps[:, g % T_SLOTS, cols(P, k)], S[:, b, cols(P, g * GB + k)], ident[:, :])
                last.then_inc(t_ready, 1)

            def values(it, b, c):
                if b == 0 and c == 0:
                    pe.wait_ge(o_taken, it + 1)
                    pe.wait_ge(v_placed, it // TILES + 1)
                pe.wait_ge(exp_done, IG * it + NG * b + 2 * (c + 1) + T_SLOTS)
                for kt in range(2 * GB * c, 2 * GB * (c + 1)):
                    j = kt % COLS
                    last = pe.matmul(Ops[32 * j:32 * (j + 1), b, :], V[:, b * TILES + kt, :], PT[:, b % 2, kt, :],
                                     start=kt < COLS, stop=kt >= TILES - COLS)
                if c == NCH - 1:
                    last.then_inc(pt_used, 1)

            def iteration(it, t, start=False, end=False):
                for b in range(B):
                    for c in range(NCH):
                        if b + 2 < B:
                            scores(it, t, b + 2, c)
                        elif not end:
                            scores(it + 1, 1 - t, b + 2 - B, c)
                        transposes(it, b, 2 * c)
                        transposes(it, b, 2 * c + 1)
                        if c:
                            values(it, b, c - 1)
                        elif b:
                            values(it, b - 1, NCH - 1)
                        elif not start:
                            values(it - 1, B - 1, NCH - 1)

            for b in range(2):
                for c in range(NCH):
                    scores(0, 0, b, c)
            iteration(0, 0, start=True)
            iteration(1, 1)
            with pe.Fori(1, ITERS // 2 - 1) as ip:
                iteration(ip * 2, 0)
                iteration(ip * 2 + 1, 1)
            iteration(ITERS - 2, 0)
            iteration(ITERS - 1, 1, end=True)
            values(ITERS - 1, B - 1, NCH - 1)


def layer1_attention(nc, a, s, ident, x1, moments):
    with ExitStack() as ctx:
        sb, ps = buffers(nc, ctx, "l")
        sem = sem_maker(nc, ctx, "l")
        SEG = N // D
        HN = N // 2
        num = sb("num", [P, 4, HN])
        den = sb("den", [P, 4, SEG])
        den_sum = sb("den_sum", [P, SEG])
        z = sb("z", [P, N])
        conv = sb("conv", [P, N])
        xin = sb("xin", [P, TILES, C])
        ln = sb("ln", [P, TILES, C])
        lnT = sb("lnT", [P, N])
        qT = sb("qT", [P, 2 * N])
        kT = sb("kT", [P, 2 * N])
        v = sb("v", [P, 2 * TILES, C])
        q_tile = sb("q_tile", [P, 2, P])
        S = sb("S", [P, 2, N])
        PT = sb("PT", [P, TILES, P])
        weights = sb("weights", [P, 4, C])
        rows = sb("rows", [1, 4, C])
        biases = sb("biases", [P, 2])
        bo_all = sb("bo_all", [P, GB, C])
        bv_all = sb("bv_all", [P, GB, C])
        ones = sb("ones", [1, P])
        eps = sb("eps", [P, 1])
        stats = sb("stats", [P, TILES, 6])
        mv = sb("mv", [P, TILES, 2])
        sd = sb("sd", [P, TILES])
        rstd = sb("rstd", [P, TILES])
        part_max = sb("part_max", [P, 2, NG])
        neg_max = sb("neg_max", [P, 2])
        total = sb("total", [P, 2])
        inv_total = sb("inv_total", [P, 2])
        row_stats = sb("row_stats", [P, 6])
        row_moments = sb("row_moments", [P, 2])

        Sps = ps("Sps", [P, 3, BANK])
        Tps = ps("Tps", [P, 3, BANK])
        Ops = ps("Ops", [P, 2, BANK])

        weights_in, constants, small_ready, small_taken = sem("weights_in"), sem("constants"), sem("small_ready"), sem("small_taken")
        den_in, half_in, conv_in, x_in = sem("den_in"), sem("half_in"), sem("conv_in"), sem("x_in")
        inv_stored, inv_in = sem("inv_stored"), sem("inv_in")
        den_step, inv_ready, sum_step, half_taken, z_ready = sem("den_step"), sem("inv_ready"), sem("sum_step"), sem("half_taken"), sem("z_ready")
        x_biased = sem("x_biased")
        ln_step, var_ready, sd_ready, ln_ready = sem("ln_step"), sem("var_ready"), sem("sd_ready"), sem("ln_ready")
        t_ready, t_taken, o_ready, o_taken = sem("t_ready"), sem("t_taken"), sem("o_ready"), sem("o_taken")
        q_staged, s_ready, s_taken = sem("q_staged"), sem("s_ready"), sem("s_taken")
        max_ready, p_ready, inv_step, row_step = sem("max_ready"), sem("p_ready"), sem("inv_step"), sem("row_step")

        S_SLOTS = T_SLOTS = 3
        O_SLOTS = 2
        S_USES = NG * TILES
        PROJECT, TRANSPOSE, TO_Q, TO_K, TO_V = 8, 11, 12, 13, 14
        T_PREP, O_PREP = 3 * NG, 2 * NG

        def t_at(b, qt, last=False, after=True):
            prep = 0 if last else sum(qt >= x if after else qt > x for x in (TRANSPOSE, TO_Q, TO_K))
            return T_PREP + (T_PREP + NG * TILES) * b + NG * (qt + prep)

        def o_at(b, qt, last=False, after=True):
            prep = 0 if last else sum(qt >= x if after else qt > x for x in (PROJECT, TO_V))
            return O_PREP + (O_PREP + TILES) * b + qt + NG * prep

        block = ctx.enter_context(nc.Block())

        @block.sync
        def _(sp):
            def load_half(i, half):
                sp.dma_start(num[:, :, :], s["o_load"][i][:, :, half * HN:(half + 1) * HN]).then_inc(half_in, 16)

            def load_x(i):
                for half in range(2):
                    sp.dma_start(xin[:, cols(HT, half), :], s["x_tiles"][i][:, cols(HT, half), :]).then_inc(x_in, 16)

            def spread_inverses(i):
                sp.wait_ge(inv_ready, i + 1)
                alone(sp)
                sp.dma_start(s["inv_store"][i], den_sum[:, :]).then_inc(inv_stored, 16)
                sp.wait_ge(inv_stored, 16 * (i + 1))
                alone(sp)
                sp.dma_start(z[:, :], s["inv_load"][i].unsqueeze(1).to_broadcast([HEADS, D, N])).then_inc(inv_in, 16)

            sp.dma_start(den[:, :, :], s["den_load"][0]).then_inc(den_in, 16)
            load_half(0, 0)
            sp.dma_start(conv[:, :], s["conv"][0]).then_inc(conv_in, 16)
            for i, w in enumerate(("Wo0", "Wq1", "Wk1", "Wv1")):
                sp.dma_start(weights[:, i, :], a[w]).then_inc(weights_in, 16)
            for i, w in enumerate(("bo0", "bq1", "bk1", "bv1")):
                sp.dma_start(rows[:, i, :], a[w].rearrange("(a n) -> a n", a=1)).then_inc(weights_in, 16)
            load_x(0)
            spread_inverses(0)
            sp.wait_ge(half_taken, 1)
            load_half(0, 1)
            with sp.Fori(1, B) as i:
                sp.wait_ge(z_ready, i)
                alone(sp)
                sp.dma_start(den[:, :, :], s["den_load"][i]).then_inc(den_in, 16)
                load_half(i, 0)
                sp.dma_start(conv[:, :], s["conv"][i]).then_inc(conv_in, 16)
                sp.wait_ge(var_ready, i)
                alone(sp)
                load_x(i)
                spread_inverses(i)
                sp.wait_ge(half_taken, 2 * i + 1)
                alone(sp)
                load_half(i, 1)

        @block.gpsimd
        def _(pool):
            pool.memset(ones[:, :], 1.0).then_inc(constants, 1)
            pool.memset(eps[:, :], 1e-5).then_inc(constants, 1)
            pool.wait_ge(small_taken, 3)
            with pool.Fori(0, B) as b:
                pool.wait_ge(x_in, 32 * (b + 1))
                for g in range(NG):
                    last = pool.tensor_tensor(xin[:, cols(GB, g), :], xin[:, cols(GB, g), :], bo_all[:, :, :], ALU.add)
                last.then_inc(x_biased, 1)

        @block.scalar
        def _(act):
            def deviations(i):
                act.wait_ge(var_ready, i + 1)
                act.activation(sd[:, :], mv[:, :, 1:2].rearrange("p t a -> p (t a)"), ACT.Sqrt, bias=eps[:, :]).then_inc(sd_ready, 1)

            def take_transposes(n):
                for g in range(NG):
                    act.wait_ge(t_ready, n + g + 1)
                    act.activation(lnT[:, cols(GW, g)], Tps[:, g % T_SLOTS, 0:GW], ACT.Copy).then_inc(t_taken, 1)

            def take_projection(n, i, m):
                for g in range(NG):
                    act.wait_ge(t_ready, n + g + 1)
                    alone(act)
                    act.activation((qT, kT)[m][:, bass.ds((i % 2) * N + g * GW, GW)], Tps[:, g % T_SLOTS, 0:GW], ACT.Identity,
                                   bias=biases[:, m:m + 1]).then_inc(t_taken, 1)

            def tile(b, qt, t, last=False, prepare=()):
                act.wait_ge(max_ready, TILES * b + qt + 1)
                act.activation(S[:, t, :], S[:, t, :], ACT.Exp, bias=neg_max[:, t:t + 1],
                               accum_out=total[:, t:t + 1]).then_inc(p_ready, 1)
                for step in prepare:
                    step()
                for g in range(NG):
                    if g == 0:
                        act.wait_ge(o_ready, o_at(b, qt, last))
                    act.wait_ge(t_ready, t_at(b, qt, last) + g + 1)
                    act.activation(PT[:, cols(GB, g), :], Tps[:, g % T_SLOTS, 0:GW].rearrange("p (t q) -> p t q", t=GB),
                                   ACT.Copy).then_inc(t_taken, 1)

            act.sem_inc(t_taken, T_SLOTS)
            act.wait_ge(small_taken, 3)
            deviations(0)
            take_transposes(0)
            take_projection(NG, 0, 0)
            take_projection(2 * NG, 0, 1)
            with act.Fori(0, B - 1) as b:
                prepare = {
                    TRANSPOSE - 1: [lambda: deviations(b + 1)],
                    TRANSPOSE: [lambda: take_transposes(t_at(b, TRANSPOSE, after=False))],
                    TO_Q: [lambda: take_projection(t_at(b, TO_Q, after=False), b + 1, 0)],
                    TO_K: [lambda: take_projection(t_at(b, TO_K, after=False), b + 1, 1)],
                }
                for qt in range(TILES):
                    tile(b, qt, qt % 2, prepare=prepare.get(qt, ()))
            with act.Fori(0, TILES // 2) as qp:
                for t in range(2):
                    tile(B - 1, 2 * qp + t, t, last=True)

        @block.tensor
        def _(pe):
            pe.wait_ge(weights_in, 16 * 8)
            pe.wait_ge(constants, 2)
            for i in range(2):
                pe.matmul(Tps[:, 0, i:i + 1], rows[0:1, 1 + i, :], ones[0:1, 0:1], start=True, stop=True)
            pe.matmul(Tps[:, 1, 0:C], ones[0:1, :], rows[0:1, 0, :], start=True, stop=True)
            pe.matmul(Tps[:, 1, C:2 * C], ones[0:1, :], rows[0:1, 3, :], start=True, stop=True).then_inc(small_ready, 1)
            pe.wait_ge(small_taken, 3)

            def project(i, n):
                pe.wait_ge(z_ready, i + 1)
                for g in range(NG):
                    pe.wait_ge(o_taken, n + g + 1)
                    for k in range(GB):
                        last = pe.matmul(Ops[:, g % 2, cols(P, k)], z[:, cols(P, g * GB + k)], weights[:, 0, :],
                                         start=True, stop=True)
                    last.then_inc(o_ready, 1)

            def transpose_ln(i, n):
                pe.wait_ge(ln_ready, i + 1)
                for g in range(NG):
                    pe.wait_ge(t_taken, n + g + 1)
                    for k in range(GB):
                        last = pe.transpose(Tps[:, g % T_SLOTS, cols(P, k)], ln[:, g * GB + k, :], ident[:, :])
                    last.then_inc(t_ready, 1)

            def to_q_or_k(m, n, first=False):
                if first:
                    pe.wait_ge(t_taken, n + T_SLOTS)
                for g in range(NG):
                    pe.wait_ge(t_taken, n + g + 1)
                    pe.matmul(Tps[:, g % T_SLOTS, 0:GW], weights[:, 1 + m, :], lnT[:, cols(GW, g)],
                              start=True, stop=True).then_inc(t_ready, 1)

            def to_v(n):
                for g in range(NG):
                    pe.wait_ge(o_taken, n + g + 1)
                    for k in range(GB):
                        last = pe.matmul(Ops[:, g % 2, cols(P, k)], lnT[:, cols(P, g * GB + k)], weights[:, 3, :],
                                         start=True, stop=True)
                    last.then_inc(o_ready, 1)

            def scores(b, qt, t):
                pe.wait_ge(q_staged, TILES * b + qt + 1)
                for g in range(NG):
                    pe.wait_ge(s_taken, S_USES * b + NG * qt + g + 1)
                    pe.matmul(Sps[:, g % S_SLOTS, 0:GW], q_tile[:, t, :], kT[:, bass.ds((b % 2) * N + g * GW, GW)],
                              start=True, stop=True).then_inc(s_ready, 1)

            def attend(b, qt, t, last=False):
                n = t_at(b, qt, last)

                def values(g):
                    if g == 0:
                        pe.wait_ge(o_taken, o_at(b, qt, last) + 1)
                    pe.wait_ge(t_taken, n + g + 1 + T_SLOTS)
                    for kt in range(g * GB, (g + 1) * GB):
                        product = pe.matmul(Ops[:, t, 0:C], PT[:, kt, :], v[:, bass.ds((b % 2) * TILES + kt, 1), :].rearrange("p t c -> p (t c)"),
                                            start=kt == 0, stop=kt == TILES - 1)
                    if g == NG - 1:
                        product.then_inc(o_ready, 1)

                pe.wait_ge(p_ready, TILES * b + qt + 1)
                for g in range(NG):
                    pe.wait_ge(t_taken, n + g + 1)
                    for k in range(GB):
                        block_t = pe.transpose(Tps[:, g % T_SLOTS, cols(P, k)], S[:, t, cols(P, g * GB + k)], ident[:, :])
                    block_t.then_inc(t_ready, 1)
                    if g > 1:
                        values(g - 2)
                values(NG - 2)
                values(NG - 1)

            def projected(t_after, o_after):
                pe.wait_ge(t_taken, t_after + T_SLOTS)
                pe.wait_ge(o_taken, o_after + O_SLOTS)

            project(0, 0)
            transpose_ln(0, 0)
            to_q_or_k(0, NG, first=True)
            to_q_or_k(1, 2 * NG)
            to_v(NG)
            projected(T_PREP, O_PREP)
            scores(0, 0, 0)
            with pe.Fori(0, B - 1) as b:
                prepare = {
                    PROJECT: lambda: project(b + 1, o_at(b, PROJECT, after=False)),
                    TRANSPOSE: lambda: transpose_ln(b + 1, t_at(b, TRANSPOSE, after=False)),
                    TO_Q: lambda: to_q_or_k(0, t_at(b, TO_Q, after=False), first=True),
                    TO_K: lambda: to_q_or_k(1, t_at(b, TO_K, after=False)),
                    TO_V: lambda: to_v(o_at(b, TO_V, after=False)),
                }
                for qt in range(TILES):
                    if qt in prepare:
                        prepare[qt]()
                    if qt + 1 < TILES:
                        scores(b, qt + 1, (qt + 1) % 2)
                    else:
                        projected(t_at(b, TO_K), o_at(b, TO_V))
                        scores(b + 1, 0, 0)
                    attend(b, qt, qt % 2)
            with pe.Fori(0, TILES // 2 - 1) as qp:
                for t in range(2):
                    scores(B - 1, 2 * qp + t + 1, 1 - t)
                    attend(B - 1, 2 * qp + t, t, last=True)
            scores(B - 1, TILES - 1, 1)
            attend(B - 1, TILES - 2, 0, last=True)
            attend(B - 1, TILES - 1, 1, last=True)

        @block.vector
        def _(dve):
            def image(i, lo, hi):
                return x1[:, bass.ds(i * TILES + lo, hi - lo), :]

            def row(i, t):
                return x1[:, bass.ds(i * TILES + t, 1), :].rearrange("p t c -> p (t c)")

            def invert(i):
                dve.wait_ge(den_in, 16 * (i + 1))
                for x in (0, 2):
                    last = dve.tensor_tensor(den[:, x, :], den[:, x, :], den[:, x + 1, :], ALU.add)
                last.then_inc(den_step, 1)
                dve.wait_ge(den_step, 2 * i + 1)
                dve.tensor_tensor(den_sum[:, :], den[:, 0, :], den[:, 2, :], ALU.add).then_inc(den_step, 1)
                dve.wait_ge(den_step, 2 * i + 2)
                dve.reciprocal(den_sum[:, :], den_sum[:, :]).then_inc(inv_ready, 1)

            def sum_half(i, half):
                dve.wait_ge(half_in, 16 * (2 * i + half + 1))
                for x in (0, 2):
                    last = dve.tensor_tensor(num[:, x, :], num[:, x, :], num[:, x + 1, :], ALU.add)
                last.then_inc(sum_step, 1)
                dve.wait_ge(sum_step, 4 * i + 2 * half + 1)
                dve.tensor_tensor(num[:, 0, :], num[:, 0, :], num[:, 2, :], ALU.add).then_inc(sum_step, 1)

            def finish_half(i, half):
                part = slice(half * HN, (half + 1) * HN)
                dve.wait_ge(sum_step, 4 * i + 2 * half + 2)
                if half == 0:
                    dve.wait_ge(inv_in, 16 * (i + 1))
                dve.tensor_tensor(z[:, part], num[:, 0, :], z[:, part], ALU.mult).then_inc(half_taken, 1)
                dve.wait_ge(half_taken, 2 * i + half + 1)
                if half == 0:
                    dve.wait_ge(conv_in, 16 * (i + 1))
                last = dve.tensor_tensor(z[:, part], z[:, part], conv[:, part], ALU.add)
                if half == 1:
                    last.then_inc(z_ready, 1)

            def take_projected(i, n):
                dve.wait_ge(x_biased, i + 1)
                for g in range(NG):
                    dve.wait_ge(o_ready, n + g + 1)
                    alone(dve)
                    dve.tensor_tensor(image(i, g * GB, (g + 1) * GB), Ops[:, g % 2, 0:GW].rearrange("p (t c) -> p t c", t=GB),
                                      xin[:, cols(GB, g), :], ALU.add).then_inc(o_taken, 1)

            def statistics(i, n):
                dve.wait_ge(o_taken, n + NG + O_SLOTS)
                alone(dve)
                for t in range(TILES):
                    last = dve.bn_stats(stats[:, t, :], row(i, t))
                last.then_inc(ln_step, 1)

            def variances(i):
                dve.wait_ge(ln_step, 2 * i + 1)
                alone(dve)
                for t in range(TILES):
                    last = dve.bn_aggr(mv[:, t, :], stats[:, t, :])
                last.then_inc(var_ready, 1)

            def normalise(i):
                dve.wait_ge(sd_ready, i + 1)
                dve.reciprocal(rstd[:, :], sd[:, :]).then_inc(ln_step, 1)
                dve.wait_ge(ln_step, 2 * i + 2)
                alone(dve)
                for t in range(TILES):
                    last = dve.tensor_scalar(ln[:, t, :], row(i, t), mv[:, t, 0:1], rstd[:, t:t + 1], ALU.subtract, ALU.mult)
                last.then_inc(ln_ready, 1)

            def take_v(i, n):
                for g in range(NG):
                    dve.wait_ge(o_ready, n + g + 1)
                    alone(dve)
                    dve.tensor_tensor(v[:, bass.ds((i % 2) * TILES + g * GB, GB), :], Ops[:, g % 2, 0:GW].rearrange("p (t c) -> p t c", t=GB),
                                      bv_all[:, :, :], ALU.add).then_inc(o_taken, 1)

            def stage(b, qt, t):
                dve.tensor_copy(q_tile[:, t, :], qT[:, bass.ds((b % 2) * N + qt * P, P)]).then_inc(q_staged, 1)

            def take_scores(b, qt, t, free):
                for g in range(NG):
                    if g == 0 and free is not None:
                        dve.wait_ge(t_ready, free)
                    dve.wait_ge(s_ready, S_USES * b + NG * qt + g + 1)
                    dve.tensor_scalar(S[:, t, cols(GW, g)], Sps[:, g % S_SLOTS, 0:GW],
                                      1.0, None, ALU.mult, ALU.max, accum_out=part_max[:, t, g:g + 1]).then_inc(s_taken, 1)
                dve.wait_ge(s_taken, S_USES * b + NG * (qt + 1) + S_SLOTS)
                dve.tensor_reduce(neg_max[:, t:t + 1], part_max[:, t, :], AX.X, ALU.max, negate=True).then_inc(max_ready, 1)

            def invert_total(b, qt, t):
                dve.wait_ge(p_ready, TILES * b + qt + 1)
                dve.reciprocal(inv_total[:, t:t + 1], total[:, t:t + 1]).then_inc(inv_step, 1)

            def take_values(b, qt, t, last=False):
                dve.wait_ge(inv_step, TILES * b + qt + 1)
                dve.wait_ge(o_ready, o_at(b, qt, last) + 1)
                alone(dve)
                dve.scalar_tensor_tensor(out=row(b, qt), in0=Ops[:, t, 0:C], scalar=inv_total[:, t:t + 1], in1=row(b, qt),
                                         op0=ALU.mult, op1=ALU.add).then_inc(o_taken, 1)
                dve.wait_ge(o_taken, o_at(b, qt, last) + 1 + O_SLOTS)
                alone(dve)
                dve.bn_stats(row_stats[:, :], row(b, qt)).then_inc(row_step, 1)
                dve.wait_ge(row_step, 2 * (TILES * b + qt) + 1)
                alone(dve)
                dve.bn_aggr(row_moments[:, :], row_stats[:, :]).then_inc(row_step, 1)
                dve.wait_ge(row_step, 2 * (TILES * b + qt) + 2)
                alone(dve)
                dve.tensor_copy(moments[:, bass.ds(b * TILES + qt, 1), :].rearrange("p t c -> p (t c)"), row_moments[:, :])

            dve.sem_inc(o_taken, O_SLOTS)
            dve.sem_inc(s_taken, S_SLOTS)
            invert(0)
            sum_half(0, 0)
            dve.wait_ge(small_ready, 1)
            dve.tensor_copy(biases[:, :], Tps[:, 0, 0:2]).then_inc(small_taken, 1)
            for dst, src in ((bo_all, Tps[:, 1, 0:C]), (bv_all, Tps[:, 1, C:2 * C])):
                for k in range(GB):
                    last = dve.tensor_copy(dst[:, k, :], src)
                last.then_inc(small_taken, 1)
            dve.wait_ge(small_taken, 3)
            finish_half(0, 0)
            sum_half(0, 1)
            finish_half(0, 1)
            take_projected(0, 0)
            statistics(0, 0)
            variances(0)
            normalise(0)
            take_v(0, NG)
            dve.wait_ge(t_taken, T_PREP + T_SLOTS)
            stage(0, 0, 0)
            stage(0, 1, 1)
            take_scores(0, 0, 0, None)
            with dve.Fori(0, B - 1) as b:
                before = {
                    PROJECT: lambda: take_projected(b + 1, o_at(b, PROJECT, after=False)),
                    TO_V: lambda: take_v(b + 1, o_at(b, TO_V, after=False)),
                }
                behind = {
                    0: lambda: invert(b + 1),
                    1: lambda: sum_half(b + 1, 0),
                    3: lambda: finish_half(b + 1, 0),
                    5: lambda: sum_half(b + 1, 1),
                    6: lambda: finish_half(b + 1, 1),
                    8: lambda: statistics(b + 1, o_at(b, PROJECT, after=False)),
                    9: lambda: variances(b + 1),
                    10: lambda: normalise(b + 1),
                }
                for qt in range(TILES):
                    t = qt % 2
                    if qt in before:
                        take_values(b, qt - 1, 1 - t)
                        before[qt]()
                    if qt + 1 < TILES:
                        take_scores(b, qt + 1, 1 - t, t_at(b, qt))
                    else:
                        take_scores(b + 1, 0, 0, t_at(b, qt))
                    if qt + 2 < TILES:
                        stage(b, qt + 2, t)
                    else:
                        if qt + 2 == TILES:
                            dve.wait_ge(t_taken, t_at(b, TO_K, after=False) + T_SLOTS)
                            alone(dve)
                        stage(b + 1, qt + 2 - TILES, t)
                    invert_total(b, qt, t)
                    if qt in behind:
                        behind[qt]()
                    if qt and qt not in before:
                        take_values(b, qt - 1, 1 - t)
                take_values(b, TILES - 1, 1)

            def last_tile(qt, t, ahead=2, values=True):
                if ahead:
                    take_scores(B - 1, qt + 1, 1 - t, t_at(B - 1, qt, True))
                if ahead > 1:
                    stage(B - 1, qt + 2, t)
                invert_total(B - 1, qt, t)
                if values:
                    take_values(B - 1, qt - 1, 1 - t, last=True)

            last_tile(0, 0, values=False)
            with dve.Fori(0, TILES // 2 - 2) as qp:
                last_tile(2 * qp + 1, 1)
                last_tile(2 * qp + 2, 0)
            last_tile(TILES - 3, 1)
            last_tile(TILES - 2, 0, ahead=1)
            last_tile(TILES - 1, 1, ahead=0)
            take_values(B - 1, TILES - 1, 1, last=True)


def layer1_ffn(nc, a, s, ident, x1, moments, out):
    with ExitStack() as ctx:
        sb, ps = buffers(nc, ctx, "e")
        sem = sem_maker(nc, ctx, "e")
        PICKS = 2 * TOPK + 1
        ln = sb("ln", [P, B * TILES, C])
        lnT = sb("lnT", [P, B, N])
        W1 = sb("W1", [P, E, FF])
        W2 = sb("W2", [P, E, FH * C])
        b1_rows = sb("b1_rows", [E * FH, P])
        b1 = sb("b1", [P, E, FH])
        b2 = sb("b2", [P, E, C])
        Wr = sb("Wr", [P, E])
        br = sb("br", [1, E])
        vectors = sb("vectors", [1, 2, C])
        gamma = sb("gamma", [P, 1, C])
        beta = sb("beta", [P, 1, C])
        ones = sb("ones", [P, P])
        eps = sb("eps", [P, 1])
        sd = sb("sd", [P, B * TILES])
        rstd = sb("rstd", [P, B * TILES])
        sums = sb("sums", [P, B, NG])
        means = sb("means", [P, B])
        r = sb("r", [B, 16, E])
        rc = sb("rc", [B, 16])
        greater = sb("greater", [B, E, 2 * E])
        choice = sb("choice", [B, PICKS, E])
        pick = sb("pick", [B, B, P])
        sel = sb("sel", [P, B, PICKS * E])
        w1s = sb("w1s", [P, 2, TOPK, FF])
        w2s = sb("w2s", [P, 2, TOPK, FH * C])
        b1s = sb("b1s", [P, 2, TOPK, FH])
        b2s = sb("b2s", [P, 2, C])
        hid = sb("hid", [P, 2, TOPK * FH, GW])
        ystats = sb("ystats", [P, TILES, 6])
        ymv = sb("ymv", [P, TILES, 2])
        ysd = sb("ysd", [P, TILES])
        yrstd = sb("yrstd", [P, TILES])
        ln_stage = sb("ln_stage", [P, TILES, C])

        Hps = ps("Hps", [P, 4, BANK])
        Yps = ps("Yps", [P, 2, BANK])
        Rps = ps("Rps", [P, 2, BANK])

        weights_in, small_in, constants, small_ready, small_taken = sem("weights_in"), sem("small_in"), sem("constants"), sem("small_ready"), sem("small_taken")
        sd_ready, rstd_ready, ln_ready, ln_kept = sem("sd_ready"), sem("rstd_ready"), sem("ln_ready"), sem("ln_kept")
        t_ready, t_taken = sem("t_ready"), sem("t_taken")
        route_pe, route_act, route_dve = sem("route_pe"), sem("route_act"), sem("route_dve")
        select_step, selected = sem("select_step"), sem("selected")
        h_ready, h_taken, y_ready, y_taken = sem("h_ready"), sem("h_taken"), sem("y_ready"), sem("y_taken")
        base_ready, y_step, yvar_ready, ysd_ready = sem("base_ready"), sem("y_step"), sem("yvar_ready"), sem("ysd_ready")
        y_normed, res_ready, scaled, out_ready, out_stored = sem("y_normed"), sem("res_ready"), sem("scaled"), sem("out_ready"), sem("out_stored")
        mean_step, sel_ready = sem("mean_step"), sem("sel_ready")
        ROUTE_STEPS = 22
        HK = TOPK * FH

        block = ctx.enter_context(nc.Block())

        @block.sync
        def _(sp):
            sp.dma_start(vectors[:, 0, :], a["gamma"].rearrange("(a n) -> a n", a=1)).then_inc(small_in, 16)
            sp.dma_start(vectors[:, 1, :], a["beta"].rearrange("(a n) -> a n", a=1)).then_inc(small_in, 16)
            sp.dma_start(b1_rows[:, :], a["b1"].rearrange("e (h p) -> (e h) p", p=P)).then_inc(small_in, 16)
            sp.dma_start(Wr[:, :], a["Wr"]).then_inc(small_in, 16)
            sp.dma_start(br[:, :], a["br"].rearrange("(a n) -> a n", a=1)).then_inc(small_in, 16)
            sp.dma_start(W1[:, :, :], a["W1"].rearrange("e p f -> p e f")).then_inc(weights_in, 16)
            sp.dma_start(W2[:, :, :].rearrange("p e (h d) -> p e h d", h=FH), a["W2"].rearrange("e (h p) d -> p e h d", p=P)).then_inc(weights_in, 16)
            sp.dma_start(b2[:, :, :], a["b2"].unsqueeze(0).to_broadcast([P, E, C])).then_inc(weights_in, 16)
            with sp.Fori(0, B) as b:
                for half in range(2):
                    sp.wait_ge(out_ready, 2 * b + half + 1)
                    alone(sp)
                    sp.dma_start(out[b][:, cols(HT, half), :], ln[:, bass.ds(b * TILES + half * HT, HT), :]).then_inc(out_stored, 16)
            sp.wait_ge(out_stored, 32 * B)

        @block.gpsimd
        def _(pool):
            pool.memset(ones[:, :], 1.0).then_inc(constants, 1)
            pool.memset(eps[:, :], 1e-5).then_inc(constants, 1)
            pool.memset(greater[:, :, :], 0.0).then_inc(constants, 1)
            def tokens(of, b, half):
                return of[:, bass.ds(b * TILES + half * HT, HT), :]

            def everywhere(vector):
                return vector.to_broadcast([P, HT, C])

            with pool.Fori(0, B) as b:
                for g in range(NG):
                    pool.wait_ge(ln_ready, NG * b + g + 1)
                    alone(pool)
                    pool.tensor_copy(ln[:, bass.ds(b * TILES + g * GB, GB), :], ln_stage[:, cols(GB, g), :]).then_inc(ln_kept, 1)
            pool.wait_ge(small_taken, 3)
            with pool.Fori(0, B) as b:
                for half in range(2):
                    last = pool.tensor_tensor(tokens(x1, b, half), tokens(x1, b, half), everywhere(beta[:, :, :]), ALU.add)
                last.then_inc(res_ready, 1)

            def base(b, t):
                pool.wait_ge(selected, b + 1)
                alone(pool)
                for half in range(2):
                    last = pool.tensor_tensor(tokens(ln, b, half), tokens(ln, b, half), everywhere(b2s[:, t:t + 1, :]), ALU.add)
                last.then_inc(base_ready, 1)

            def result(b):
                for half in range(2):
                    pool.wait_ge(y_normed, 2 * b + half + 1)
                    alone(pool)
                    pool.tensor_tensor(tokens(ln, b, half), tokens(ln, b, half), everywhere(gamma[:, :, :]), ALU.mult).then_inc(scaled, 1)
                    pool.wait_ge(res_ready, B)
                    pool.wait_ge(scaled, 2 * b + half + 1)
                    alone(pool)
                    pool.tensor_tensor(tokens(ln, b, half), tokens(ln, b, half), tokens(x1, b, half), ALU.add).then_inc(out_ready, 1)

            pool.wait_ge(ln_kept, NG * (B + 1))
            base(0, 0)
            with pool.Fori(0, B // 2 - 1) as bp:
                for t in range(2):
                    base(2 * bp + t + 1, 1 - t)
                    result(2 * bp + t)
            base(B - 1, 1)
            result(B - 2)
            result(B - 1)

        @block.scalar
        def _(act):
            act.sem_inc(t_taken, 2)
            act.sem_inc(h_taken, 4)
            act.wait_ge(constants, 3)
            act.activation(sd[:, :], moments[:, :, 1:2].rearrange("p t a -> p (t a)"), ACT.Sqrt, bias=eps[:, :]).then_inc(sd_ready, 1)
            with act.Fori(0, B) as b:
                for g in range(NG):
                    act.wait_ge(t_ready, NG * (b + 1) + g + 1)
                    alone(act)
                    act.activation(lnT[:, bass.ds(b, 1), cols(GW, g)].rearrange("p a n -> p (a n)"), Rps[:, g % 2, 0:GW], ACT.Copy,
                                   accum_out=sums[:, bass.ds(b, 1), g:g + 1].rearrange("p a n -> p (a n)")).then_inc(t_taken, 1)
            act.wait_ge(route_dve, 2)
            act.activation(r[:, 1, :], r[:, 0, :], ACT.Exp, bias=rc[:, 0:1], accum_out=rc[:, 1:2]).then_inc(route_act, 1)
            act.wait_ge(route_dve, 9)
            act.activation(r[:, 6, :], r[:, 5, :], ACT.Exp, bias=rc[:, 3:4], accum_out=rc[:, 4:5]).then_inc(route_act, 1)
            act.wait_ge(route_dve, 17)
            act.activation(rc[:, 9:10], rc[:, 8:9], ACT.Exp).then_inc(route_act, 1)

            def gelu(b, g):
                n = NG * b + g
                act.wait_ge(selected, b + 1)
                if n > 1:
                    act.wait_ge(y_ready, n - 1)
                for i in range(HK):
                    act.wait_ge(h_ready, HK * n + i + 1)
                    act.activation(hid[:, g % 2, i, :], Hps[:, i, 0:GW], ACT.Gelu,
                                   bias=b1s[:, b % 2, i // FH, i % FH:i % FH + 1]).then_inc(h_taken, 1)

            gelu(0, 0)
            for b in range(B):
                for g in range(1, NG):
                    gelu(b, g)
                if b + 1 < B:
                    gelu(b + 1, 0)
                act.wait_ge(yvar_ready, b + 1)
                act.activation(ysd[:, :], ymv[:, :, 1:2].rearrange("p t a -> p (t a)"), ACT.Sqrt, bias=eps[:, :]).then_inc(ysd_ready, 1)

        @block.tensor
        def _(pe):
            pe.wait_ge(small_in, 16 * 5)
            pe.wait_ge(constants, 3)
            pe.matmul(Hps[:, 0, 0:C], ones[0:1, :], vectors[0:1, 0, :], start=True, stop=True)
            pe.matmul(Hps[:, 1, 0:C], ones[0:1, :], vectors[0:1, 1, :], start=True, stop=True)
            pe.transpose(Hps[:, 2, 0:E * FH], b1_rows[:, :], ident[0:E * FH, 0:E * FH]).then_inc(small_ready, 1)
            pe.sem_inc(t_ready, NG)
            with pe.Fori(0, B) as b:
                for g in range(NG):
                    pe.wait_ge(ln_ready, NG * b + g + 1)
                    pe.wait_ge(t_taken, NG * b + g + 1)
                    for k in range(GB):
                        last = pe.transpose(Rps[:, g % 2, cols(P, k)], ln_stage[:, g * GB + k, :], ident[:, :])
                    last.then_inc(t_ready, 1)
            pe.wait_ge(route_dve, 1)
            pe.matmul(Rps[0:B, 0, 0:E], means[:, :], Wr[:, :], start=True, stop=False)
            pe.matmul(Rps[0:B, 0, 0:E], ones[0:1, 0:B], br[:, :], start=False, stop=True).then_inc(route_pe, 1)
            pe.wait_ge(route_dve, 4)
            pe.matmul(Rps[0:B, 0, 0:E], ones[0:B, 0:B], r[:, 2, :], start=True, stop=True).then_inc(route_pe, 1)
            pe.wait_ge(route_dve, ROUTE_STEPS)
            for b in range(B):
                last = pe.matmul(Rps[:, 0, cols(PICKS * E, b)], pick[:, b, :], choice[:, :, :].rearrange("b s e -> b (s e)"), start=True, stop=True)
            last.then_inc(route_pe, 1)
            pe.wait_ge(small_taken, 3)

            def hidden(b, t, g):
                n = NG * b + g
                if g == 0:
                    pe.wait_ge(selected, b + 1)
                for i in range(HK):
                    pe.wait_ge(h_taken, HK * n + i + 1)
                    pe.matmul(Hps[:, i, 0:GW], w1s[:, t, i // FH, cols(P, i % FH)],
                              lnT[:, bass.ds(b, 1), cols(GW, g)].rearrange("p a n -> p (a n)"), start=True, stop=True).then_inc(h_ready, 1)

            def outputs(b, t, g):
                n = NG * b + g
                pe.wait_ge(h_taken, HK * (n + 1) + 4)
                pe.wait_ge(y_taken, n + 1)
                for k in range(GB):
                    for i in range(HK):
                        last = pe.matmul(Yps[:, g % 2, cols(P, k)], hid[:, g % 2, i, cols(P, k)],
                                         w2s[:, t, i // FH, cols(C, i % FH)], start=i == 0, stop=i == HK - 1)
                last.then_inc(y_ready, 1)

            hidden(0, 0, 0)
            with pe.Fori(0, B // 2 - 1) as bp:
                for t in range(2):
                    for g in range(NG):
                        if g + 1 < NG:
                            hidden(2 * bp + t, t, g + 1)
                        else:
                            hidden(2 * bp + t + 1, 1 - t, 0)
                        outputs(2 * bp + t, t, g)
            for t in range(2):
                for g in range(NG):
                    if g + 1 < NG:
                        hidden(B - 2 + t, t, g + 1)
                    elif t == 0:
                        hidden(B - 1, 1, 0)
                    outputs(B - 2 + t, t, g)

        @block.vector
        def _(dve):
            dve.sem_inc(y_taken, 2)
            dve.wait_ge(small_ready, 1)
            dve.tensor_copy(gamma[:, 0, :], Hps[:, 0, 0:C]).then_inc(small_taken, 1)
            dve.tensor_copy(beta[:, 0, :], Hps[:, 1, 0:C]).then_inc(small_taken, 1)
            dve.tensor_copy(b1[:, :, :].rearrange("p e h -> p (e h)"), Hps[:, 2, 0:E * FH]).then_inc(small_taken, 1)
            dve.sem_inc(ln_kept, NG)
            dve.wait_ge(sd_ready, 1)
            dve.reciprocal(rstd[:, :], sd[:, :]).then_inc(rstd_ready, 1)
            dve.wait_ge(rstd_ready, 1)
            with dve.Fori(0, B) as b:
                for g in range(NG):
                    dve.wait_ge(t_ready, NG * b + g + 1)
                    dve.wait_ge(ln_kept, NG * b + g + 1)
                    alone(dve)
                    for k in range(GB):
                        at = b * TILES + (g * GB + k)
                        last = dve.tensor_scalar(ln_stage[:, g * GB + k, :], x1[:, bass.ds(at, 1), :].rearrange("p t c -> p (t c)"),
                                                 moments[:, bass.ds(at, 1), 0:1].rearrange("p t c -> p (t c)"), rstd[:, bass.ds(at, 1)],
                                                 ALU.subtract, ALU.mult)
                    last.then_inc(ln_ready, 1)

            steps = [0]

            def step(instruction):
                steps[0] += 1
                instruction.then_inc(route_dve, 1)
                dve.wait_ge(route_dve, steps[0])

            dve.wait_ge(t_taken, NG * B + 2)
            dve.tensor_reduce(means[:, :], sums[:, :, :], AX.X, ALU.add).then_inc(mean_step, 1)
            dve.wait_ge(mean_step, 1)
            for b in range(B):
                dve.tensor_scalar(pick[:, b, :], ones[0:B, :], ident[0:B, b:b + 1], None, ALU.mult)
            step(dve.tensor_scalar(means[:, :], means[:, :], 1.0 / N, None, ALU.mult))
            dve.wait_ge(route_pe, 1)
            dve.tensor_copy(r[:, 0, :], Rps[0:B, 0, 0:E])
            step(dve.tensor_reduce(rc[:, 0:1], Rps[0:B, 0, 0:E], AX.X, ALU.max, negate=True))
            dve.wait_ge(route_act, 1)
            step(dve.reciprocal(rc[:, 2:3], rc[:, 1:2]))
            step(dve.tensor_scalar(r[:, 2, :], r[:, 1, :], rc[:, 2:3], None, ALU.mult))
            dve.wait_ge(route_pe, 2)
            step(dve.tensor_scalar(r[:, 3, :], Rps[0:B, 0, 0:E], float(N), None, ALU.mult))
            step(dve.reciprocal(r[:, 4, :], r[:, 3, :]))
            step(dve.tensor_scalar(r[:, 4, :], r[:, 4, :], CAPACITY, 1.0, ALU.mult, ALU.min))
            step(dve.tensor_tensor(r[:, 5, :], r[:, 2, :], r[:, 4, :], ALU.mult))
            step(dve.tensor_reduce(rc[:, 3:4], r[:, 5, :], AX.X, ALU.max, negate=True))
            dve.wait_ge(route_act, 2)
            step(dve.reciprocal(rc[:, 5:6], rc[:, 4:5]))
            step(dve.tensor_scalar(r[:, 7, :], r[:, 6, :], rc[:, 5:6], None, ALU.mult))
            for e in range(E):
                last = dve.tensor_scalar(greater[:, e, 0:E], r[:, 7, :], r[:, 7, e:e + 1], None, ALU.is_gt)
                if e:
                    last = dve.tensor_scalar(greater[:, e, E:E + e], r[:, 7, 0:e], r[:, 7, e:e + 1], None, ALU.is_equal)
            step(last)
            step(dve.tensor_reduce(r[:, 8, :], greater[:, :, :], AX.X, ALU.add))
            for k in range(TOPK):
                last = dve.tensor_scalar(choice[:, k, :], r[:, 8, :], float(k), None, ALU.is_equal)
            step(last)
            for k in range(TOPK):
                last = dve.tensor_tensor(r[:, 9 + k, :], choice[:, k, :], r[:, 7, :], ALU.mult)
            step(last)
            step(dve.tensor_reduce(rc[:, 6:8], r[:, 9:9 + TOPK, :], AX.X, ALU.add))
            step(dve.tensor_tensor(rc[:, 8:9], rc[:, 7:8], rc[:, 6:7], ALU.subtract))
            assert steps[0] == 17, steps
            dve.wait_ge(route_act, 3)
            step(dve.tensor_scalar(rc[:, 10:11], rc[:, 9:10], 1.0, None, ALU.add))
            step(dve.reciprocal(rc[:, 11:12], rc[:, 10:11]))
            step(dve.tensor_tensor(rc[:, 12:13], rc[:, 11:12], rc[:, 9:10], ALU.mult))
            for k in range(TOPK):
                last = dve.tensor_scalar(choice[:, TOPK + k, :], choice[:, k, :], rc[:, 11 + k:12 + k], None, ALU.mult)
            step(last)
            step(dve.tensor_tensor(choice[:, 2 * TOPK, :], choice[:, TOPK, :], choice[:, TOPK + 1, :], ALU.add))
            assert steps[0] == ROUTE_STEPS, steps
            dve.wait_ge(route_pe, 3)
            dve.tensor_copy(sel[:, :, :].rearrange("p b s -> p (b s)"), Rps[:, 0, 0:B * PICKS * E]).then_inc(sel_ready, 1)
            dve.wait_ge(sel_ready, 1)
            dve.wait_ge(weights_in, 16 * 3)

            def select(b, t, experts):
                for e in experts:
                    def of(slot):
                        return sel[:, bass.ds(b, 1), slot * E + e:slot * E + e + 1].rearrange("p a n -> p (a n)")

                    jobs = [(b2s[:, t, :], b2[:, e, :], of(2 * TOPK))]
                    for k in range(TOPK):
                        jobs.append((w1s[:, t, k, :], W1[:, e, :], of(k)))
                        jobs.append((b1s[:, t, k, :], b1[:, e, :], of(k)))
                        jobs.append((w2s[:, t, k, :], W2[:, e, :], of(TOPK + k)))
                    if e:
                        dve.wait_ge(select_step, (E - 1) * b + e)
                        alone(dve)
                    for dst, src, factor in jobs:
                        if e == 0:
                            last = dve.tensor_scalar(dst, src, factor, None, ALU.mult)
                        else:
                            last = dve.scalar_tensor_tensor(out=dst, in0=src, scalar=factor, in1=dst, op0=ALU.mult, op1=ALU.add)
                    last.then_inc(select_step if e < E - 1 else selected, 1)

            def variances(b, g):
                dve.wait_ge(y_step, (NG + 1) * b + g + 1)
                alone(dve)
                for t in tiles_of(g):
                    last = dve.bn_aggr(ymv[:, t, :], ystats[:, t, :])
                return last

            def close(b, g):
                n = NG * b + g
                if g == 0:
                    dve.wait_ge(base_ready, b + 1)
                dve.wait_ge(y_ready, n + 1)
                alone(dve)
                tok = ln[:, bass.ds(b * TILES + g * GB, GB), :]
                dve.tensor_tensor(tok, Yps[:, g % 2, 0:GW].rearrange("p (t c) -> p t c", t=GB), tok, ALU.add).then_inc(y_taken, 1)
                if g:
                    variances(b, g - 1)
                dve.wait_ge(y_taken, n + 1 + 2)
                alone(dve)
                for t in tiles_of(g):
                    last = dve.bn_stats(ystats[:, t, :], ln[:, bass.ds(b * TILES + t, 1), :].rearrange("p t c -> p (t c)"))
                last.then_inc(y_step, 1)

            def finish(b):
                variances(b, NG - 1).then_inc(yvar_ready, 1)
                dve.wait_ge(ysd_ready, b + 1)
                dve.reciprocal(yrstd[:, :], ysd[:, :]).then_inc(y_step, 1)
                dve.wait_ge(y_step, (NG + 1) * (b + 1))
                alone(dve)
                for t in range(TILES):
                    row = ln[:, bass.ds(b * TILES + t, 1), :].rearrange("p t c -> p (t c)")
                    last = dve.tensor_scalar(row, row, ymv[:, t, 0:1], yrstd[:, t:t + 1], ALU.subtract, ALU.mult)
                    if t % HT == HT - 1:
                        last.then_inc(y_normed, 1)

            def experts_products(b, t, ahead=True):
                for g in range(NG):
                    if ahead:
                        select(b + 1, 1 - t, range(2 * g, min(2 * g + 2, E)))
                    close(b, g)
                finish(b)

            select(0, 0, range(E))
            with dve.Fori(0, B // 2 - 1) as bp:
                for t in range(2):
                    experts_products(2 * bp + t, t)
            experts_products(B - 2, 0)
            experts_products(B - 1, 1, ahead=False)


def hybrid(nc, a, out):
    def scratch(name, n, dt=F32):
        return nc.dram_tensor(name, (n,), dt, kind="Internal").ap()

    q = scratch("q_parts", HEADS * KR * B * N, BF16).rearrange(
        "(h s d b n) -> h s d b n", h=HEADS, s=len(Q_SLOTS), d=D, b=B)
    k = scratch("k_parts", HEADS * 3 * D * B * N, BF16).rearrange(
        "(h s d b n) -> h s d b n", h=HEADS, s=3, d=D, b=B)
    v = scratch("v_heads", HEADS * P * B * TILES * D).rearrange("(h p b x) -> h p b x", h=HEADS, p=P, b=B)
    num = scratch("numerators", B * 4 * C * N)
    den = scratch("denominators", B * 4 * HEADS * N)
    inv = scratch("inverses", B * HEADS * N).rearrange("(b h n) -> b h n", b=B, h=HEADS)
    vpad = scratch("v_padded", B * C * IMAGE_IN).rearrange("(b c n) -> b c n", b=B, c=C)
    conv = scratch("conv_out", B * C * N)
    s = {
        "x_tiles": a["x"].rearrange("b h w c -> b (h w) c").rearrange("b (t p) c -> b p t c", p=P),
        "mask": a["mask"].rearrange("h (t p) n -> (h t) p n", p=P),
        "q_store": q.rearrange("h s d b n -> b s h d n"),
        "k_store": k.rearrange("h s d b n -> b s h d n"),
        "v_store": v.rearrange("h p b x -> b p h x"),
        "q_load": q.rearrange("h s d b n -> h (s d) b n"),
        "k_load": k.rearrange("h s d b n -> h (s d) (b n)"),
        "v_load": v.rearrange("h p b x -> h p (b x)"),
        "o_store": num.rearrange("(b j h d n) -> j h d b n", b=B, j=4, h=HEADS, d=D),
        "o_load": num.rearrange("(b j c n) -> b c j n", b=B, j=4, c=C),
        "den_store": den.rearrange("(b j h n) -> h j b n", b=B, j=4, h=HEADS),
        "den_load": den.rearrange("(b j p n) -> b p j n", b=B, j=4, p=P),
        "inv_store": inv.rearrange("b h (s n) -> b (h s) n", s=D),
        "inv_load": inv,
        "vpad_store": vpad,
        "vpad_load": vpad,
        "conv_store": conv.rearrange("(b c f h w) -> b f c h w", b=B, c=C, f=2, w=W),
        "conv": conv.rearrange("(b c n) -> b c n", b=B, c=C),
    }
    out_tiles = out.rearrange("b h w c -> b (h w) c").rearrange("b (t p) c -> b p t c", p=P)
    with ExitStack() as ctx:
        ident = ctx.enter_context(nc.sbuf_tensor("ident", [P, P], F32))
        taps = ctx.enter_context(nc.sbuf_tensor("taps", [P, TAPS], F32))
        conv_bias = ctx.enter_context(nc.sbuf_tensor("conv_bias", [P, 1], F32))
        layer0_front(nc, {k: a[k] for k in ("Wq", "Wk", "Wv", "bq", "bk", "bv", "dw_w", "dw_b", "sin", "cos")}, s, ident, taps, conv_bias)
        layer0_core(nc, a, s, ident, taps, conv_bias)
        x1 = ctx.enter_context(nc.sbuf_tensor("x1", [P, B * TILES, C], F32))
        moments = ctx.enter_context(nc.sbuf_tensor("moments", [P, B * TILES, 2], F32))
        layer1_attention(nc, a, s, ident, x1, moments)
        layer1_ffn(nc, a, s, ident, x1, moments, out_tiles)


SHORT = {
    "x": "x", "sin": "L0_conv_sin", "cos": "L0_conv_cos", "mask": "L0_conv_mask", "Wq": "L0_conv_Wq",
    "bq": "L0_conv_bq", "Wk": "L0_conv_Wk", "bk": "L0_conv_bk", "Wv": "L0_conv_Wv", "bv": "L0_conv_bv",
    "dw_w": "L0_conv_dw_w", "dw_b": "L0_conv_dw_b", "Wo0": "L0_conv_Wo", "bo0": "L0_conv_bo",
    "Wq1": "L1_attn_Wq", "bq1": "L1_attn_bq", "Wk1": "L1_attn_Wk", "bk1": "L1_attn_bk",
    "Wv1": "L1_attn_Wv", "bv1": "L1_attn_bv", "Wr": "L1_ffn_Wr", "br": "L1_ffn_br", "W1": "L1_ffn_W1",
    "b1": "L1_ffn_b1", "W2": "L1_ffn_W2", "b2": "L1_ffn_b2", "gamma": "L1_ffn_gamma", "beta": "L1_ffn_beta",
}


def kernel(**inputs):
    import concourse.bacc as bacc
    from concourse.bass_utils import run_bass_kernel_spmd

    nc = bacc.Bacc("TRN2", target_bir_lowering=False, num_devices=1)
    arrays, a = {}, {}
    for short, name in SHORT.items():
        x = np.ascontiguousarray(inputs[name])
        arrays[f"in_{short}"] = x
        a[short] = nc.dram_tensor(f"in_{short}", x.shape, mybir.dt.from_np(x.dtype), kind="ExternalInput").ap()
    out = nc.dram_tensor("out", (B, H, W, C), F32, kind="ExternalOutput").ap()
    hybrid(nc, a, out)
    return run_bass_kernel_spmd(nc, [arrays], core_ids=[0]).results[0]["out"]
```

```python
from contextlib import ExitStack

import numpy as np
import concourse.bass as bass
from concourse import mybir

F32 = mybir.dt.float32
BF16 = mybir.dt.bfloat16
ALU = mybir.AluOpType
ACT = mybir.ActivationFunctionType
AX = mybir.AxisListType

P = 128
B, H, W, C = 4, 48, 48, 128
N = H * W
HEADS = 8
D = C // HEADS
TILES = N // P
HT = TILES // 2
GB = 3
GW = GB * P
NG = TILES // GB
CH = 2 * GW
NCH = N // CH
BANK = 512
GROUP = 4
PAD = 2
WP = W + 2 * PAD
TAPS = 25
HALF_H = H // 2
HALF_OUT = HALF_H * WP
PIECES = TILES // 2
PIECE = -(-HALF_OUT // PIECES)
HALF_IN = PIECE * PIECES + (TAPS // 5 - 1) * (WP + 1)
IMAGE_IN = HALF_OUT + HALF_IN
Q_SLOTS = [0, 0, 0, 1, 1, 2]
K_SLOTS = [0, 1, 2, 0, 1, 0]
KR = len(Q_SLOTS) * D
E = 8
FF = 256
FH = FF // P
TOPK = 2
CAPACITY = float(-(-B * N * 1.25 // E))
LOWEST = -3.0e38


def sem_maker(nc, ctx, prefix):
    return lambda name: ctx.enter_context(nc.semaphore(f"{prefix}_{name}"))


def buffers(nc, ctx, prefix):
    def sb(name, shape, dt=F32):
        return ctx.enter_context(nc.sbuf_tensor(f"{prefix}_{name}", shape, dt))

    def ps(name, shape):
        return ctx.enter_context(nc.psum_tensor(f"{prefix}_{name}", shape, F32))

    return sb, ps


def alone(engine):
    engine.nop(nofuse=True)


def cols(b, g):
    return slice(g * b, (g + 1) * b)


def tiles_of(g):
    return range(g * GB, (g + 1) * GB)


def layer0_front(nc, a, s, ident, taps, conv_bias, mask):
    with ExitStack() as ctx:
        sb, ps = buffers(nc, ctx, "f")
        sem = sem_maker(nc, ctx, "f")
        X = sb("X", [P, TILES, C])
        XT = sb("XT", [P, N])
        XN = sb("XN", [P, N])
        cosT = sb("cosT", [P, N])
        sinT = sb("sinT", [P, N])
        angles = sb("angles", [P, 2, TILES, D])
        angles8 = sb("angles8", [P, TILES, HEADS, D])
        rot_sum = sb("rot_sum", [P, 2, N])
        parts = sb("parts", [P, 2, 3, N], BF16)
        t1 = sb("t1", [P, 2, GW])
        t2 = sb("t2", [P, 2, GW])
        V = sb("V", [P, HEADS, TILES, D])
        vpad = sb("vpad", [P, IMAGE_IN])
        weights = sb("weights", [P, 5, C])
        rows = sb("rows", [1, 6, C])
        biases = sb("biases", [P, 6])
        bv_all = sb("bv_all", [P, GB, C])
        ones = sb("ones", [1, P])
        eps = sb("eps", [P, 1])
        average = sb("average", [P, P])
        taps_row = sb("taps_row", [TAPS, C])
        stats = sb("stats", [P, NG, 6])
        mv = sb("mv", [P, 2])
        moments = sb("moments", [P, 2])
        group = sb("group", [P, 2])
        var = sb("var", [P, 1])
        sd = sb("sd", [P, 1])
        rstd = sb("rstd", [P, 1])

        tr = ps("tr", [P, 2, BANK])
        mm = ps("mm", [P, 4, BANK])
        vps = ps("vps", [P, 2, BANK])
        misc = vps[:, 0, :]

        weights_in = sem("weights_in")
        angles_in = sem("angles_in")
        mask_in = sem("mask_in")
        x_in = sem("x_in")
        constants = sem("constants")
        prep = sem("prep")
        scaled_k = sem("scaled_k")
        rotated_w = sem("rotated_w")
        angles_wide = sem("angles_wide")
        small_ready = sem("small_ready")
        small_taken = sem("small_taken")
        tr_ready = sem("tr_ready")
        tr_taken = sem("tr_taken")
        stats_ready = sem("stats_ready")
        norm_step = sem("norm_step")
        group_ready = sem("group_ready")
        var_ready = sem("var_ready")
        sd_ready = sem("sd_ready")
        xn_ready = sem("xn_ready")
        mm_ready = sem("mm_ready")
        mm_taken = sem("mm_taken")
        rot_ready = sem("rot_ready")
        p1_ready = sem("p1_ready")
        d1_ready = sem("d1_ready")
        p2_ready = sem("p2_ready")
        p3_ready = sem("p3_ready")
        q_stored = sem("q_stored")
        k_stored = sem("k_stored")
        v_stored = sem("v_stored")
        vpad_stored = sem("vpad_stored")
        vps_ready = sem("vps_ready")
        vps_taken = sem("vps_taken")

        TR_USES = 2 * NG
        TR_FIRST = 3 * NG
        MM_USES = 4 * NG

        block = ctx.enter_context(nc.Block())

        def remainders(engine, b, m):
            engine.wait_ge(p1_ready, 2 * b + m + 1)
            alone(engine)
            engine.tensor_tensor(rot_sum[:, m, :], rot_sum[:, m, :], parts[:, m, 0, :], ALU.subtract).then_inc(d1_ready, 1)
            engine.wait_ge(p2_ready, 2 * b + m + 1)
            alone(engine)
            engine.tensor_tensor(parts[:, m, 2, :], rot_sum[:, m, :], parts[:, m, 1, :], ALU.subtract).then_inc(p3_ready, 1)

        @block.sync
        def _(sp):
            def load_x(b):
                for half in range(2):
                    sp.dma_start(X[:, cols(HT, half), :], s["x_tiles"][b][:, cols(HT, half), :]).then_inc(x_in, 16)

            load_x(0)
            sp.dma_start(angles[:, 0, :, :], a["cos"].rearrange("h w d -> (h w) d").rearrange("(t p) d -> p t d", p=P)).then_inc(angles_in, 16)
            sp.dma_start(angles[:, 1, :, :], a["sin"].rearrange("h w d -> (h w) d").rearrange("(t p) d -> p t d", p=P)).then_inc(angles_in, 16)
            for i, w in enumerate((a["Wq"], None, a["Wk"], None, a["Wv"])):
                if w is not None:
                    sp.dma_start(weights[:, i, :], w).then_inc(weights_in, 16)
            for i, v in enumerate((a["bq"], None, a["bk"], None, a["bv"], a["dw_b"])):
                if v is not None:
                    sp.dma_start(rows[:, i, :], v.rearrange("(a n) -> a n", a=1)).then_inc(weights_in, 16)
            sp.dma_start(taps_row[:, :], a["dw_w"].rearrange("a b o c -> (a b o) c")).then_inc(weights_in, 16)

            def store_v(b):
                sp.wait_ge(vps_taken, NG * (b + 1) + 2)
                sp.dma_start(s["v_store"][b], V[:, :, :, :].rearrange("p h t d -> p h (t d)")).then_inc(v_stored, 16)

            def store(b):
                sp.wait_ge(tr_taken, TR_FIRST + TR_USES * b + NG + 2)
                sp.dma_start(s["vpad_store"][b], vpad[:, :]).then_inc(vpad_stored, 16)
                for m, (to, stored) in enumerate(((s["q_store"], q_stored), (s["k_store"], k_stored))):
                    for part, (ready, credit) in enumerate(((p1_ready, 0), (p2_ready, 0), (p3_ready, 2))):
                        sp.wait_ge(ready, 2 * b + (m + 1 + credit))
                        sp.dma_start(to[b, part], parts[:, m, part, :]).then_inc(stored, 16)

            sp.wait_ge(tr_ready, NG)
            load_x(1)
            for it in range(4):
                sp.dma_start(mask[:, it, :], s["mask"][it]).then_inc(mask_in, 16)
            with sp.Fori(0, B - 2) as b:
                store_v(b)
                sp.wait_ge(tr_ready, TR_FIRST + TR_USES * (b + 1))
                load_x(b + 2)
                store(b)
            for b in (B - 2, B - 1):
                store_v(b)
                store(b)
            sp.wait_ge(q_stored, 16 * 3 * (B + 1))
            sp.wait_ge(k_stored, 16 * 3 * (B + 1))
            sp.wait_ge(v_stored, 16 * (B + 1))
            sp.wait_ge(vpad_stored, 16 * (B + 1))
            sp.wait_ge(mask_in, 16 * 4)

        @block.gpsimd
        def _(pool):
            pool.memset(average[:, :], 1.0 / GROUP).then_inc(prep, 1)
            pool.memset(ident[:, :], 0.0).then_inc(prep, 1)
            pool.memset(vpad[:, :], 0.0).then_inc(constants, 1)
            pool.memset(ones[:, :], 1.0).then_inc(constants, 1)
            pool.memset(eps[:, :], 1e-5).then_inc(constants, 1)
            pool.wait_ge(prep, 2)
            pool.affine_select(out=ident[:, :], in_=ident[:, :], compare_op=ALU.not_equal, fill=1.0,
                               base=0, pattern=[[-1, P]], channel_multiplier=1).then_inc(constants, 1)
            av = average[:, :].rearrange("p (g k) -> p g k", k=GROUP)
            pool.affine_select(out=av, in_=av, compare_op=ALU.is_ge, fill=0.0, base=0,
                               pattern=[[-GROUP, P // GROUP], [0, GROUP]], channel_multiplier=1).then_inc(prep, 1)
            pool.wait_ge(prep, 3)
            pool.affine_select(out=av, in_=av, compare_op=ALU.is_ge, fill=0.0, base=GROUP - 1,
                               pattern=[[GROUP, P // GROUP], [0, GROUP]], channel_multiplier=-1).then_inc(constants, 1)
            with pool.Fori(0, B - 1) as b:
                for m in range(2):
                    remainders(pool, b, m)
            remainders(pool, B - 1, 0)

        @block.scalar
        def _(act):
            def take_x(b, n):
                for g in range(NG):
                    act.wait_ge(tr_ready, n + g + 1)
                    act.activation(XT[:, cols(GW, g)], tr[:, g % 2, 0:GW], ACT.Copy).then_inc(tr_taken, 1)

            def deviation(b):
                act.wait_ge(var_ready, b + 1)
                act.activation(sd[:, :], var[:, :], ACT.Sqrt, bias=eps[:, :]).then_inc(sd_ready, 1)

            def take_v_image(b):
                act.wait_ge(vpad_stored, 16 * (b + 1))
                for g in range(NG):
                    act.wait_ge(tr_ready, TR_FIRST + TR_USES * b + g + 1)
                    rows_of = GW // W
                    image = vpad[:, 0:(H + 2 * PAD) * WP].rearrange("p (h w) -> p h w", w=WP)
                    dst = image[:, PAD + g * rows_of:PAD + (g + 1) * rows_of, PAD:PAD + W]
                    src = tr[:, g % 2, 0:GW].rearrange("p (h w) -> p h w", w=W)
                    act.activation(dst, src, ACT.Identity, bias=biases[:, 4:5]).then_inc(tr_taken, 1)

            def first_part(b, m):
                act.wait_ge((q_stored, k_stored)[m], 16 * 3 * (b + 1))
                act.wait_ge(rot_ready, 2 * b + m + 1)
                act.activation(parts[:, m, 0, :], rot_sum[:, m, :], ACT.Copy).then_inc(p1_ready, 1)

            def second_part(b, m):
                act.wait_ge(d1_ready, 2 * b + m + 1)
                act.activation(parts[:, m, 1, :], rot_sum[:, m, :], ACT.Copy).then_inc(p2_ready, 1)

            act.sem_inc(q_stored, 16 * 3)
            act.sem_inc(k_stored, 16 * 3)
            act.sem_inc(vpad_stored, 16)
            act.sem_inc(tr_taken, 2)
            take_x(0, 0)
            for m in range(2):
                for g in range(NG):
                    if m == 1 and g == 0:
                        deviation(0)
                    act.wait_ge(tr_ready, NG * (m + 1) + g + 1)
                    act.activation((cosT, sinT)[m][:, cols(GW, g)], tr[:, g % 2, 0:GW], ACT.Copy).then_inc(tr_taken, 1)
            with act.Fori(0, B - 1) as b:
                take_v_image(b)
                take_x(b + 1, TR_FIRST + TR_USES * b + NG)
                first_part(b, 0)
                deviation(b + 1)
                second_part(b, 0)
                first_part(b, 1)
                second_part(b, 1)
            take_v_image(B - 1)
            for m in range(2):
                first_part(B - 1, m)
                second_part(B - 1, m)

        @block.tensor
        def _(pe):
            def transpose_x(b, n):
                pe.wait_ge(x_in, 32 * (b + 1))
                for g in range(NG):
                    pe.wait_ge(tr_taken, n + g + 1)
                    for k in range(GB):
                        last = pe.transpose(tr[:, g % 2, cols(P, k)], X[:, g * GB + k, :], ident[:, :])
                    last.then_inc(tr_ready, 1)

            def transpose_angles(m):
                pe.wait_ge(angles_wide, m + 1)
                for g in range(NG):
                    pe.wait_ge(tr_taken, NG * (m + 1) + g + 1)
                    for k in range(GB):
                        t = g * GB + k
                        last = pe.transpose(tr[:, g % 2, cols(P, k)],
                                            angles8[:, t, :, :].rearrange("p h d -> p (h d)"), ident[:, :])
                    last.then_inc(tr_ready, 1)

            def group_means(b):
                pe.wait_ge(stats_ready, b + 1)
                pe.matmul(misc[:, 0:2], average[:, :], moments[:, :], start=True, stop=True).then_inc(group_ready, 1)

            def v_tokens(b):
                pe.wait_ge(xn_ready, b + 1)
                for g in range(NG):
                    pe.wait_ge(vps_taken, NG * b + g + 1)
                    for k in range(GB):
                        last = pe.matmul(vps[:, g % 2, cols(P, k)], XN[:, cols(P, g * GB + k)], weights[:, 4, :],
                                         start=True, stop=True)
                    last.then_inc(vps_ready, 1)

            def v_image(b):
                for g in range(NG):
                    pe.wait_ge(tr_taken, TR_FIRST + TR_USES * b + g + 1)
                    pe.matmul(tr[:, g % 2, 0:GW], weights[:, 4, :], XN[:, cols(GW, g)],
                              start=True, stop=True).then_inc(tr_ready, 1)

            def project(b, m, groups):
                for g in groups:
                    for r in range(2):
                        n = (m * NG + g) * 2 + r
                        pe.wait_ge(mm_taken, MM_USES * b + n + 1)
                        pe.matmul(mm[:, n % 4, 0:GW], weights[:, 2 * m + r, :], XN[:, cols(GW, g)],
                                  start=True, stop=True).then_inc(mm_ready, 1)

            pe.wait_ge(constants, 5)
            transpose_x(0, 0)
            transpose_angles(0)
            group_means(0)
            transpose_angles(1)
            pe.wait_ge(rotated_w, 1)
            for i in range(6):
                pe.matmul(misc[:, 2 + i:3 + i], rows[0:1, i, :], ones[0:1, 0:1], start=True, stop=True)
            pe.matmul(misc[:, P:2 * P], ones[0:1, :], rows[0:1, 4, :], start=True, stop=True)
            pe.transpose(misc[:, 2 * P:2 * P + TAPS], taps_row[:, :], ident[0:TAPS, 0:TAPS]).then_inc(small_ready, 1)
            pe.wait_ge(small_taken, 3)
            with pe.Fori(0, B - 1) as b:
                v_tokens(b)
                project(b, 0, range(NG))
                v_image(b)
                transpose_x(b + 1, TR_FIRST + TR_USES * b + NG)
                project(b, 1, range(2))
                group_means(b + 1)
                project(b, 1, range(2, NG))
            v_tokens(B - 1)
            project(B - 1, 0, range(NG))
            v_image(B - 1)
            project(B - 1, 1, range(NG))

        @block.vector
        def _(dve):
            NS = 6

            def widen(m):
                for h in range(HEADS):
                    last = dve.tensor_copy(angles8[:, :, h, :], angles[:, m, :, :])
                last.then_inc(angles_wide, 1)

            def statistics(b, n):
                for g in range(NG):
                    dve.wait_ge(tr_taken, n + g + 1 + 2)
                    last = dve.bn_stats(stats[:, g, :], XT[:, cols(GW, g)])
                last.then_inc(norm_step, 1)
                dve.wait_ge(norm_step, NS * b + 1)
                alone(dve)
                dve.bn_aggr(mv[:, :], stats[:, :, :]).then_inc(norm_step, 1)
                dve.wait_ge(norm_step, NS * b + 2)
                dve.tensor_copy(moments[:, 0:1], mv[:, 0:1])
                dve.scalar_tensor_tensor(out=moments[:, 1:2], in0=mv[:, 0:1], scalar=mv[:, 0:1], in1=mv[:, 1:2],
                                         op0=ALU.mult, op1=ALU.add).then_inc(stats_ready, 1)

            def variance(b):
                dve.wait_ge(group_ready, b + 1)
                dve.tensor_copy(group[:, :], misc[:, 0:2]).then_inc(norm_step, 1)
                dve.wait_ge(norm_step, NS * b + 3)
                dve.tensor_tensor(var[:, :], group[:, 0:1], group[:, 0:1], ALU.mult).then_inc(norm_step, 1)
                dve.wait_ge(norm_step, NS * b + 4)
                dve.tensor_tensor(var[:, :], group[:, 1:2], var[:, :], ALU.subtract).then_inc(norm_step, 1)
                dve.wait_ge(norm_step, NS * b + 5)
                dve.tensor_scalar(var[:, :], var[:, :], 0.0, None, ALU.max).then_inc(var_ready, 1)

            def normalise(b, used=None):
                dve.wait_ge(sd_ready, b + 1)
                dve.reciprocal(rstd[:, :], sd[:, :]).then_inc(norm_step, 1)
                dve.wait_ge(norm_step, NS * b + 6)
                if used is not None:
                    dve.wait_ge(mm_ready, used)
                dve.tensor_scalar(XN[:, :], XT[:, :], group[:, 0:1], rstd[:, :], ALU.subtract, ALU.mult).then_inc(xn_ready, 1)

            def take_v(b):
                dve.wait_ge(v_stored, 16 * (b + 1))
                for g in range(NG):
                    dve.wait_ge(vps_ready, NG * b + g + 1)
                    dst = V[:, :, cols(GB, g), :].rearrange("p h t d -> p t h d")
                    src = vps[:, g % 2, 0:GW].rearrange("p (t h d) -> p t h d", t=GB, h=HEADS)
                    bias = bv_all[:, :, :].rearrange("p t (h d) -> p t h d", h=HEADS)
                    dve.tensor_tensor(dst, src, bias, ALU.add).then_inc(vps_taken, 1)

            def rotate(b, m, groups):
                if 0 in groups:
                    dve.wait_ge(p3_ready, 2 * b + m + 1)
                for g in groups:
                    n = (m * NG + g) * 2
                    dve.wait_ge(mm_ready, MM_USES * b + n + 2)
                    dve.scalar_tensor_tensor(out=t1[:, g % 2, :], in0=mm[:, n % 4, 0:GW], scalar=biases[:, 2 * m:2 * m + 1],
                                             in1=cosT[:, cols(GW, g)], op0=ALU.add, op1=ALU.mult).then_inc(mm_taken, 1)
                    dve.scalar_tensor_tensor(out=t2[:, g % 2, :], in0=mm[:, (n + 1) % 4, 0:GW], scalar=biases[:, 2 * m + 1:2 * m + 2],
                                             in1=sinT[:, cols(GW, g)], op0=ALU.add, op1=ALU.mult).then_inc(mm_taken, 1)
                    dve.wait_ge(mm_taken, MM_USES * b + n + 2 + 4)
                    last = dve.tensor_tensor(rot_sum[:, m, cols(GW, g)], t1[:, g % 2, :], t2[:, g % 2, :], ALU.add)
                if NG - 1 in groups:
                    last.then_inc(rot_ready, 1)

            dve.sem_inc(mm_taken, 4)
            dve.sem_inc(vps_taken, 2)
            dve.sem_inc(p3_ready, 2)
            dve.sem_inc(v_stored, 16)
            dve.wait_ge(angles_in, 32)
            widen(0)
            statistics(0, 0)
            dve.wait_ge(tr_ready, 2 * NG)
            widen(1)
            variance(0)
            dve.wait_ge(weights_in, 16 * 8)
            dve.tensor_scalar(weights[:, 2, :], weights[:, 2, :], D ** -0.5, None, ALU.mult).then_inc(scaled_k, 1)
            dve.tensor_scalar(rows[:, 2, :], rows[:, 2, :], D ** -0.5, None, ALU.mult).then_inc(scaled_k, 1)
            dve.wait_ge(scaled_k, 2)
            for of in (weights, rows):
                for src_i in (0, 2):
                    src = of[:, src_i, :].rearrange("p (i two) -> p i two", two=2)
                    dst = of[:, src_i + 1, :].rearrange("p (i two) -> p i two", two=2)
                    dve.tensor_scalar(dst[:, :, 0], src[:, :, 1], -1.0, None, ALU.mult)
                    last = dve.tensor_copy(dst[:, :, 1], src[:, :, 0])
            last.then_inc(rotated_w, 1)
            normalise(0)
            dve.wait_ge(small_ready, 1)
            dve.tensor_copy(conv_bias[:, :], misc[:, 7:8])
            dve.tensor_copy(biases[:, :], misc[:, 2:8]).then_inc(small_taken, 1)
            for k in range(GB):
                last = dve.tensor_copy(bv_all[:, k, :], misc[:, P:2 * P])
            last.then_inc(small_taken, 1)
            dve.tensor_copy(taps[:, :], misc[:, 2 * P:2 * P + TAPS]).then_inc(small_taken, 1)
            dve.wait_ge(small_taken, 3)
            dve.wait_ge(tr_taken, TR_FIRST + 2)
            with dve.Fori(0, B - 1) as b:
                take_v(b)
                rotate(b, 0, range(NG))
                statistics(b + 1, TR_FIRST + TR_USES * b + NG)
                rotate(b, 1, range(2))
                variance(b + 1)
                rotate(b, 1, range(2, NG))
                normalise(b + 1, MM_USES * (b + 1))
            take_v(B - 1)
            rotate(B - 1, 0, range(NG))
            rotate(B - 1, 1, range(NG))
            dve.wait_ge(p3_ready, 2 * (B - 1) + 1 + 2)
            remainders(dve, B - 1, 1)


def layer0_core(nc, a, s, ident, taps, conv_bias, mask):
    with ExitStack() as ctx:
        sb, ps = buffers(nc, ctx, "c")
        sem = sem_maker(nc, ctx, "c")
        K = sb("K", [KR, 2 * B * N], BF16)
        Q = sb("Q", [KR, 2, B, 2 * P], BF16)
        S = sb("S", [P, 4, N])
        part_max = sb("part_max", [P, 4, NCH])
        row_max = sb("row_max", [P, 4])
        PT = sb("PT", [P, 2, TILES, 2 * P])
        V_next = sb("V_next", [P, B * TILES, D])
        V = sb("V", [P, B * TILES, 2 * D])
        O = sb("O", [P, 2, B, 2 * P])
        vpad = sb("vpad", [P, 2 * HALF_IN])
        conv = sb("conv", [P, 2 * PIECE * PIECES])

        Sps = ps("Sps", [P, 2, 2, BANK])
        Tps = ps("Tps", [P, 2, BANK])
        Ops = ps("Ops", [P, B, 2 * P])

        k_in, v_in, q_in, mask_in = sem("k_in"), sem("v_in"), sem("q_in"), sem("mask_in")
        v_ones, v_placed = sem("v_ones"), sem("v_placed")
        s_ready, s_taken = sem("s_ready"), sem("s_taken")
        max_ready, shifted = sem("max_ready"), sem("shifted")
        t_ready, exp_done, pt_used = sem("t_ready"), sem("exp_done"), sem("pt_used")
        o_taken, o_stored = sem("o_taken"), sem("o_stored")
        vpad_in, conv_step, conv_stored = sem("vpad_in"), sem("conv_step"), sem("conv_stored")

        HEAD_PAIRS = TILES // 2
        PAIRS = HEADS * HEAD_PAIRS
        UNITS = 2 * B
        COLS = 4
        STORES = COLS + 1
        S_SLOTS, T_SLOTS, PT_SLOTS, O_SLOTS = 2, 2, 2, 2
        UNIT_SLOTS = 4

        block = ctx.enter_context(nc.Block())

        @block.sync
        def _(sp):
            def load_head(h):
                k = K[:, bass.ds((h % 2) * (B * N), B * N)]
                sp.dma_start(k[0:3 * D, :], s["k_load"][h]).then_inc(k_in, 16)
                sp.dma_start(k[3 * D:5 * D, :], s["k_load"][h][0:2 * D, :]).then_inc(k_in, 16)
                sp.dma_start(k[5 * D:6 * D, :], s["k_load"][h][0:D, :]).then_inc(k_in, 16)
                sp.dma_start(V_next[:, :, :].rearrange("p t d -> p (t d)"), s["v_load"][h]).then_inc(v_in, 16)

            def load_half(h):
                sp.dma_start(vpad[:, bass.ds((h % 2) * HALF_IN, HALF_IN)],
                             s["vpad_load"][h // 2][:, bass.ds((h % 2) * HALF_OUT, HALF_IN)]).then_inc(vpad_in, 16)

            def store_half(h):
                sp.wait_ge(conv_step, TAPS * HEAD_PAIRS * (h + 1))
                alone(sp)
                rows = conv[:, bass.ds((h % 2) * PIECE * PIECES, HALF_OUT)].rearrange("p (h w) -> p h w", w=WP)
                sp.dma_start(s["conv_store"][h // 2][h % 2], rows[:, :, 0:W]).then_inc(conv_stored, 16)

            def columns(ip):
                return bass.ds((ip % HEAD_PAIRS) * (2 * P), 2 * P)

            def load_q(ip):
                source = s["q_load"][ip // HEAD_PAIRS][ip % HEAD_PAIRS]
                for part in range(3):
                    first, count = Q_SLOTS.index(part), Q_SLOTS.count(part)
                    sp.dma_start(Q[first * D:(first + count) * D, bass.ds(ip % 2, 1), :, :].rearrange("r a b q -> r (a b q)"),
                                 source[part].unsqueeze(0).to_broadcast([count, D, B * 2 * P])).then_inc(q_in, 16)

            def load_mask(ip):
                for t in range(2):
                    sp.dma_start(mask[:, bass.ds(2 * (ip % 2) + t, 1), :].rearrange("p a n -> p (a n)"),
                                 s["mask"][2 * ip + t]).then_inc(mask_in, 16)

            def store_pair(ip):
                o = O[:, bass.ds(ip % 2, 1), :, :].rearrange("p a b q -> p (a b) q")
                sp.wait_ge(o_stored, 16 * STORES * (ip + 2))
                sp.wait_ge(o_taken, 2 * (ip + 1) + O_SLOTS)
                h = ip // HEAD_PAIRS
                for j in range(COLS):
                    sp.dma_start(s["o_store"][j][h][:, :, columns(ip)], o[32 * j:32 * j + D]).then_inc(o_stored, 16)
                sp.dma_start(s["den_store"][h][:, :, columns(ip)], o[D:P:32]).then_inc(o_stored, 16)

            def step(ip):
                sp.wait_ge(q_in, 48 * (ip + 2))
                alone(sp)
                sp.wait_ge(mask_in, 32 * (ip + 2))
                alone(sp)
                sp.wait_ge(s_taken, UNITS * NCH * (ip + 1) + S_SLOTS)
                load_q(ip + 2)
                load_mask(ip + 2)
                store_pair(ip)

            sp.sem_inc(mask_in, 32 * 2)
            load_q(0)
            load_head(0)
            sp.wait_ge(q_in, 48)
            load_q(1)
            load_half(0)
            with sp.Fori(0, HEADS - 1) as h:
                step(h * HEAD_PAIRS)
                sp.wait_ge(k_in, 48 * (h + 1))
                alone(sp)
                sp.wait_ge(v_placed, 2 * (h + 1))
                load_head(h + 1)
                sp.wait_ge(conv_step, TAPS * HEAD_PAIRS * h + 1)
                alone(sp)
                sp.wait_ge(vpad_in, 16 * (h + 1))
                alone(sp)
                load_half(h + 1)
                with sp.Fori(1, HEAD_PAIRS) as qp:
                    step(h * HEAD_PAIRS + qp)
                store_half(h)
            with sp.Fori(PAIRS - HEAD_PAIRS, PAIRS - 2) as ip:
                step(ip)
            store_half(HEADS - 1)
            store_pair(PAIRS - 2)
            store_pair(PAIRS - 1)
            sp.wait_ge(conv_stored, 16 * (HEADS + 2))
            sp.wait_ge(o_stored, 16 * STORES * (PAIRS + 2))

        @block.gpsimd
        def _(pool):
            pool.memset(V[:, :, :], 1.0).then_inc(v_ones, 1)
            with pool.Fori(0, PAIRS * UNITS // UNIT_SLOTS) as i:
                for slot in range(UNIT_SLOTS):
                    pool.wait_ge(max_ready, UNIT_SLOTS * i + slot + 1)
                    alone(pool)
                    pool.tensor_scalar(S[:, slot, :], S[:, slot, :], -1.0, row_max[:, slot:slot + 1],
                                       ALU.mult, ALU.add).then_inc(shifted, 1)

        @block.scalar
        def _(act):
            act.sem_inc(exp_done, T_SLOTS)
            act.sem_inc(o_stored, 2 * 16 * STORES)

            def place_v(h, half):
                images = cols(B // 2 * TILES, half)
                act.wait_ge(v_in, 16 * (h + 1))
                act.activation(V[:, images, 0:D], V_next[:, images, :], ACT.Copy).then_inc(v_placed, 1)

            def exp(ip, w):
                b, t = w // 2, w % 2
                if t == 0:
                    act.wait_ge(pt_used, B * ip + b + 1)
                for g in range(NG):
                    act.wait_ge(t_ready, NG * (UNITS * ip + w) + (g + 1 + NG * UNIT_SLOTS))
                    act.activation(PT[:, b % 2, cols(GB, g), cols(P, t)], Tps[:, g % T_SLOTS, 0:GW].rearrange("p (t q) -> p t q", t=GB),
                                   ACT.Exp, scale=-1.0).then_inc(exp_done, 1)

            def take_o(ip, p, half):
                act.wait_ge(pt_used, B * ip + (2 * (half + 1) + PT_SLOTS))
                if half == 0:
                    act.wait_ge(o_stored, 16 * STORES * (ip + 1))
                    alone(act)
                act.activation(O[:, bass.ds(p, 1), cols(2, half), :].rearrange("p a b q -> p (a b) q"), Ops[:, cols(2, half), :],
                               ACT.Copy).then_inc(o_taken, 1)

            def pair(ip, next_head=None, end=False):
                for w in range(LAG, UNITS):
                    exp(ip, w)
                    if w == UNITS // 2 + 2:
                        take_o(ip, ip % 2, 0)
                        if next_head is not None:
                            place_v(next_head, 0)
                if not end:
                    for w in range(LAG):
                        exp(ip + 1, w)
                take_o(ip, ip % 2, 1)
                if next_head is not None:
                    place_v(next_head, 1)

            LAG = 3
            act.wait_ge(v_ones, 1)
            for half in range(2):
                place_v(0, half)
            for w in range(LAG):
                exp(0, w)
            with act.Fori(0, HEADS - 1) as h:
                with act.Fori(0, HEAD_PAIRS - 1) as qp:
                    pair(h * HEAD_PAIRS + qp)
                pair(h * HEAD_PAIRS + (HEAD_PAIRS - 1), next_head=h + 1)
            with act.Fori(0, HEAD_PAIRS - 1) as qp:
                pair((HEADS - 1) * HEAD_PAIRS + qp)
            pair(PAIRS - 1, end=True)

        @block.vector
        def _(dve):
            dve.sem_inc(s_taken, S_SLOTS)
            dve.sem_inc(conv_stored, 2 * 16)

            def conv_tap(ip, tap):
                h, piece = ip // HEAD_PAIRS, ip % HEAD_PAIRS
                if tap == 0:
                    dve.wait_ge(vpad_in, 16 * (h + 1))
                    dve.wait_ge(conv_stored, 16 * (h + 1))
                else:
                    dve.wait_ge(conv_step, TAPS * ip + tap)
                dy, dx = divmod(tap, 5)
                window = vpad[:, bass.ds((h % 2) * HALF_IN + piece * PIECE + (dy * WP + dx), PIECE)]
                dst = conv[:, bass.ds((h % 2) * (PIECE * PIECES) + piece * PIECE, PIECE)]
                if tap == 0:
                    dve.tensor_scalar(dst, window, taps[:, 0:1], conv_bias[:, :], ALU.mult, ALU.add).then_inc(conv_step, 1)
                else:
                    dve.scalar_tensor_tensor(out=dst, in0=window, scalar=taps[:, tap:tap + 1], in1=dst,
                                             op0=ALU.mult, op1=ALU.add).then_inc(conv_step, 1)

            with dve.Fori(0, PAIRS // 2) as i:
                for p in range(2):
                    ip = i * 2 + p
                    dve.wait_ge(mask_in, 32 * (ip + 1))
                    for w in range(UNITS):
                        slot = w % UNIT_SLOTS
                        dve.wait_ge(t_ready, NG * (UNITS * ip + w + 1))
                        for c in range(NCH):
                            n = NCH * w + c
                            dve.wait_ge(s_ready, UNITS * NCH * ip + n + 1)
                            alone(dve)
                            dve.tensor_tensor_reduce(
                                out=S[:, slot, cols(CH, c)].rearrange("p (k n) -> p k n", k=2),
                                in0=Sps[:, n % S_SLOTS, :, 0:GW],
                                in1=mask[:, 2 * p + w % 2, cols(CH, c)].rearrange("p (k n) -> p k n", k=2),
                                scale=1.0, scalar=LOWEST, op0=ALU.add, op1=ALU.max,
                                accum_out=part_max[:, slot, c:c + 1]).then_inc(s_taken, 1)
                            if c < NCH - 1:
                                conv_tap(ip, n)
                        dve.wait_ge(s_taken, UNITS * NCH * ip + n + 1 + S_SLOTS)
                        dve.tensor_reduce(row_max[:, slot:slot + 1], part_max[:, slot, :], AX.X, ALU.max).then_inc(max_ready, 1)
                        conv_tap(ip, n)
                    conv_tap(ip, TAPS - 1)

        @block.tensor
        def _(pe):
            pe.sem_inc(t_ready, NG * UNIT_SLOTS)
            pe.sem_inc(pt_used, PT_SLOTS)
            pe.sem_inc(o_taken, O_SLOTS)

            def scores(ip, p, w, c):
                if w == 0 and c == 0:
                    pe.wait_ge(q_in, 48 * (ip + 1))
                    pe.wait_ge(k_in, 48 * (ip // HEAD_PAIRS + 1))
                n = NCH * w + c
                pe.wait_ge(s_taken, UNITS * NCH * ip + n + 1)
                for k in range(2):
                    start = ((ip // HEAD_PAIRS) % 2) * (B * N) + ((w // 2) * N + c * CH + k * GW)
                    last = pe.matmul(Sps[:, n % S_SLOTS, k, 0:GW], Q[:, p, w // 2, cols(P, w % 2)], K[:, bass.ds(start, GW)],
                                     start=True, stop=True)
                last.then_inc(s_ready, 1)

            def transposes(ip, w, g):
                if g == 0:
                    pe.wait_ge(shifted, UNITS * ip + w + 1)
                pe.wait_ge(exp_done, NG * (UNITS * ip + w) + g + 1)
                for k in range(GB):
                    last = pe.transpose(Tps[:, g % T_SLOTS, cols(P, k)], S[:, w % UNIT_SLOTS, cols(P, g * GB + k)], ident[:, :])
                last.then_inc(t_ready, 1)

            def values(ip, b, part):
                first, end = GB * part, GB * (part + 1)
                if part == 0:
                    pe.wait_ge(o_taken, 2 * ip + b // 2 + 1)
                    pe.wait_ge(v_placed, 2 * (ip // HEAD_PAIRS) + b // 2 + 1)
                pe.wait_ge(exp_done, NG * (UNITS * ip + 2 * b + 1) + (part + 1 + T_SLOTS))
                for kt in range(first, end):
                    j = kt % COLS
                    last = pe.matmul(Ops[32 * j:32 * (j + 1), b, :], V[:, b * TILES + kt, :], PT[:, b % 2, kt, :],
                                     start=kt < COLS, stop=kt >= TILES - COLS)
                if end == TILES:
                    last.then_inc(pt_used, 1)

            def pair(ip, p, start=False, end=False):
                for w in range(UNITS):
                    for c in range(NCH):
                        transposes(ip, w, 2 * c)
                        if w + 2 < UNITS:
                            scores(ip, p, w + 2, c)
                        elif not end:
                            scores(ip + 1, 1 - p, w + 2 - UNITS, c)
                        transposes(ip, w, 2 * c + 1)
                        part = NCH * (w % 2) + c
                        if w > 1:
                            values(ip, w // 2 - 1, part)
                        elif not start:
                            values(ip - 1, B - 1, part)

            for w in range(2):
                for c in range(NCH):
                    scores(0, 0, w, c)
            pair(0, 0, start=True)
            pair(1, 1)
            with pe.Fori(1, PAIRS // 2 - 1) as i:
                for p in range(2):
                    pair(i * 2 + p, p)
            pair(PAIRS - 2, 0)
            pair(PAIRS - 1, 1, end=True)
            for part in range(2 * NCH):
                values(PAIRS - 1, B - 1, part)


def layer1_attention(nc, a, s, ident, x1, moments):
    with ExitStack() as ctx:
        sb, ps = buffers(nc, ctx, "l")
        sem = sem_maker(nc, ctx, "l")
        SEG = N // D
        HN = N // 2
        num = sb("num", [P, 4, HN])
        den = sb("den", [P, 4, SEG])
        den_sum = sb("den_sum", [P, SEG])
        z = sb("z", [P, N])
        conv = sb("conv", [P, N])
        xin = sb("xin", [P, TILES, C])
        ln = sb("ln", [P, TILES, C])
        lnT = sb("lnT", [P, N])
        qT = sb("qT", [P, 2 * N])
        kT = sb("kT", [P, 2 * N])
        v = sb("v", [P, 2 * TILES, C])
        q_tile = sb("q_tile", [P, 2, P])
        S = sb("S", [P, 2, N])
        PT = sb("PT", [P, TILES, P])
        weights = sb("weights", [P, 4, C])
        rows = sb("rows", [1, 4, C])
        biases = sb("biases", [P, 2])
        bo_all = sb("bo_all", [P, GB, C])
        bv_all = sb("bv_all", [P, GB, C])
        ones = sb("ones", [1, P])
        eps = sb("eps", [P, 1])
        stats = sb("stats", [P, TILES, 6])
        mv = sb("mv", [P, TILES, 2])
        sd = sb("sd", [P, TILES])
        rstd = sb("rstd", [P, TILES])
        part_max = sb("part_max", [P, 2, NG])
        neg_max = sb("neg_max", [P, 2])
        total = sb("total", [P, 2])
        inv_total = sb("inv_total", [P, 2])
        row_stats = sb("row_stats", [P, 6])
        row_moments = sb("row_moments", [P, 2])

        Sps = ps("Sps", [P, 3, BANK])
        Tps = ps("Tps", [P, 3, BANK])
        Ops = ps("Ops", [P, 2, BANK])

        weights_in, constants, small_ready, small_taken = sem("weights_in"), sem("constants"), sem("small_ready"), sem("small_taken")
        den_in, half_in, conv_in, x_in = sem("den_in"), sem("half_in"), sem("conv_in"), sem("x_in")
        inv_stored, inv_in = sem("inv_stored"), sem("inv_in")
        den_step, inv_ready, sum_step, half_taken, z_ready = sem("den_step"), sem("inv_ready"), sem("sum_step"), sem("half_taken"), sem("z_ready")
        x_biased = sem("x_biased")
        ln_step, var_ready, sd_ready, ln_ready = sem("ln_step"), sem("var_ready"), sem("sd_ready"), sem("ln_ready")
        t_ready, t_taken, o_ready, o_taken = sem("t_ready"), sem("t_taken"), sem("o_ready"), sem("o_taken")
        q_staged, s_ready, s_taken = sem("q_staged"), sem("s_ready"), sem("s_taken")
        max_ready, p_ready, inv_step, row_step = sem("max_ready"), sem("p_ready"), sem("inv_step"), sem("row_step")

        S_SLOTS = T_SLOTS = 3
        O_SLOTS = 2
        S_USES = NG * TILES
        PROJECT, TRANSPOSE, TO_Q, TO_K, TO_V = 8, 11, 12, 13, 14
        T_PREP, O_PREP = 3 * NG, 2 * NG

        def t_at(b, qt, last=False, after=True):
            prep = 0 if last else sum(qt >= x if after else qt > x for x in (TRANSPOSE, TO_Q, TO_K))
            return T_PREP + (T_PREP + NG * TILES) * b + NG * (qt + prep)

        def o_at(b, qt, last=False, after=True):
            prep = 0 if last else sum(qt >= x if after else qt > x for x in (PROJECT, TO_V))
            return O_PREP + (O_PREP + TILES) * b + qt + NG * prep

        block = ctx.enter_context(nc.Block())

        @block.sync
        def _(sp):
            def load_half(i, half):
                sp.dma_start(num[:, :, :], s["o_load"][i][:, :, half * HN:(half + 1) * HN]).then_inc(half_in, 16)

            def load_x(i):
                for half in range(2):
                    sp.dma_start(xin[:, cols(HT, half), :], s["x_tiles"][i][:, cols(HT, half), :]).then_inc(x_in, 16)

            def spread_inverses(i):
                sp.wait_ge(inv_ready, i + 1)
                alone(sp)
                sp.dma_start(s["inv_store"][i], den_sum[:, :]).then_inc(inv_stored, 16)
                sp.wait_ge(inv_stored, 16 * (i + 1))
                alone(sp)
                sp.dma_start(z[:, :], s["inv_load"][i].unsqueeze(1).to_broadcast([HEADS, D, N])).then_inc(inv_in, 16)

            sp.dma_start(den[:, :, :], s["den_load"][0]).then_inc(den_in, 16)
            for i, w in enumerate(("Wo0", "Wq1", "Wk1", "Wv1")):
                sp.dma_start(weights[:, i, :], a[w]).then_inc(weights_in, 16)
            for i, w in enumerate(("bo0", "bq1", "bk1", "bv1")):
                sp.dma_start(rows[:, i, :], a[w].rearrange("(a n) -> a n", a=1)).then_inc(weights_in, 16)
            load_half(0, 0)
            spread_inverses(0)
            sp.dma_start(conv[:, :], s["conv"][0]).then_inc(conv_in, 16)
            sp.wait_ge(half_taken, 1)
            load_half(0, 1)
            load_x(0)
            with sp.Fori(1, B) as i:
                sp.wait_ge(z_ready, i)
                alone(sp)
                sp.dma_start(den[:, :, :], s["den_load"][i]).then_inc(den_in, 16)
                load_half(i, 0)
                sp.dma_start(conv[:, :], s["conv"][i]).then_inc(conv_in, 16)
                sp.wait_ge(var_ready, i)
                alone(sp)
                load_x(i)
                spread_inverses(i)
                sp.wait_ge(half_taken, 2 * i + 1)
                alone(sp)
                load_half(i, 1)

        @block.gpsimd
        def _(pool):
            pool.memset(ones[:, :], 1.0).then_inc(constants, 1)
            pool.memset(eps[:, :], 1e-5).then_inc(constants, 1)
            pool.wait_ge(small_taken, 3)
            with pool.Fori(0, B) as b:
                pool.wait_ge(x_in, 32 * (b + 1))
                for g in range(NG):
                    last = pool.tensor_tensor(xin[:, cols(GB, g), :], xin[:, cols(GB, g), :], bo_all[:, :, :], ALU.add)
                last.then_inc(x_biased, 1)

        @block.scalar
        def _(act):
            def deviations(i):
                act.wait_ge(var_ready, i + 1)
                act.activation(sd[:, :], mv[:, :, 1:2].rearrange("p t a -> p (t a)"), ACT.Sqrt, bias=eps[:, :]).then_inc(sd_ready, 1)

            def take_transposes(n):
                for g in range(NG):
                    act.wait_ge(t_ready, n + g + 1)
                    act.activation(lnT[:, cols(GW, g)], Tps[:, g % T_SLOTS, 0:GW], ACT.Copy).then_inc(t_taken, 1)

            def take_projection(n, i, m):
                for g in range(NG):
                    act.wait_ge(t_ready, n + g + 1)
                    alone(act)
                    act.activation((qT, kT)[m][:, bass.ds((i % 2) * N + g * GW, GW)], Tps[:, g % T_SLOTS, 0:GW], ACT.Identity,
                                   bias=biases[:, m:m + 1]).then_inc(t_taken, 1)

            def tile(b, qt, t, last=False, prepare=()):
                act.wait_ge(max_ready, TILES * b + qt + 1)
                act.activation(S[:, t, :], S[:, t, :], ACT.Exp, bias=neg_max[:, t:t + 1],
                               accum_out=total[:, t:t + 1]).then_inc(p_ready, 1)
                for step in prepare:
                    step()
                for g in range(NG):
                    if g == 0:
                        act.wait_ge(o_ready, o_at(b, qt, last))
                    act.wait_ge(t_ready, t_at(b, qt, last) + g + 1)
                    act.activation(PT[:, cols(GB, g), :], Tps[:, g % T_SLOTS, 0:GW].rearrange("p (t q) -> p t q", t=GB),
                                   ACT.Copy).then_inc(t_taken, 1)

            act.sem_inc(t_taken, T_SLOTS)
            act.wait_ge(small_taken, 3)
            deviations(0)
            take_transposes(0)
            take_projection(NG, 0, 0)
            take_projection(2 * NG, 0, 1)
            with act.Fori(0, B - 1) as b:
                prepare = {
                    TRANSPOSE - 1: [lambda: deviations(b + 1)],
                    TRANSPOSE: [lambda: take_transposes(t_at(b, TRANSPOSE, after=False))],
                    TO_Q: [lambda: take_projection(t_at(b, TO_Q, after=False), b + 1, 0)],
                    TO_K: [lambda: take_projection(t_at(b, TO_K, after=False), b + 1, 1)],
                }
                for qt in range(TILES):
                    tile(b, qt, qt % 2, prepare=prepare.get(qt, ()))
            with act.Fori(0, TILES // 2) as qp:
                for t in range(2):
                    tile(B - 1, 2 * qp + t, t, last=True)

        @block.tensor
        def _(pe):
            pe.wait_ge(weights_in, 16 * 8)
            pe.wait_ge(constants, 2)
            for i in range(2):
                pe.matmul(Tps[:, 0, i:i + 1], rows[0:1, 1 + i, :], ones[0:1, 0:1], start=True, stop=True)
            pe.matmul(Tps[:, 1, 0:C], ones[0:1, :], rows[0:1, 0, :], start=True, stop=True)
            pe.matmul(Tps[:, 1, C:2 * C], ones[0:1, :], rows[0:1, 3, :], start=True, stop=True).then_inc(small_ready, 1)
            pe.wait_ge(small_taken, 3)

            def project(i, n):
                pe.wait_ge(z_ready, i + 1)
                for g in range(NG):
                    pe.wait_ge(o_taken, n + g + 1)
                    for k in range(GB):
                        last = pe.matmul(Ops[:, g % 2, cols(P, k)], z[:, cols(P, g * GB + k)], weights[:, 0, :],
                                         start=True, stop=True)
                    last.then_inc(o_ready, 1)

            def transpose_ln(i, n):
                for g in range(NG):
                    pe.wait_ge(ln_ready, NG * i + g + 1)
                    pe.wait_ge(t_taken, n + g + 1)
                    for k in range(GB):
                        last = pe.transpose(Tps[:, g % T_SLOTS, cols(P, k)], ln[:, g * GB + k, :], ident[:, :])
                    last.then_inc(t_ready, 1)

            def to_q_or_k(m, n, first=False):
                if first:
                    pe.wait_ge(t_taken, n + T_SLOTS)
                for g in range(NG):
                    pe.wait_ge(t_taken, n + g + 1)
                    pe.matmul(Tps[:, g % T_SLOTS, 0:GW], weights[:, 1 + m, :], lnT[:, cols(GW, g)],
                              start=True, stop=True).then_inc(t_ready, 1)

            def to_v(n):
                for g in range(NG):
                    pe.wait_ge(o_taken, n + g + 1)
                    for k in range(GB):
                        last = pe.matmul(Ops[:, g % 2, cols(P, k)], lnT[:, cols(P, g * GB + k)], weights[:, 3, :],
                                         start=True, stop=True)
                    last.then_inc(o_ready, 1)

            def scores(b, qt, t):
                pe.wait_ge(q_staged, TILES * b + qt + 1)
                for g in range(NG):
                    pe.wait_ge(s_taken, S_USES * b + NG * qt + g + 1)
                    pe.matmul(Sps[:, g % S_SLOTS, 0:GW], q_tile[:, t, :], kT[:, bass.ds((b % 2) * N + g * GW, GW)],
                              start=True, stop=True).then_inc(s_ready, 1)

            def attend(b, qt, t, last=False):
                n = t_at(b, qt, last)

                def values(g):
                    if g == 0:
                        pe.wait_ge(o_taken, o_at(b, qt, last) + 1)
                    pe.wait_ge(t_taken, n + g + 1 + T_SLOTS)
                    for kt in range(g * GB, (g + 1) * GB):
                        product = pe.matmul(Ops[:, t, 0:C], PT[:, kt, :], v[:, bass.ds((b % 2) * TILES + kt, 1), :].rearrange("p t c -> p (t c)"),
                                            start=kt == 0, stop=kt == TILES - 1)
                    if g == NG - 1:
                        product.then_inc(o_ready, 1)

                pe.wait_ge(p_ready, TILES * b + qt + 1)
                for g in range(NG):
                    pe.wait_ge(t_taken, n + g + 1)
                    for k in range(GB):
                        block_t = pe.transpose(Tps[:, g % T_SLOTS, cols(P, k)], S[:, t, cols(P, g * GB + k)], ident[:, :])
                    block_t.then_inc(t_ready, 1)
                    if g > 1:
                        values(g - 2)
                values(NG - 2)
                values(NG - 1)

            def projected(t_after, o_after):
                pe.wait_ge(t_taken, t_after + T_SLOTS)
                pe.wait_ge(o_taken, o_after + O_SLOTS)

            project(0, 0)
            transpose_ln(0, 0)
            to_q_or_k(0, NG, first=True)
            to_q_or_k(1, 2 * NG)
            to_v(NG)
            projected(T_PREP, O_PREP)
            scores(0, 0, 0)
            with pe.Fori(0, B - 1) as b:
                prepare = {
                    PROJECT: lambda: project(b + 1, o_at(b, PROJECT, after=False)),
                    TRANSPOSE: lambda: transpose_ln(b + 1, t_at(b, TRANSPOSE, after=False)),
                    TO_Q: lambda: to_q_or_k(0, t_at(b, TO_Q, after=False), first=True),
                    TO_K: lambda: to_q_or_k(1, t_at(b, TO_K, after=False)),
                    TO_V: lambda: to_v(o_at(b, TO_V, after=False)),
                }
                for qt in range(TILES):
                    if qt in prepare:
                        prepare[qt]()
                    if qt + 1 < TILES:
                        scores(b, qt + 1, (qt + 1) % 2)
                    else:
                        projected(t_at(b, TO_K), o_at(b, TO_V))
                        scores(b + 1, 0, 0)
                    attend(b, qt, qt % 2)
            with pe.Fori(0, TILES // 2 - 1) as qp:
                for t in range(2):
                    scores(B - 1, 2 * qp + t + 1, 1 - t)
                    attend(B - 1, 2 * qp + t, t, last=True)
            scores(B - 1, TILES - 1, 1)
            attend(B - 1, TILES - 2, 0, last=True)
            attend(B - 1, TILES - 1, 1, last=True)

        @block.vector
        def _(dve):
            def image(i, lo, hi):
                return x1[:, bass.ds(i * TILES + lo, hi - lo), :]

            def row(i, t):
                return x1[:, bass.ds(i * TILES + t, 1), :].rearrange("p t c -> p (t c)")

            def invert(i):
                dve.wait_ge(den_in, 16 * (i + 1))
                for x in (0, 2):
                    last = dve.tensor_tensor(den[:, x, :], den[:, x, :], den[:, x + 1, :], ALU.add)
                last.then_inc(den_step, 1)
                dve.wait_ge(den_step, 2 * i + 1)
                dve.tensor_tensor(den_sum[:, :], den[:, 0, :], den[:, 2, :], ALU.add).then_inc(den_step, 1)
                dve.wait_ge(den_step, 2 * i + 2)
                dve.reciprocal(den_sum[:, :], den_sum[:, :]).then_inc(inv_ready, 1)

            def sum_half(i, half):
                dve.wait_ge(half_in, 16 * (2 * i + half + 1))
                for x in (0, 2):
                    last = dve.tensor_tensor(num[:, x, :], num[:, x, :], num[:, x + 1, :], ALU.add)
                last.then_inc(sum_step, 1)
                dve.wait_ge(sum_step, 4 * i + 2 * half + 1)
                dve.tensor_tensor(num[:, 0, :], num[:, 0, :], num[:, 2, :], ALU.add).then_inc(sum_step, 1)

            def finish_half(i, half):
                part = slice(half * HN, (half + 1) * HN)
                dve.wait_ge(sum_step, 4 * i + 2 * half + 2)
                if half == 0:
                    dve.wait_ge(inv_in, 16 * (i + 1))
                dve.tensor_tensor(z[:, part], num[:, 0, :], z[:, part], ALU.mult).then_inc(half_taken, 1)
                dve.wait_ge(half_taken, 2 * i + half + 1)
                if half == 0:
                    dve.wait_ge(conv_in, 16 * (i + 1))
                last = dve.tensor_tensor(z[:, part], z[:, part], conv[:, part], ALU.add)
                if half == 1:
                    last.then_inc(z_ready, 1)

            def take_projected(i, n):
                dve.wait_ge(x_biased, i + 1)
                for g in range(NG):
                    dve.wait_ge(o_ready, n + g + 1)
                    alone(dve)
                    dve.tensor_tensor(image(i, g * GB, (g + 1) * GB), Ops[:, g % 2, 0:GW].rearrange("p (t c) -> p t c", t=GB),
                                      xin[:, cols(GB, g), :], ALU.add).then_inc(o_taken, 1)

            def statistics(i, n):
                dve.wait_ge(o_taken, n + NG + O_SLOTS)
                alone(dve)
                for t in range(TILES):
                    last = dve.bn_stats(stats[:, t, :], row(i, t))
                last.then_inc(ln_step, 1)

            def variances(i):
                dve.wait_ge(ln_step, 2 * i + 1)
                alone(dve)
                for t in range(TILES):
                    last = dve.bn_aggr(mv[:, t, :], stats[:, t, :])
                last.then_inc(var_ready, 1)

            def normalise(i):
                dve.wait_ge(sd_ready, i + 1)
                dve.reciprocal(rstd[:, :], sd[:, :]).then_inc(ln_step, 1)
                dve.wait_ge(ln_step, 2 * i + 2)
                alone(dve)
                for g in range(NG):
                    for t in tiles_of(g):
                        last = dve.tensor_scalar(ln[:, t, :], row(i, t), mv[:, t, 0:1], rstd[:, t:t + 1], ALU.subtract, ALU.mult)
                    last.then_inc(ln_ready, 1)

            def take_v(i, n):
                for g in range(NG):
                    dve.wait_ge(o_ready, n + g + 1)
                    alone(dve)
                    dve.tensor_tensor(v[:, bass.ds((i % 2) * TILES + g * GB, GB), :], Ops[:, g % 2, 0:GW].rearrange("p (t c) -> p t c", t=GB),
                                      bv_all[:, :, :], ALU.add).then_inc(o_taken, 1)

            def stage(b, qt, t):
                dve.tensor_copy(q_tile[:, t, :], qT[:, bass.ds((b % 2) * N + qt * P, P)]).then_inc(q_staged, 1)

            def take_scores(b, qt, t, free):
                for g in range(NG):
                    if g == 0 and free is not None:
                        dve.wait_ge(t_ready, free)
                    dve.wait_ge(s_ready, S_USES * b + NG * qt + g + 1)
                    dve.tensor_scalar(S[:, t, cols(GW, g)], Sps[:, g % S_SLOTS, 0:GW],
                                      1.0, None, ALU.mult, ALU.max, accum_out=part_max[:, t, g:g + 1]).then_inc(s_taken, 1)
                dve.wait_ge(s_taken, S_USES * b + NG * (qt + 1) + S_SLOTS)
                dve.tensor_reduce(neg_max[:, t:t + 1], part_max[:, t, :], AX.X, ALU.max, negate=True).then_inc(max_ready, 1)

            def invert_total(b, qt, t):
                dve.wait_ge(p_ready, TILES * b + qt + 1)
                dve.reciprocal(inv_total[:, t:t + 1], total[:, t:t + 1]).then_inc(inv_step, 1)

            def take_values(b, qt, t, last=False):
                dve.wait_ge(inv_step, TILES * b + qt + 1)
                dve.wait_ge(o_ready, o_at(b, qt, last) + 1)
                alone(dve)
                dve.scalar_tensor_tensor(out=row(b, qt), in0=Ops[:, t, 0:C], scalar=inv_total[:, t:t + 1], in1=row(b, qt),
                                         op0=ALU.mult, op1=ALU.add).then_inc(o_taken, 1)
                dve.wait_ge(o_taken, o_at(b, qt, last) + 1 + O_SLOTS)
                alone(dve)
                dve.bn_stats(row_stats[:, :], row(b, qt)).then_inc(row_step, 1)
                dve.wait_ge(row_step, 2 * (TILES * b + qt) + 1)
                alone(dve)
                dve.bn_aggr(row_moments[:, :], row_stats[:, :]).then_inc(row_step, 1)
                dve.wait_ge(row_step, 2 * (TILES * b + qt) + 2)
                alone(dve)
                dve.tensor_copy(moments[:, bass.ds(b * TILES + qt, 1), :].rearrange("p t c -> p (t c)"), row_moments[:, :])

            dve.sem_inc(o_taken, O_SLOTS)
            dve.sem_inc(s_taken, S_SLOTS)
            invert(0)
            sum_half(0, 0)
            dve.wait_ge(small_ready, 1)
            dve.tensor_copy(biases[:, :], Tps[:, 0, 0:2]).then_inc(small_taken, 1)
            for dst, src in ((bo_all, Tps[:, 1, 0:C]), (bv_all, Tps[:, 1, C:2 * C])):
                for k in range(GB):
                    last = dve.tensor_copy(dst[:, k, :], src)
                last.then_inc(small_taken, 1)
            dve.wait_ge(small_taken, 3)
            finish_half(0, 0)
            sum_half(0, 1)
            finish_half(0, 1)
            take_projected(0, 0)
            statistics(0, 0)
            variances(0)
            normalise(0)
            take_v(0, NG)
            dve.wait_ge(t_taken, T_PREP + T_SLOTS)
            stage(0, 0, 0)
            stage(0, 1, 1)
            take_scores(0, 0, 0, None)
            with dve.Fori(0, B - 1) as b:
                before = {
                    PROJECT: lambda: take_projected(b + 1, o_at(b, PROJECT, after=False)),
                    TO_V: lambda: take_v(b + 1, o_at(b, TO_V, after=False)),
                }
                behind = {
                    0: lambda: invert(b + 1),
                    1: lambda: sum_half(b + 1, 0),
                    3: lambda: finish_half(b + 1, 0),
                    5: lambda: sum_half(b + 1, 1),
                    6: lambda: finish_half(b + 1, 1),
                    8: lambda: statistics(b + 1, o_at(b, PROJECT, after=False)),
                    9: lambda: variances(b + 1),
                    10: lambda: normalise(b + 1),
                }
                for qt in range(TILES):
                    t = qt % 2
                    if qt in before:
                        take_values(b, qt - 1, 1 - t)
                        before[qt]()
                    if qt + 1 < TILES:
                        take_scores(b, qt + 1, 1 - t, t_at(b, qt))
                    else:
                        take_scores(b + 1, 0, 0, t_at(b, qt))
                    if qt + 2 < TILES:
                        stage(b, qt + 2, t)
                    else:
                        if qt + 2 == TILES:
                            dve.wait_ge(t_taken, t_at(b, TO_K, after=False) + T_SLOTS)
                            alone(dve)
                        stage(b + 1, qt + 2 - TILES, t)
                    invert_total(b, qt, t)
                    if qt in behind:
                        behind[qt]()
                    if qt and qt not in before:
                        take_values(b, qt - 1, 1 - t)
                take_values(b, TILES - 1, 1)

            def last_tile(qt, t, ahead=2, values=True):
                if ahead:
                    take_scores(B - 1, qt + 1, 1 - t, t_at(B - 1, qt, True))
                if ahead > 1:
                    stage(B - 1, qt + 2, t)
                invert_total(B - 1, qt, t)
                if values:
                    take_values(B - 1, qt - 1, 1 - t, last=True)

            last_tile(0, 0, values=False)
            with dve.Fori(0, TILES // 2 - 2) as qp:
                last_tile(2 * qp + 1, 1)
                last_tile(2 * qp + 2, 0)
            last_tile(TILES - 3, 1)
            last_tile(TILES - 2, 0, ahead=1)
            last_tile(TILES - 1, 1, ahead=0)
            take_values(B - 1, TILES - 1, 1, last=True)


def layer1_ffn(nc, a, s, ident, x1, moments, out):
    with ExitStack() as ctx:
        sb, ps = buffers(nc, ctx, "e")
        sem = sem_maker(nc, ctx, "e")
        PICKS = 2 * TOPK + 1
        ln = sb("ln", [P, B * TILES, C])
        lnT = sb("lnT", [P, B, N])
        W1 = sb("W1", [P, E, FF])
        W2 = sb("W2", [P, E, FH * C])
        b1_rows = sb("b1_rows", [E * FH, P])
        b1 = sb("b1", [P, E, FH])
        b2 = sb("b2", [P, E, C])
        Wr = sb("Wr", [P, E])
        br = sb("br", [1, E])
        vectors = sb("vectors", [1, 2, C])
        gamma = sb("gamma", [P, 1, C])
        beta = sb("beta", [P, 1, C])
        ones = sb("ones", [P, P])
        eps = sb("eps", [P, 1])
        sd = sb("sd", [P, B * TILES])
        rstd = sb("rstd", [P, B * TILES])
        sums = sb("sums", [P, B, NG])
        means = sb("means", [P, B])
        r = sb("r", [B, 16, E])
        rc = sb("rc", [B, 16])
        greater = sb("greater", [B, E, 2 * E])
        choice = sb("choice", [B, PICKS, E])
        pick = sb("pick", [B, B, P])
        sel = sb("sel", [P, B, PICKS * E])
        w1s = sb("w1s", [P, 2, TOPK, FF])
        w2s = sb("w2s", [P, 2, TOPK, FH * C])
        b1s = sb("b1s", [P, 2, TOPK, FH])
        b2s = sb("b2s", [P, 2, C])
        hid = sb("hid", [P, 2, TOPK * FH, GW])
        ystats = sb("ystats", [P, TILES, 6])
        ymv = sb("ymv", [P, TILES, 2])
        ysd = sb("ysd", [P, TILES])
        yrstd = sb("yrstd", [P, TILES])

        Hps = ps("Hps", [P, 4, BANK])
        Yps = ps("Yps", [P, 2, BANK])
        Rps = ps("Rps", [P, 2, BANK])

        weights_in, small_in, constants, small_ready, small_taken = sem("weights_in"), sem("small_in"), sem("constants"), sem("small_ready"), sem("small_taken")
        sd_ready, rstd_ready, ln_ready = sem("sd_ready"), sem("rstd_ready"), sem("ln_ready")
        t_ready, t_taken = sem("t_ready"), sem("t_taken")
        route_pe, route_act, route_dve = sem("route_pe"), sem("route_act"), sem("route_dve")
        select_step, selected_1, selected_2 = sem("select_step"), sem("selected_1"), sem("selected_2")
        h_ready, h_taken, y_ready, y_taken = sem("h_ready"), sem("h_taken"), sem("y_ready"), sem("y_taken")
        base_ready, y_step, yvar_ready, ysd_ready = sem("base_ready"), sem("y_step"), sem("yvar_ready"), sem("ysd_ready")
        y_normed, res_ready, scaled, out_ready, out_stored = sem("y_normed"), sem("res_ready"), sem("scaled"), sem("out_ready"), sem("out_stored")
        mean_step, sel_ready = sem("mean_step"), sem("sel_ready")
        last_scaled, last_out_ready = sem("last_scaled"), sem("last_out_ready")
        ROUTE_STEPS = 22
        T_SLOTS = 2
        HK = TOPK * FH

        def tokens(of, b, half):
            return of[:, bass.ds(b * TILES + half * HT, HT), :]

        def everywhere(vector):
            return vector.to_broadcast([P, HT, C])

        block = ctx.enter_context(nc.Block())

        @block.sync
        def _(sp):
            sp.dma_start(vectors[:, 0, :], a["gamma"].rearrange("(a n) -> a n", a=1)).then_inc(small_in, 16)
            sp.dma_start(vectors[:, 1, :], a["beta"].rearrange("(a n) -> a n", a=1)).then_inc(small_in, 16)
            sp.dma_start(b1_rows[:, :], a["b1"].rearrange("e (h p) -> (e h) p", p=P)).then_inc(small_in, 16)
            sp.dma_start(Wr[:, :], a["Wr"]).then_inc(small_in, 16)
            sp.dma_start(br[:, :], a["br"].rearrange("(a n) -> a n", a=1)).then_inc(small_in, 16)
            sp.dma_start(W1[:, :, :], a["W1"].rearrange("e p f -> p e f")).then_inc(weights_in, 16)
            sp.dma_start(W2[:, :, :].rearrange("p e (h d) -> p e h d", h=FH), a["W2"].rearrange("e (h p) d -> p e h d", p=P)).then_inc(weights_in, 16)
            sp.dma_start(b2[:, :, :], a["b2"].unsqueeze(0).to_broadcast([P, E, C])).then_inc(weights_in, 16)
            def store(b, half):
                sp.dma_start(out[b][:, cols(HT, half), :], ln[:, bass.ds(b * TILES + half * HT, HT), :]).then_inc(out_stored, 16)

            with sp.Fori(0, B - 1) as b:
                for half in range(2):
                    sp.wait_ge(out_ready, 2 * b + half + 1)
                    alone(sp)
                    store(b, half)
            sp.wait_ge(out_ready, 2 * B - 1)
            store(B - 1, 0)
            sp.wait_ge(last_out_ready, 1)
            store(B - 1, 1)
            sp.wait_ge(out_stored, 32 * B)

        @block.gpsimd
        def _(pool):
            pool.memset(ones[:, :], 1.0).then_inc(constants, 1)
            pool.memset(eps[:, :], 1e-5).then_inc(constants, 1)
            pool.memset(greater[:, :, :], 0.0).then_inc(constants, 1)
            pool.wait_ge(small_taken, 3)
            pool.wait_ge(ln_ready, NG * B)
            with pool.Fori(0, B) as b:
                for half in range(2):
                    last = pool.tensor_tensor(tokens(x1, b, half), tokens(x1, b, half), everywhere(beta[:, :, :]), ALU.add)
                last.then_inc(res_ready, 1)

            def base(b, t):
                pool.wait_ge(selected_2, b + 1)
                alone(pool)
                for half in range(2):
                    last = pool.tensor_tensor(tokens(ln, b, half), tokens(ln, b, half), everywhere(b2s[:, t:t + 1, :]), ALU.add)
                last.then_inc(base_ready, 1)

            def result(b, halves=2):
                for half in range(halves):
                    pool.wait_ge(y_normed, 2 * b + half + 1)
                    alone(pool)
                    pool.tensor_tensor(tokens(ln, b, half), tokens(ln, b, half), everywhere(gamma[:, :, :]), ALU.mult).then_inc(scaled, 1)
                    pool.wait_ge(res_ready, B)
                    pool.wait_ge(scaled, 2 * b + half + 1)
                    alone(pool)
                    pool.tensor_tensor(tokens(ln, b, half), tokens(ln, b, half), tokens(x1, b, half), ALU.add).then_inc(out_ready, 1)

            base(0, 0)
            with pool.Fori(0, B // 2 - 1) as bp:
                for t in range(2):
                    base(2 * bp + t + 1, 1 - t)
                    result(2 * bp + t)
            base(B - 1, 1)
            result(B - 2)
            result(B - 1, halves=1)

        @block.scalar
        def _(act):
            act.sem_inc(t_taken, T_SLOTS)
            act.sem_inc(h_taken, 4)
            act.wait_ge(constants, 3)
            act.activation(sd[:, :], moments[:, :, 1:2].rearrange("p t a -> p (t a)"), ACT.Sqrt, bias=eps[:, :]).then_inc(sd_ready, 1)
            with act.Fori(0, B) as b:
                for g in range(NG):
                    act.wait_ge(t_ready, NG * b + g + 1)
                    alone(act)
                    act.activation(lnT[:, bass.ds(b, 1), cols(GW, g)].rearrange("p a n -> p (a n)"), Rps[:, g % 2, 0:GW], ACT.Copy,
                                   accum_out=sums[:, bass.ds(b, 1), g:g + 1].rearrange("p a n -> p (a n)")).then_inc(t_taken, 1)
            act.wait_ge(route_dve, 2)
            act.activation(r[:, 1, :], r[:, 0, :], ACT.Exp, bias=rc[:, 0:1], accum_out=rc[:, 1:2]).then_inc(route_act, 1)
            act.wait_ge(route_dve, 9)
            act.activation(r[:, 6, :], r[:, 5, :], ACT.Exp, bias=rc[:, 3:4], accum_out=rc[:, 4:5]).then_inc(route_act, 1)
            act.wait_ge(route_dve, 17)
            act.activation(rc[:, 9:10], rc[:, 8:9], ACT.Exp).then_inc(route_act, 1)

            def gelu(b, g):
                n = NG * b + g
                act.wait_ge(selected_1, b + 1)
                if n > 1:
                    act.wait_ge(y_ready, n - 1)
                for i in range(HK):
                    act.wait_ge(h_ready, HK * n + i + 1)
                    act.activation(hid[:, g % 2, i, :], Hps[:, i, 0:GW], ACT.Gelu,
                                   bias=b1s[:, b % 2, i // FH, i % FH:i % FH + 1]).then_inc(h_taken, 1)

            gelu(0, 0)
            for b in range(B):
                for g in range(1, NG):
                    gelu(b, g)
                if b + 1 < B:
                    gelu(b + 1, 0)
                act.wait_ge(yvar_ready, b + 1)
                act.activation(ysd[:, :], ymv[:, :, 1:2].rearrange("p t a -> p (t a)"), ACT.Sqrt, bias=eps[:, :]).then_inc(ysd_ready, 1)

        @block.tensor
        def _(pe):
            pe.wait_ge(small_in, 16 * 5)
            pe.wait_ge(constants, 3)
            pe.matmul(Hps[:, 0, 0:C], ones[0:1, :], vectors[0:1, 0, :], start=True, stop=True)
            pe.matmul(Hps[:, 1, 0:C], ones[0:1, :], vectors[0:1, 1, :], start=True, stop=True)
            pe.transpose(Hps[:, 2, 0:E * FH], b1_rows[:, :], ident[0:E * FH, 0:E * FH]).then_inc(small_ready, 1)
            for b in range(B):
                for g in range(NG):
                    pe.wait_ge(ln_ready, NG * b + g + 1)
                    pe.wait_ge(t_taken, NG * b + g + 1)
                    for k in range(GB):
                        last = pe.transpose(Rps[:, g % 2, cols(P, k)], ln[:, b * TILES + g * GB + k, :], ident[:, :])
                    last.then_inc(t_ready, 1)
            pe.wait_ge(route_dve, 1)
            pe.matmul(Rps[0:B, 0, 0:E], means[:, :], Wr[:, :], start=True, stop=False)
            pe.matmul(Rps[0:B, 0, 0:E], ones[0:1, 0:B], br[:, :], start=False, stop=True).then_inc(route_pe, 1)
            pe.wait_ge(route_dve, 4)
            pe.matmul(Rps[0:B, 0, 0:E], ones[0:B, 0:B], r[:, 2, :], start=True, stop=True).then_inc(route_pe, 1)
            pe.wait_ge(route_dve, ROUTE_STEPS)
            for b in range(B):
                last = pe.matmul(Rps[:, 0, cols(PICKS * E, b)], pick[:, b, :], choice[:, :, :].rearrange("b s e -> b (s e)"), start=True, stop=True)
            last.then_inc(route_pe, 1)
            pe.wait_ge(small_taken, 3)

            def hidden(b, t, g):
                n = NG * b + g
                if g == 0:
                    pe.wait_ge(selected_1, b + 1)
                for i in range(HK):
                    pe.wait_ge(h_taken, HK * n + i + 1)
                    pe.matmul(Hps[:, i, 0:GW], w1s[:, t, i // FH, cols(P, i % FH)],
                              lnT[:, bass.ds(b, 1), cols(GW, g)].rearrange("p a n -> p (a n)"), start=True, stop=True).then_inc(h_ready, 1)

            def outputs(b, t, g):
                n = NG * b + g
                if g == 0:
                    pe.wait_ge(selected_2, b + 1)
                pe.wait_ge(h_taken, HK * (n + 1) + 4)
                pe.wait_ge(y_taken, n + 1)
                for k in range(GB):
                    for i in range(HK):
                        last = pe.matmul(Yps[:, g % 2, cols(P, k)], hid[:, g % 2, i, cols(P, k)],
                                         w2s[:, t, i // FH, cols(C, i % FH)], start=i == 0, stop=i == HK - 1)
                last.then_inc(y_ready, 1)

            hidden(0, 0, 0)
            with pe.Fori(0, B // 2 - 1) as bp:
                for t in range(2):
                    for g in range(NG):
                        if g + 1 < NG:
                            hidden(2 * bp + t, t, g + 1)
                        else:
                            hidden(2 * bp + t + 1, 1 - t, 0)
                        outputs(2 * bp + t, t, g)
            for t in range(2):
                for g in range(NG):
                    if g + 1 < NG:
                        hidden(B - 2 + t, t, g + 1)
                    elif t == 0:
                        hidden(B - 1, 1, 0)
                    outputs(B - 2 + t, t, g)

        @block.vector
        def _(dve):
            dve.sem_inc(y_taken, 2)
            dve.wait_ge(small_ready, 1)
            dve.tensor_copy(gamma[:, 0, :], Hps[:, 0, 0:C]).then_inc(small_taken, 1)
            dve.tensor_copy(beta[:, 0, :], Hps[:, 1, 0:C]).then_inc(small_taken, 1)
            dve.tensor_copy(b1[:, :, :].rearrange("p e h -> p (e h)"), Hps[:, 2, 0:E * FH]).then_inc(small_taken, 1)
            dve.wait_ge(sd_ready, 1)
            dve.reciprocal(rstd[:, :], sd[:, :]).then_inc(rstd_ready, 1)
            dve.wait_ge(rstd_ready, 1)
            for group in range(B * NG):
                for t in tiles_of(group):
                    last = dve.tensor_scalar(ln[:, t, :], x1[:, t, :], moments[:, t, 0:1], rstd[:, t:t + 1],
                                             ALU.subtract, ALU.mult)
                last.then_inc(ln_ready, 1)

            steps = [0]

            def step(instruction):
                steps[0] += 1
                instruction.then_inc(route_dve, 1)
                dve.wait_ge(route_dve, steps[0])

            dve.wait_ge(t_taken, NG * B + T_SLOTS)
            dve.tensor_reduce(means[:, :], sums[:, :, :], AX.X, ALU.add).then_inc(mean_step, 1)
            dve.wait_ge(mean_step, 1)
            for b in range(B):
                dve.tensor_scalar(pick[:, b, :], ones[0:B, :], ident[0:B, b:b + 1], None, ALU.mult)
            step(dve.tensor_scalar(means[:, :], means[:, :], 1.0 / N, None, ALU.mult))
            dve.wait_ge(route_pe, 1)
            dve.tensor_copy(r[:, 0, :], Rps[0:B, 0, 0:E])
            step(dve.tensor_reduce(rc[:, 0:1], Rps[0:B, 0, 0:E], AX.X, ALU.max, negate=True))
            dve.wait_ge(route_act, 1)
            step(dve.reciprocal(rc[:, 2:3], rc[:, 1:2]))
            step(dve.tensor_scalar(r[:, 2, :], r[:, 1, :], rc[:, 2:3], None, ALU.mult))
            dve.wait_ge(route_pe, 2)
            step(dve.tensor_scalar(r[:, 3, :], Rps[0:B, 0, 0:E], float(N), None, ALU.mult))
            step(dve.reciprocal(r[:, 4, :], r[:, 3, :]))
            step(dve.tensor_scalar(r[:, 4, :], r[:, 4, :], CAPACITY, 1.0, ALU.mult, ALU.min))
            step(dve.tensor_tensor(r[:, 5, :], r[:, 2, :], r[:, 4, :], ALU.mult))
            step(dve.tensor_reduce(rc[:, 3:4], r[:, 5, :], AX.X, ALU.max, negate=True))
            dve.wait_ge(route_act, 2)
            step(dve.reciprocal(rc[:, 5:6], rc[:, 4:5]))
            step(dve.tensor_scalar(r[:, 7, :], r[:, 6, :], rc[:, 5:6], None, ALU.mult))
            for e in range(E):
                last = dve.tensor_scalar(greater[:, e, 0:E], r[:, 7, :], r[:, 7, e:e + 1], None, ALU.is_gt)
                if e:
                    last = dve.tensor_scalar(greater[:, e, E:E + e], r[:, 7, 0:e], r[:, 7, e:e + 1], None, ALU.is_equal)
            step(last)
            step(dve.tensor_reduce(r[:, 8, :], greater[:, :, :], AX.X, ALU.add))
            for k in range(TOPK):
                last = dve.tensor_scalar(choice[:, k, :], r[:, 8, :], float(k), None, ALU.is_equal)
            step(last)
            for k in range(TOPK):
                last = dve.tensor_tensor(r[:, 9 + k, :], choice[:, k, :], r[:, 7, :], ALU.mult)
            step(last)
            step(dve.tensor_reduce(rc[:, 6:8], r[:, 9:9 + TOPK, :], AX.X, ALU.add))
            step(dve.tensor_tensor(rc[:, 8:9], rc[:, 7:8], rc[:, 6:7], ALU.subtract))
            assert steps[0] == 17, steps
            dve.wait_ge(route_act, 3)
            step(dve.tensor_scalar(rc[:, 10:11], rc[:, 9:10], 1.0, None, ALU.add))
            step(dve.reciprocal(rc[:, 11:12], rc[:, 10:11]))
            step(dve.tensor_tensor(rc[:, 12:13], rc[:, 11:12], rc[:, 9:10], ALU.mult))
            for k in range(TOPK):
                last = dve.tensor_scalar(choice[:, TOPK + k, :], choice[:, k, :], rc[:, 11 + k:12 + k], None, ALU.mult)
            step(last)
            step(dve.tensor_tensor(choice[:, 2 * TOPK, :], choice[:, TOPK, :], choice[:, TOPK + 1, :], ALU.add))
            assert steps[0] == ROUTE_STEPS, steps
            dve.wait_ge(route_pe, 3)
            dve.tensor_copy(sel[:, :, :].rearrange("p b s -> p (b s)"), Rps[:, 0, 0:B * PICKS * E]).then_inc(sel_ready, 1)
            dve.wait_ge(sel_ready, 1)
            dve.wait_ge(weights_in, 16 * 3)

            def select(b, t, layer, e):
                def of(slot):
                    return sel[:, bass.ds(b, 1), slot * E + e:slot * E + e + 1].rearrange("p a n -> p (a n)")

                if layer == 0:
                    jobs = [(w1s[:, t, k, :], W1[:, e, :], of(k)) for k in range(TOPK)]
                    jobs += [(b1s[:, t, k, :], b1[:, e, :], of(k)) for k in range(TOPK)]
                else:
                    jobs = [(w2s[:, t, k, :], W2[:, e, :], of(TOPK + k)) for k in range(TOPK)]
                    jobs.append((b2s[:, t, :], b2[:, e, :], of(2 * TOPK)))
                if e:
                    dve.wait_ge(select_step, (E - 1) * (2 * b + layer) + e)
                    alone(dve)
                for dst, src, factor in jobs:
                    if e == 0:
                        last = dve.tensor_scalar(dst, src, factor, None, ALU.mult)
                    else:
                        last = dve.scalar_tensor_tensor(out=dst, in0=src, scalar=factor, in1=dst, op0=ALU.mult, op1=ALU.add)
                last.then_inc(select_step if e < E - 1 else (selected_1, selected_2)[layer], 1)

            def variances(b, g):
                dve.wait_ge(y_step, (NG + 1) * b + g + 1)
                alone(dve)
                for t in tiles_of(g):
                    last = dve.bn_aggr(ymv[:, t, :], ystats[:, t, :])
                return last

            def close(b, g):
                n = NG * b + g
                if g == 0:
                    dve.wait_ge(base_ready, b + 1)
                dve.wait_ge(y_ready, n + 1)
                alone(dve)
                tok = ln[:, bass.ds(b * TILES + g * GB, GB), :]
                dve.tensor_tensor(tok, Yps[:, g % 2, 0:GW].rearrange("p (t c) -> p t c", t=GB), tok, ALU.add).then_inc(y_taken, 1)
                if g:
                    variances(b, g - 1)
                dve.wait_ge(y_taken, n + 1 + 2)
                alone(dve)
                for t in tiles_of(g):
                    last = dve.bn_stats(ystats[:, t, :], ln[:, bass.ds(b * TILES + t, 1), :].rearrange("p t c -> p (t c)"))
                last.then_inc(y_step, 1)

            def finish(b):
                variances(b, NG - 1).then_inc(yvar_ready, 1)
                dve.wait_ge(ysd_ready, b + 1)
                dve.reciprocal(yrstd[:, :], ysd[:, :]).then_inc(y_step, 1)
                dve.wait_ge(y_step, (NG + 1) * (b + 1))
                alone(dve)
                for t in range(TILES):
                    row = ln[:, bass.ds(b * TILES + t, 1), :].rearrange("p t c -> p (t c)")
                    last = dve.tensor_scalar(row, row, ymv[:, t, 0:1], yrstd[:, t:t + 1], ALU.subtract, ALU.mult)
                    if t % HT == HT - 1:
                        last.then_inc(y_normed, 1)

            SELECTIONS = [(layer, e) for layer in range(2) for e in range(E)]

            def experts_products(b, t, ahead=True):
                for g in range(NG):
                    if ahead:
                        for layer, e in SELECTIONS[3 * g:3 * g + 3]:
                            select(b + 1, 1 - t, layer, e)
                    close(b, g)
                finish(b)

            for layer, e in SELECTIONS:
                select(0, 0, layer, e)
            with dve.Fori(0, B // 2 - 1) as bp:
                for t in range(2):
                    experts_products(2 * bp + t, t)
            experts_products(B - 2, 0)
            experts_products(B - 1, 1, ahead=False)
            last_half = tokens(ln, B - 1, 1)
            dve.wait_ge(y_normed, 2 * B)
            dve.tensor_tensor(last_half, last_half, everywhere(gamma[:, :, :]), ALU.mult).then_inc(last_scaled, 1)
            dve.wait_ge(last_scaled, 1)
            dve.wait_ge(res_ready, B)
            dve.tensor_tensor(last_half, last_half, tokens(x1, B - 1, 1), ALU.add).then_inc(last_out_ready, 1)


def hybrid(nc, a, out):
    def scratch(name, n, dt=F32):
        return nc.dram_tensor(name, (n,), dt, kind="Internal").ap()

    q = scratch("q_parts", HEADS * 3 * D * B * N, BF16).rearrange(
        "(s u h d b n) -> s u h d b n", h=HEADS, s=3, u=TILES // 2, d=D, b=B)
    k = scratch("k_parts", HEADS * 3 * D * B * N, BF16).rearrange(
        "(h s d b n) -> h s d b n", h=HEADS, s=3, d=D, b=B)
    v = scratch("v_heads", HEADS * P * B * TILES * D).rearrange("(h p b x) -> h p b x", h=HEADS, p=P, b=B)
    num = scratch("numerators", B * 4 * C * N)
    den = scratch("denominators", B * 4 * HEADS * N)
    inv = scratch("inverses", B * HEADS * N).rearrange("(b h n) -> b h n", b=B, h=HEADS)
    vpad = scratch("v_padded", B * C * IMAGE_IN).rearrange("(b c n) -> b c n", b=B, c=C)
    conv = scratch("conv_out", B * C * N)
    s = {
        "x_tiles": a["x"].rearrange("b h w c -> b (h w) c").rearrange("b (t p) c -> b p t c", p=P),
        "mask": a["mask"].rearrange("h (t p) n -> (h t) p n", p=P),
        "q_store": q.rearrange("s u h d b n -> b s (h d) u n"),
        "k_store": k.rearrange("h s d b n -> b s h d n"),
        "v_store": v.rearrange("h p b x -> b p h x"),
        "q_load": q.rearrange("s u h d b n -> h u s d (b n)"),
        "k_load": k.rearrange("h s d b n -> h (s d) (b n)"),
        "v_load": v.rearrange("h p b x -> h p (b x)"),
        "o_store": num.rearrange("(b j h d n) -> j h d b n", b=B, j=4, h=HEADS, d=D),
        "o_load": num.rearrange("(b j c n) -> b c j n", b=B, j=4, c=C),
        "den_store": den.rearrange("(b j h n) -> h j b n", b=B, j=4, h=HEADS),
        "den_load": den.rearrange("(b j p n) -> b p j n", b=B, j=4, p=P),
        "inv_store": inv.rearrange("b h (s n) -> b (h s) n", s=D),
        "inv_load": inv,
        "vpad_store": vpad,
        "vpad_load": vpad,
        "conv_store": conv.rearrange("(b c f h w) -> b f c h w", b=B, c=C, f=2, w=W),
        "conv": conv.rearrange("(b c n) -> b c n", b=B, c=C),
    }
    out_tiles = out.rearrange("b h w c -> b (h w) c").rearrange("b (t p) c -> b p t c", p=P)
    with ExitStack() as ctx:
        ident = ctx.enter_context(nc.sbuf_tensor("ident", [P, P], F32))
        taps = ctx.enter_context(nc.sbuf_tensor("taps", [P, TAPS], F32))
        conv_bias = ctx.enter_context(nc.sbuf_tensor("conv_bias", [P, 1], F32))
        stages12 = ctx.enter_context(ExitStack())
        mask = stages12.enter_context(nc.sbuf_tensor("mask_tiles", [P, 4, N], F32))
        layer0_front(nc, {k: a[k] for k in ("Wq", "Wk", "Wv", "bq", "bk", "bv", "dw_w", "dw_b", "sin", "cos")}, s, ident, taps, conv_bias, mask)
        layer0_core(nc, a, s, ident, taps, conv_bias, mask)
        stages12.close()
        x1 = ctx.enter_context(nc.sbuf_tensor("x1", [P, B * TILES, C], F32))
        moments = ctx.enter_context(nc.sbuf_tensor("moments", [P, B * TILES, 2], F32))
        layer1_attention(nc, a, s, ident, x1, moments)
        layer1_ffn(nc, a, s, ident, x1, moments, out_tiles)


SHORT = {
    "x": "x", "sin": "L0_conv_sin", "cos": "L0_conv_cos", "mask": "L0_conv_mask", "Wq": "L0_conv_Wq",
    "bq": "L0_conv_bq", "Wk": "L0_conv_Wk", "bk": "L0_conv_bk", "Wv": "L0_conv_Wv", "bv": "L0_conv_bv",
    "dw_w": "L0_conv_dw_w", "dw_b": "L0_conv_dw_b", "Wo0": "L0_conv_Wo", "bo0": "L0_conv_bo",
    "Wq1": "L1_attn_Wq", "bq1": "L1_attn_bq", "Wk1": "L1_attn_Wk", "bk1": "L1_attn_bk",
    "Wv1": "L1_attn_Wv", "bv1": "L1_attn_bv", "Wr": "L1_ffn_Wr", "br": "L1_ffn_br", "W1": "L1_ffn_W1",
    "b1": "L1_ffn_b1", "W2": "L1_ffn_W2", "b2": "L1_ffn_b2", "gamma": "L1_ffn_gamma", "beta": "L1_ffn_beta",
}


def kernel(**inputs):
    import concourse.bacc as bacc
    from concourse.bass_utils import run_bass_kernel_spmd

    nc = bacc.Bacc("TRN2", target_bir_lowering=False, num_devices=1)
    arrays, a = {}, {}
    for short, name in SHORT.items():
        x = np.ascontiguousarray(inputs[name])
        arrays[f"in_{short}"] = x
        a[short] = nc.dram_tensor(f"in_{short}", x.shape, mybir.dt.from_np(x.dtype), kind="ExternalInput").ap()
    out = nc.dram_tensor("out", (B, H, W, C), F32, kind="ExternalOutput").ap()
    hybrid(nc, a, out)
    return run_bass_kernel_spmd(nc, [arrays], core_ids=[0]).results[0]["out"]
```
